# Optimizing a Trainium2 kernel written in Bass

```python
import numpy as np
import jax
import jax.numpy as jnp

def _softmax(x, axis=-1):
    return jax.nn.softmax(x, axis=axis)

def _gelu(x):
    return jax.nn.gelu(x, approximate=True)

def _silu(x):
    return jax.nn.silu(x)

def _sigmoid(x):
    return jax.nn.sigmoid(x)

def _layernorm(x, axis=-1, eps=1e-05):
    m = jnp.mean(x, axis=axis, keepdims=True)
    v = jnp.var(x, axis=axis, keepdims=True)
    return (x - m) / jnp.sqrt(v + eps)

def _scatter_add(tgt, idx, src, axis=0):
    return tgt.at[idx].add(src)

def _segment_sum(src, seg, n):
    return jax.ops.segment_sum(src, seg, n)
kernel_name = 'mk_decoder_postln_d4_seqx_r8_d5ea24'

def setup_inputs(seed: int=0):
    np.random.seed(seed)
    _w = jnp.asarray

    def _rec_inputs():
        import jax
        import jax.numpy as jnp
        _rk = jax.random.key(seed)
        x = -0.0003929 + 0.9999 * jax.random.normal(jax.random.fold_in(_rk, 1), (32, 64, 128), jnp.float32)
        _lenS = 64 - jax.random.randint(jax.random.fold_in(_rk, 7), (32,), 0, max(1, 64 // 4) + 1, jnp.int32)
        _lenS2 = 64 - jax.random.randint(jax.random.fold_in(_rk, 8), (32,), 0, max(1, 64 // 4) + 1, jnp.int32)
        _ctx_1024P = jax.random.normal(jax.random.fold_in(_rk, 11), (32, 16, 128), jnp.float32)
        _ctx_1024c = jax.random.dirichlet(jax.random.fold_in(_rk, 511), 0.3 * jnp.ones((16,), jnp.float32), (32, 64))
        _ctx_1024t = jnp.einsum('bsk,bkd->bsd', _ctx_1024c, _ctx_1024P)
        _ctx_1024t = _ctx_1024t * jax.lax.rsqrt(jnp.mean(jnp.square(_ctx_1024t)) + 1e-12) * 0.953939
        ctx_1024 = 4.13588e-05 + 0.999923 * (_ctx_1024t + 0.3 * jax.random.normal(jax.random.fold_in(_rk, 611), (32, 64, 128), jnp.float32))
        _validS = jnp.arange(64)[None, :] < _lenS[:, None]
        _validS2 = jnp.arange(64)[None, :] < _lenS2[:, None]
        _causal = jnp.tril(jnp.ones((64, 64), dtype=bool))
        mask_1x1xSxS2_bk0 = jnp.logical_not(jnp.broadcast_to(_validS2[0:1, None, None, :], (1, 1, 64, 64)))
        mask_Bx1x1xS2_ik0 = jnp.where(jnp.broadcast_to(_validS2[:, None, None, :], (32, 1, 1, 64)), 0, 1).astype(jnp.int32)
        mask_1x1xSxS2_ik0 = jnp.where(jnp.broadcast_to(_validS2[0:1, None, None, :], (1, 1, 64, 64)), 0, 1).astype(jnp.int32)
        return (x, ctx_1024, mask_1x1xSxS2_bk0, mask_Bx1x1xS2_ik0, mask_1x1xSxS2_ik0)
    x, ctx_1024, mask_1x1xSxS2_bk0, mask_Bx1x1xS2_ik0, mask_1x1xSxS2_ik0 = _rec_inputs()

    def _L0_attn_setup():
        import jax, jax.numpy as jnp
        import numpy as np
        import math
        DIM = 128
        N_HEADS = 16
        HEAD_DIM = DIM // N_HEADS

        def rope(x):
            S = x.shape[-2]
            D = x.shape[-1]
            pos = jnp.arange(S, dtype=x.dtype)[:, None]
            dim = jnp.arange(D // 2, dtype=x.dtype)[None, :]
            theta = pos / jnp.exp(2.0 * dim / D * math.log(10000.0))
            sin = jnp.sin(theta)[None, None]
            cos = jnp.cos(theta)[None, None]
            x1 = x[..., ::2]
            x2 = x[..., 1::2]
            out1 = x1 * cos - x2 * sin
            out2 = x1 * sin + x2 * cos
            return jnp.stack([out1, out2], axis=-1).reshape(x.shape)
        key = jax.random.key(seed)
        ks = jax.random.split(key, 9)
        B, S = (2, 256)
        s = 1.0 / math.sqrt(DIM)
        inp = {'x': jax.random.normal(ks[0], (B, S, DIM), dtype=jnp.float32), 'wq': jax.random.normal(ks[1], (DIM, DIM), dtype=jnp.float32) * s, 'bq': jnp.zeros((DIM,), dtype=jnp.float32), 'wk': jax.random.normal(ks[2], (DIM, DIM), dtype=jnp.float32) * s, 'bk': jnp.zeros((DIM,), dtype=jnp.float32), 'wv': jax.random.normal(ks[3], (DIM, DIM), dtype=jnp.float32) * s, 'bv': jnp.zeros((DIM,), dtype=jnp.float32), 'wo': jax.random.normal(ks[4], (DIM, DIM), dtype=jnp.float32) * s, 'bo': jnp.zeros((DIM,), dtype=jnp.float32)}
        return inp
    _L0_attn_all = _L0_attn_setup()
    _L0_attn_in = {k: v for k, v in _L0_attn_all.items() if k in ('wq', 'bq', 'wk', 'bk', 'wv', 'bv', 'wo', 'bo')}
    del _L0_attn_all

    def _L0_xattn_setup():
        import jax, jax.numpy as jnp
        import numpy as np
        H = 128
        B = 8
        L_CHAR = 256
        L_SUB = 128

        def _linear(x, W, b):
            return jnp.einsum('blh,oh->blo', x, W) + b

        def _interp_linear(x, out_len):
            L_in = x.shape[1]
            pos = (jnp.arange(out_len, dtype=x.dtype) + 0.5) * (L_in / out_len) - 0.5
            pos = jnp.clip(pos, 0.0, L_in - 1)
            lo = jnp.floor(pos).astype(jnp.int32)
            hi = jnp.minimum(lo + 1, L_in - 1)
            w = (pos - lo.astype(x.dtype))[None, :, None]
            return x[:, lo] * (1 - w) + x[:, hi] * w
        key = jax.random.key(seed)
        ks = jax.random.split(key, 18)
        s = 0.02
        inp = {'char_emb': jax.random.normal(ks[0], (B, L_CHAR, H), jnp.float32), 'subword_emb': jax.random.normal(ks[1], (B, L_SUB, H), jnp.float32)}
        names = ['Wq_c', 'Wk_s', 'Wv_s', 'Wq_s', 'Wk_c', 'Wv_c']
        for i, n in enumerate(names):
            inp[n] = jax.random.normal(ks[2 + 2 * i], (H, H), jnp.float32) * s
            inp['b' + n[1:]] = jax.random.normal(ks[3 + 2 * i], (H,), jnp.float32) * s
        inp['Wg'] = jax.random.normal(ks[14], (H, 2 * H), jnp.float32) * s
        inp['bg'] = jax.random.normal(ks[15], (H,), jnp.float32) * s
        return inp
    _L0_xattn_all = _L0_xattn_setup()
    _L0_xattn_in = {k: v for k, v in _L0_xattn_all.items() if k in ('Wq_c', 'bq_c', 'Wk_s', 'bk_s', 'Wv_s', 'bv_s', 'Wq_s', 'bq_s', 'Wk_c', 'bk_c', 'Wv_c', 'bv_c', 'Wg', 'bg')}
    del _L0_xattn_all

    def _L0_ffn_setup():
        import jax, jax.numpy as jnp
        import numpy as np
        DIM = 128
        DEPTH = 2
        HEADS = 8
        DIM_HEAD = 64
        WINDOW = 64
        INNER = HEADS * DIM_HEAD
        HID = int(DIM * 4 * 2 / 3)
        B, N = (2, 1024)
        QK_SCALE = 8.0

        def shift_token(t):
            t1, t2 = jnp.split(t, 2, axis=-1)
            t2 = jnp.pad(t2, ((0, 0), (1, 0), (0, 0)))[:, :-1]
            return jnp.concatenate([t1, t2], axis=-1)

        def l2norm(t):
            return t / jnp.clip(jnp.linalg.norm(t, axis=-1, keepdims=True), 1e-12)

        def rotate_half(x):
            x1, x2 = jnp.split(x, 2, axis=-1)
            return jnp.concatenate([-x2, x1], axis=-1)

        def rotary_xpos(q, k):
            n = q.shape[-2]
            half_idx = jnp.arange(0, DIM_HEAD, 2, dtype=jnp.float32)
            inv_freq = 1.0 / 10000.0 ** (half_idx / DIM_HEAD)
            t = jnp.arange(n, dtype=jnp.float32)
            freqs = t[:, None] * inv_freq[None, :]
            freqs = jnp.concatenate([freqs, freqs], axis=-1)
            base = (half_idx + 0.4 * DIM_HEAD) / (1.4 * DIM_HEAD)
            power = (t - n // 2) / float(WINDOW // 2)
            scale = base[None, :] ** power[:, None]
            scale = jnp.concatenate([scale, scale], axis=-1)
            cos, sin = (jnp.cos(freqs), jnp.sin(freqs))
            q = q * cos * scale + rotate_half(q) * sin * scale
            k = k * cos / scale + rotate_half(k) * sin / scale
            return (q, k)

        def local_attention(q, k, v):
            b, h, n, d = q.shape
            w = n // WINDOW
            bq = q.reshape(b, h, w, WINDOW, d) * QK_SCALE
            bk = k.reshape(b, h, w, WINDOW, d)
            bv = v.reshape(b, h, w, WINDOW, d)

            def look_around(t):
                p = jnp.pad(t, ((0, 0), (0, 0), (1, 0), (0, 0), (0, 0)))
                return jnp.concatenate([p[:, :, :w], p[:, :, 1:]], axis=3)
            bk, bv = (look_around(bk), look_around(bv))
            bt = jnp.arange(n).reshape(w, WINDOW)
            btp = jnp.pad(bt, ((1, 0), (0, 0)), constant_values=-1)
            btk = jnp.concatenate([btp[:w], btp[1:]], axis=1)
            sim = jnp.einsum('bhwid,bhwjd->bhwij', bq, bk)
            i = bt[:, :, None]
            j = btk[:, None, :]
            mask = (i < j) | (i > j + WINDOW) | (j == -1)
            sim = jnp.where(mask, -jnp.finfo(sim.dtype).max, sim)
            attn = jax.nn.softmax(sim, axis=-1)
            out = jnp.einsum('bhwij,bhwjd->bhwid', attn, bv)
            return out.reshape(b, h, n, d)

        def _layer(x, wqkv, qs, ksc, wo, lg, lb, w1, b1, w2, b2):
            b, n, _ = x.shape
            h = shift_token(x)
            qkv = h @ wqkv
            q, k, v = jnp.split(qkv, 3, axis=-1)
            to_heads = lambda t: t.reshape(b, n, HEADS, DIM_HEAD).transpose(0, 2, 1, 3)
            q, k, v = (to_heads(q), to_heads(k), to_heads(v))
            q = l2norm(q) * qs
            k = l2norm(k) * ksc
            q, k = rotary_xpos(q, k)
            o = local_attention(q, k, v)
            o = o.transpose(0, 2, 1, 3).reshape(b, n, INNER)
            x = x + o @ wo
            h = shift_token(x)
            mu = h.mean(-1, keepdims=True)
            var = h.var(-1, keepdims=True)
            h = (h - mu) / jnp.sqrt(var + 1e-05) * lg + lb
            h = h @ w1 + b1
            a, g = jnp.split(h, 2, axis=-1)
            h = a * jax.nn.gelu(g, approximate=False)
            x = x + h @ w2 + b2
            return x
        key = jax.random.key(seed)
        ks = jax.random.split(key, 6)
        return {'x': jax.random.normal(ks[0], (B, N, DIM), jnp.float32), 'wqkv': jax.random.normal(ks[1], (DEPTH, DIM, 3 * INNER), jnp.float32) * 0.02, 'q_scale': jnp.ones((DEPTH, DIM_HEAD), jnp.float32), 'k_scale': jnp.ones((DEPTH, DIM_HEAD), jnp.float32), 'wo': jax.random.normal(ks[2], (DEPTH, INNER, DIM), jnp.float32) * 0.02, 'ln_g': jnp.ones((DEPTH, DIM), jnp.float32), 'ln_b': jnp.zeros((DEPTH, DIM), jnp.float32), 'w1': jax.random.normal(ks[3], (DEPTH, DIM, 2 * HID), jnp.float32) * 0.02, 'b1': jnp.zeros((DEPTH, 2 * HID), jnp.float32), 'w2': jax.random.normal(ks[4], (DEPTH, HID, DIM), jnp.float32) * 0.02, 'b2': jnp.zeros((DEPTH, DIM), jnp.float32)}
    _L0_ffn_all = _L0_ffn_setup()
    _L0_ffn_in = {k: v for k, v in _L0_ffn_all.items() if k in ('wqkv', 'q_scale', 'k_scale', 'wo', 'ln_g', 'ln_b', 'w1', 'b1', 'w2', 'b2')}
    del _L0_ffn_all

    def _L1_attn_setup():
        import jax, jax.numpy as jnp
        import numpy as np
        N_HEADS = 16
        HEAD_DIM = 64
        ROPE_THETA = 10000.0

        def _rope_cos_sin(seq_len, dim, theta):
            inv_freq = 1.0 / theta ** (jnp.arange(0, dim, 2, dtype=jnp.float32) / dim)
            pos = jnp.arange(seq_len, dtype=jnp.float32)
            freqs = pos[:, None] * inv_freq[None, :]
            emb = jnp.concatenate([freqs, freqs], axis=-1)
            return (jnp.cos(emb), jnp.sin(emb))

        def _rotate_half(x):
            d = x.shape[-1] // 2
            return jnp.concatenate([-x[..., d:], x[..., :d]], axis=-1)
        key = jax.random.key(seed)
        ks = jax.random.split(key, 6)
        B, S, D_MODEL, LATENT = (1, 512, 128, 64)
        q_dim = N_HEADS * HEAD_DIM
        sd = lambda fan_in: 1.0 / np.sqrt(fan_in)
        return {'x': jax.random.normal(ks[0], (B, S, D_MODEL), jnp.float32), 'wq': jax.random.normal(ks[1], (q_dim, D_MODEL), jnp.float32) * sd(D_MODEL), 'w_kv_down': jax.random.normal(ks[2], (LATENT, D_MODEL), jnp.float32) * sd(D_MODEL), 'w_k_up': jax.random.normal(ks[3], (q_dim, LATENT), jnp.float32) * sd(LATENT), 'w_v_up': jax.random.normal(ks[4], (q_dim, LATENT), jnp.float32) * sd(LATENT), 'wo': jax.random.normal(ks[5], (D_MODEL, q_dim), jnp.float32) * sd(q_dim)}
    _L1_attn_all = _L1_attn_setup()
    _L1_attn_in = {k: v for k, v in _L1_attn_all.items() if k in ('wq', 'w_kv_down', 'w_k_up', 'w_v_up', 'wo')}
    del _L1_attn_all

    def _L1_xattn_setup():
        import jax, jax.numpy as jnp
        import numpy as np
        EMBED_DIM = 128
        HEADS = 16
        D_K = EMBED_DIM // HEADS
        B, S = (2, 256)

        def _split_heads(x):
            b, s, _ = x.shape
            return x.reshape(b, s, HEADS, D_K).transpose(0, 2, 1, 3)
        key = jax.random.key(seed)
        ks = jax.random.split(key, 8)
        scale = 1.0 / np.sqrt(EMBED_DIM)
        inp = {'key': jax.random.normal(ks[0], (B, S, EMBED_DIM), dtype=jnp.float32), 'query': jax.random.normal(ks[1], (B, S, EMBED_DIM), dtype=jnp.float32), 'value': jax.random.normal(ks[2], (B, S, EMBED_DIM), dtype=jnp.float32), 'Wq': jax.random.normal(ks[3], (EMBED_DIM, EMBED_DIM), dtype=jnp.float32) * scale, 'Wk': jax.random.normal(ks[4], (EMBED_DIM, EMBED_DIM), dtype=jnp.float32) * scale, 'Wv': jax.random.normal(ks[5], (EMBED_DIM, EMBED_DIM), dtype=jnp.float32) * scale, 'Wo': jax.random.normal(ks[6], (EMBED_DIM, EMBED_DIM), dtype=jnp.float32) * scale, 'bo': jax.random.normal(ks[7], (EMBED_DIM,), dtype=jnp.float32) * scale, 'mask': jnp.tril(jnp.ones((S, S), dtype=jnp.bool_))[None, None, :, :]}
        return inp
    _L1_xattn_all = _L1_xattn_setup()
    _L1_xattn_in = {k: v for k, v in _L1_xattn_all.items() if k in ('Wq', 'Wk', 'Wv', 'Wo', 'bo')}
    del _L1_xattn_all

    def _L1_ffn_setup():
        import jax, jax.numpy as jnp
        import numpy as np
        D_MODEL, D_FF, N_EXP = (128, 512, 8)
        key = jax.random.key(seed)
        ks = jax.random.split(key, 8)
        s = lambda fan_in: 1.0 / np.sqrt(fan_in)
        x = jax.random.normal(ks[0], (4, 256, D_MODEL), dtype=jnp.float32)
        Wr = jax.random.uniform(ks[1], (N_EXP, D_MODEL), jnp.float32, -s(D_MODEL), s(D_MODEL))
        br = jax.random.uniform(ks[2], (N_EXP,), jnp.float32, -s(D_MODEL), s(D_MODEL))
        W1 = jax.random.uniform(ks[3], (N_EXP, D_FF, D_MODEL), jnp.float32, -s(D_MODEL), s(D_MODEL))
        b1 = jax.random.uniform(ks[4], (N_EXP, D_FF), jnp.float32, -s(D_MODEL), s(D_MODEL))
        W2 = jax.random.uniform(ks[5], (N_EXP, D_MODEL, D_FF), jnp.float32, -s(D_FF), s(D_FF))
        b2 = jax.random.uniform(ks[6], (N_EXP, D_MODEL), jnp.float32, -s(D_FF), s(D_FF))
        return {'x': x, 'Wr': Wr, 'br': br, 'W1': W1, 'b1': b1, 'W2': W2, 'b2': b2}
    _L1_ffn_all = _L1_ffn_setup()
    _L1_ffn_in = {k: v for k, v in _L1_ffn_all.items() if k in ('Wr', 'br', 'W1', 'b1', 'W2', 'b2')}
    del _L1_ffn_all

    def _L2_attn_setup():
        import math
        import jax, jax.numpy as jnp
        import numpy as np
        D_MODEL = 128
        N_HEADS = 16
        D_HEAD = D_MODEL // N_HEADS

        def get_alibi_slopes(n_heads: int) -> np.ndarray:

            def pow2_slopes(n):
                start = 2 ** (-2 ** (-(math.log2(n) - 3)))
                return np.array([start * start ** i for i in range(n)], dtype=np.float32)
            if math.log2(n_heads).is_integer():
                return pow2_slopes(n_heads)
            closest = 2 ** math.floor(math.log2(n_heads))
            slopes = pow2_slopes(closest)
            extra = pow2_slopes(2 * closest)[0::2][:n_heads - closest]
            return np.concatenate([slopes, extra], axis=0)
        key = jax.random.key(seed)
        ks = jax.random.split(key, 9)
        B, S, D = (2, 256, D_MODEL)
        scale = 1.0 / math.sqrt(D)
        inp = {'x': jax.random.normal(ks[0], (B, S, D), dtype=jnp.float32), 'Wq': jax.random.normal(ks[1], (D, D), dtype=jnp.float32) * scale, 'bq': jnp.zeros((D,), dtype=jnp.float32), 'Wk': jax.random.normal(ks[2], (D, D), dtype=jnp.float32) * scale, 'bk': jnp.zeros((D,), dtype=jnp.float32), 'Wv': jax.random.normal(ks[3], (D, D), dtype=jnp.float32) * scale, 'bv': jnp.zeros((D,), dtype=jnp.float32), 'Wo': jax.random.normal(ks[4], (D, D), dtype=jnp.float32) * scale, 'bo': jnp.zeros((D,), dtype=jnp.float32)}
        return inp
    _L2_attn_all = _L2_attn_setup()
    _L2_attn_in = {k: v for k, v in _L2_attn_all.items() if k in ('Wq', 'bq', 'Wk', 'bk', 'Wv', 'bv', 'Wo', 'bo')}
    del _L2_attn_all

    def _L2_xattn_setup():
        import jax, jax.numpy as jnp
        import numpy as np
        D_MODEL = 128
        NHEAD = 16
        HEAD_DIM = D_MODEL // NHEAD
        key = jax.random.key(seed)
        ks = jax.random.split(key, 11)
        B, S, D = (4, 256, D_MODEL)
        scale = 1.0 / np.sqrt(D)
        inp = {'q': jax.random.normal(ks[0], (B, S, D), jnp.float32), 'k': jax.random.normal(ks[1], (B, S, D), jnp.float32), 'v': jax.random.normal(ks[2], (B, S, D), jnp.float32), 'Wq': jax.random.normal(ks[3], (D, D), jnp.float32) * scale, 'bq': jnp.zeros((D,), jnp.float32), 'Wk': jax.random.normal(ks[4], (D, D), jnp.float32) * scale, 'bk': jnp.zeros((D,), jnp.float32), 'Wv': jax.random.normal(ks[5], (D, D), jnp.float32) * scale, 'bv': jnp.zeros((D,), jnp.float32), 'Wo': jax.random.normal(ks[6], (D, D), jnp.float32) * scale, 'bo': jnp.zeros((D,), jnp.float32)}
        return inp
    _L2_xattn_all = _L2_xattn_setup()
    _L2_xattn_in = {k: v for k, v in _L2_xattn_all.items() if k in ('Wq', 'bq', 'Wk', 'bk', 'Wv', 'bv', 'Wo', 'bo')}
    del _L2_xattn_all

    def _L2_ffn_setup():
        import jax, jax.numpy as jnp
        import numpy as np
        NUM_EXPERTS = 8
        CAPACITY = 80
        key = jax.random.key(seed)
        ks = jax.random.split(key, 5)
        D, E, F = (128, NUM_EXPERTS, 512)
        inputs = jax.random.normal(ks[0], (2, 256, D), dtype=jnp.float32)
        gate_w = jax.random.normal(ks[1], (D, E), dtype=jnp.float32) * 0.02
        gate_b = jnp.zeros((E,), dtype=jnp.float32)
        w1 = jax.random.normal(ks[2], (E, D, F), dtype=jnp.float32) * 0.02
        b1 = jnp.zeros((E, F), dtype=jnp.float32)
        w2 = jax.random.normal(ks[3], (E, F, D), dtype=jnp.float32) * 0.02
        b2 = jnp.zeros((E, D), dtype=jnp.float32)
        return {'inputs': inputs, 'gate_w': gate_w, 'gate_b': gate_b, 'w1': w1, 'b1': b1, 'w2': w2, 'b2': b2}
    _L2_ffn_all = _L2_ffn_setup()
    _L2_ffn_in = {k: v for k, v in _L2_ffn_all.items() if k in ('gate_w', 'gate_b', 'w1', 'b1', 'w2', 'b2')}
    del _L2_ffn_all

    def _L3_attn_setup():
        import jax, jax.numpy as jnp
        import numpy as np
        D_MODEL = 128
        NUM_HEADS = 16
        D_K = D_MODEL // NUM_HEADS
        THETA = 10000.0
        NEG_INF = -1000000000.0

        def _rope(x, positions):
            half = D_K // 2
            inv_freq = 1.0 / THETA ** (jnp.arange(0, D_K, 2, dtype=jnp.float32) / D_K)
            angles = positions.astype(jnp.float32)[:, None] * inv_freq
            cos, sin = (jnp.cos(angles), jnp.sin(angles))
            xe = x[..., 0::2]
            xo = x[..., 1::2]
            re = xe * cos - xo * sin
            ro = xe * sin + xo * cos
            return jnp.stack([re, ro], axis=-1).reshape(x.shape).astype(x.dtype)
        key = jax.random.key(seed)
        ks = jax.random.split(key, 5)
        sigma = np.sqrt(2.0 / (D_MODEL + D_MODEL))
        x = jax.random.normal(ks[0], (2, 256, D_MODEL), dtype=jnp.float32)
        mk = lambda k: (sigma * jax.random.normal(k, (D_MODEL, D_MODEL))).astype(jnp.float32)
        return {'x': x, 'Wq': mk(ks[1]), 'bq': jnp.zeros((D_MODEL,), jnp.float32), 'Wk': mk(ks[2]), 'bk': jnp.zeros((D_MODEL,), jnp.float32), 'Wv': mk(ks[3]), 'bv': jnp.zeros((D_MODEL,), jnp.float32), 'Wo': mk(ks[4]), 'bo': jnp.zeros((D_MODEL,), jnp.float32), 'token_positions': jnp.arange(256, dtype=jnp.int64) if jax.config.jax_enable_x64 else jnp.arange(256, dtype=jnp.int32)}
    _L3_attn_all = _L3_attn_setup()
    _L3_attn_in = {k: v for k, v in _L3_attn_all.items() if k in ('Wq', 'bq', 'Wk', 'bk', 'Wv', 'bv', 'Wo', 'bo', 'token_positions')}
    del _L3_attn_all

    def _L3_xattn_setup():
        import jax, jax.numpy as jnp
        import numpy as np
        E, H = (128, 16)
        N, S, T = (2, 256, 256)
        key = jax.random.key(seed)
        ks = jax.random.split(key, 8)
        scale = 1.0 / np.sqrt(E)
        q = jax.random.normal(ks[0], (N, S, E), dtype=jnp.float32)
        k = jax.random.normal(ks[1], (N, T, E), dtype=jnp.float32)
        v = jax.random.normal(ks[2], (N, T, E), dtype=jnp.float32)
        pad_mask = jax.random.randint(ks[3], (N, 1, 1, T), 0, 2, dtype=jnp.int32)
        subsq_mask = jnp.tril(jnp.ones((S, T), dtype=jnp.int32))[None, None]
        Wq = jax.random.normal(ks[4], (E, E), dtype=jnp.float32) * scale
        Wk = jax.random.normal(ks[5], (E, E), dtype=jnp.float32) * scale
        Wv = jax.random.normal(ks[6], (E, E), dtype=jnp.float32) * scale
        bq = jnp.zeros((E,), dtype=jnp.float32)
        bk = jnp.zeros((E,), dtype=jnp.float32)
        bv = jnp.zeros((E,), dtype=jnp.float32)
        return {'query': q, 'key': k, 'value': v, 'pad_mask': pad_mask, 'subsq_mask': subsq_mask, 'Wq': Wq, 'bq': bq, 'Wk': Wk, 'bk': bk, 'Wv': Wv, 'bv': bv}
    _L3_xattn_all = _L3_xattn_setup()
    _L3_xattn_in = {k: v for k, v in _L3_xattn_all.items() if k in ('Wq', 'bq', 'Wk', 'bk', 'Wv', 'bv')}
    del _L3_xattn_all

    def _L3_ffn_setup():
        import jax, jax.numpy as jnp
        import numpy as np
        FEATURES = 128
        D_IN = 128

        def fp8_gemm_optimized(x, input_scale, kernel, kernel_scale):
            s_in = input_scale[0]
            s_k = kernel_scale[0]
            x_q = (x.astype(jnp.float32) / s_in).astype(jnp.float8_e4m3fn)
            k_q = (kernel.astype(jnp.float32) / s_k).astype(jnp.float8_e4m3fn)
            y = jnp.dot(x_q.astype(jnp.float32), k_q.astype(jnp.float32), preferred_element_type=jnp.float32)
            return y * (s_in * s_k)
        key = jax.random.key(seed)
        kx, kk, kb = jax.random.split(key, 3)
        x = jax.random.normal(kx, (4, 1024, D_IN), dtype=jnp.float32)
        limit = np.sqrt(6.0 / (D_IN + FEATURES)).astype(np.float32)
        kernel = jax.random.uniform(kk, (D_IN, FEATURES), dtype=jnp.float32, minval=-limit, maxval=limit).astype(jnp.bfloat16)
        input_scale = jnp.ones((1,), dtype=jnp.float32)
        kernel_scale = jnp.ones((1,), dtype=jnp.float32)
        bias = jnp.zeros((FEATURES,), dtype=jnp.bfloat16)
        return {'x': x, 'kernel': kernel, 'input_scale': input_scale, 'kernel_scale': kernel_scale, 'bias': bias}
    _L3_ffn_all = _L3_ffn_setup()
    _L3_ffn_in = {k: v for k, v in _L3_ffn_all.items() if k in ('kernel', 'input_scale', 'kernel_scale', 'bias')}
    del _L3_ffn_all
    return {'x': x, 'ctx_1024': ctx_1024, 'mask_1x1xSxS2_bk0': mask_1x1xSxS2_bk0, 'mask_Bx1x1xS2_ik0': mask_Bx1x1xS2_ik0, 'mask_1x1xSxS2_ik0': mask_1x1xSxS2_ik0, 'L0_attn_wq': _L0_attn_in['wq'], 'L0_attn_bq': _L0_attn_in['bq'], 'L0_attn_wk': _L0_attn_in['wk'], 'L0_attn_bk': _L0_attn_in['bk'], 'L0_attn_wv': _L0_attn_in['wv'], 'L0_attn_bv': _L0_attn_in['bv'], 'L0_attn_wo': _L0_attn_in['wo'], 'L0_attn_bo': _L0_attn_in['bo'], 'L0_xattn_Wq_c': _L0_xattn_in['Wq_c'], 'L0_xattn_bq_c': _L0_xattn_in['bq_c'], 'L0_xattn_Wk_s': _L0_xattn_in['Wk_s'], 'L0_xattn_bk_s': _L0_xattn_in['bk_s'], 'L0_xattn_Wv_s': _L0_xattn_in['Wv_s'], 'L0_xattn_bv_s': _L0_xattn_in['bv_s'], 'L0_xattn_Wq_s': _L0_xattn_in['Wq_s'], 'L0_xattn_bq_s': _L0_xattn_in['bq_s'], 'L0_xattn_Wk_c': _L0_xattn_in['Wk_c'], 'L0_xattn_bk_c': _L0_xattn_in['bk_c'], 'L0_xattn_Wv_c': _L0_xattn_in['Wv_c'], 'L0_xattn_bv_c': _L0_xattn_in['bv_c'], 'L0_xattn_Wg': _L0_xattn_in['Wg'], 'L0_xattn_bg': _L0_xattn_in['bg'], 'L0_ffn_wqkv': _L0_ffn_in['wqkv'], 'L0_ffn_q_scale': _L0_ffn_in['q_scale'], 'L0_ffn_k_scale': _L0_ffn_in['k_scale'], 'L0_ffn_wo': _L0_ffn_in['wo'], 'L0_ffn_ln_g': _L0_ffn_in['ln_g'], 'L0_ffn_ln_b': _L0_ffn_in['ln_b'], 'L0_ffn_w1': _L0_ffn_in['w1'], 'L0_ffn_b1': _L0_ffn_in['b1'], 'L0_ffn_w2': _L0_ffn_in['w2'], 'L0_ffn_b2': _L0_ffn_in['b2'], 'L1_attn_wq': _L1_attn_in['wq'], 'L1_attn_w_kv_down': _L1_attn_in['w_kv_down'], 'L1_attn_w_k_up': _L1_attn_in['w_k_up'], 'L1_attn_w_v_up': _L1_attn_in['w_v_up'], 'L1_attn_wo': _L1_attn_in['wo'], 'L1_xattn_Wq': _L1_xattn_in['Wq'], 'L1_xattn_Wk': _L1_xattn_in['Wk'], 'L1_xattn_Wv': _L1_xattn_in['Wv'], 'L1_xattn_Wo': _L1_xattn_in['Wo'], 'L1_xattn_bo': _L1_xattn_in['bo'], 'L1_ffn_Wr': _L1_ffn_in['Wr'], 'L1_ffn_br': _L1_ffn_in['br'], 'L1_ffn_W1': _L1_ffn_in['W1'], 'L1_ffn_b1': _L1_ffn_in['b1'], 'L1_ffn_W2': _L1_ffn_in['W2'], 'L1_ffn_b2': _L1_ffn_in['b2'], 'L2_attn_Wq': _L2_attn_in['Wq'], 'L2_attn_bq': _L2_attn_in['bq'], 'L2_attn_Wk': _L2_attn_in['Wk'], 'L2_attn_bk': _L2_attn_in['bk'], 'L2_attn_Wv': _L2_attn_in['Wv'], 'L2_attn_bv': _L2_attn_in['bv'], 'L2_attn_Wo': _L2_attn_in['Wo'], 'L2_attn_bo': _L2_attn_in['bo'], 'L2_xattn_Wq': _L2_xattn_in['Wq'], 'L2_xattn_bq': _L2_xattn_in['bq'], 'L2_xattn_Wk': _L2_xattn_in['Wk'], 'L2_xattn_bk': _L2_xattn_in['bk'], 'L2_xattn_Wv': _L2_xattn_in['Wv'], 'L2_xattn_bv': _L2_xattn_in['bv'], 'L2_xattn_Wo': _L2_xattn_in['Wo'], 'L2_xattn_bo': _L2_xattn_in['bo'], 'L2_ffn_gate_w': _L2_ffn_in['gate_w'], 'L2_ffn_gate_b': _L2_ffn_in['gate_b'], 'L2_ffn_w1': _L2_ffn_in['w1'], 'L2_ffn_b1': _L2_ffn_in['b1'], 'L2_ffn_w2': _L2_ffn_in['w2'], 'L2_ffn_b2': _L2_ffn_in['b2'], 'L3_attn_Wq': _L3_attn_in['Wq'], 'L3_attn_bq': _L3_attn_in['bq'], 'L3_attn_Wk': _L3_attn_in['Wk'], 'L3_attn_bk': _L3_attn_in['bk'], 'L3_attn_Wv': _L3_attn_in['Wv'], 'L3_attn_bv': _L3_attn_in['bv'], 'L3_attn_Wo': _L3_attn_in['Wo'], 'L3_attn_bo': _L3_attn_in['bo'], 'L3_attn_token_positions': _L3_attn_in['token_positions'], 'L3_xattn_Wq': _L3_xattn_in['Wq'], 'L3_xattn_bq': _L3_xattn_in['bq'], 'L3_xattn_Wk': _L3_xattn_in['Wk'], 'L3_xattn_bk': _L3_xattn_in['bk'], 'L3_xattn_Wv': _L3_xattn_in['Wv'], 'L3_xattn_bv': _L3_xattn_in['bv'], 'L3_ffn_kernel': _L3_ffn_in['kernel'], 'L3_ffn_input_scale': _L3_ffn_in['input_scale'], 'L3_ffn_kernel_scale': _L3_ffn_in['kernel_scale'], 'L3_ffn_bias': _L3_ffn_in['bias']}

def reference(x, ctx_1024, mask_1x1xSxS2_bk0, mask_Bx1x1xS2_ik0, mask_1x1xSxS2_ik0, L0_attn_wq, L0_attn_bq, L0_attn_wk, L0_attn_bk, L0_attn_wv, L0_attn_bv, L0_attn_wo, L0_attn_bo, L0_xattn_Wq_c, L0_xattn_bq_c, L0_xattn_Wk_s, L0_xattn_bk_s, L0_xattn_Wv_s, L0_xattn_bv_s, L0_xattn_Wq_s, L0_xattn_bq_s, L0_xattn_Wk_c, L0_xattn_bk_c, L0_xattn_Wv_c, L0_xattn_bv_c, L0_xattn_Wg, L0_xattn_bg, L0_ffn_wqkv, L0_ffn_q_scale, L0_ffn_k_scale, L0_ffn_wo, L0_ffn_ln_g, L0_ffn_ln_b, L0_ffn_w1, L0_ffn_b1, L0_ffn_w2, L0_ffn_b2, L1_attn_wq, L1_attn_w_kv_down, L1_attn_w_k_up, L1_attn_w_v_up, L1_attn_wo, L1_xattn_Wq, L1_xattn_Wk, L1_xattn_Wv, L1_xattn_Wo, L1_xattn_bo, L1_ffn_Wr, L1_ffn_br, L1_ffn_W1, L1_ffn_b1, L1_ffn_W2, L1_ffn_b2, L2_attn_Wq, L2_attn_bq, L2_attn_Wk, L2_attn_bk, L2_attn_Wv, L2_attn_bv, L2_attn_Wo, L2_attn_bo, L2_xattn_Wq, L2_xattn_bq, L2_xattn_Wk, L2_xattn_bk, L2_xattn_Wv, L2_xattn_bv, L2_xattn_Wo, L2_xattn_bo, L2_ffn_gate_w, L2_ffn_gate_b, L2_ffn_w1, L2_ffn_b1, L2_ffn_w2, L2_ffn_b2, L3_attn_Wq, L3_attn_bq, L3_attn_Wk, L3_attn_bk, L3_attn_Wv, L3_attn_bv, L3_attn_Wo, L3_attn_bo, L3_attn_token_positions, L3_xattn_Wq, L3_xattn_bq, L3_xattn_Wk, L3_xattn_bk, L3_xattn_Wv, L3_xattn_bv, L3_ffn_kernel, L3_ffn_input_scale, L3_ffn_kernel_scale, L3_ffn_bias):
    import jax
    import jax.numpy as jnp

    def _L0_attn_ref(x, wq, bq, wk, bk, wv, bv, wo, bo):
        import jax, jax.numpy as jnp
        import numpy as np
        import math
        DIM = 128
        N_HEADS = 16
        HEAD_DIM = DIM // N_HEADS

        def rope(x):
            S = x.shape[-2]
            D = x.shape[-1]
            pos = jnp.arange(S, dtype=x.dtype)[:, None]
            dim = jnp.arange(D // 2, dtype=x.dtype)[None, :]
            theta = pos / jnp.exp(2.0 * dim / D * math.log(10000.0))
            sin = jnp.sin(theta)[None, None]
            cos = jnp.cos(theta)[None, None]
            x1 = x[..., ::2]
            x2 = x[..., 1::2]
            out1 = x1 * cos - x2 * sin
            out2 = x1 * sin + x2 * cos
            return jnp.stack([out1, out2], axis=-1).reshape(x.shape)
        B, S, _ = x.shape

        def proj(w, b):
            y = jnp.einsum('bsd,ed->bse', x, w) + b
            return y.reshape(B, S, N_HEADS, HEAD_DIM).transpose(0, 2, 1, 3)
        q = rope(proj(wq, bq))
        k = rope(proj(wk, bk))
        v = proj(wv, bv)
        score = jnp.einsum('bhqd,bhkd->bhqk', q, k) / math.sqrt(HEAD_DIM)
        causal = jnp.tril(jnp.ones((S, S), dtype=bool))
        score = jnp.where(causal[None, None], score, -jnp.inf)
        attn = jax.nn.softmax(score, axis=-1)
        out = jnp.einsum('bhqk,bhkd->bhqd', attn, v)
        out = out.transpose(0, 2, 1, 3).reshape(B, S, DIM)
        return jnp.einsum('bsd,ed->bse', out, wo) + bo

    def _L0_xattn_ref(char_emb, subword_emb, Wq_c, bq_c, Wk_s, bk_s, Wv_s, bv_s, Wq_s, bq_s, Wk_c, bk_c, Wv_c, bv_c, Wg, bg):
        import jax, jax.numpy as jnp
        import numpy as np
        H = 128
        B = 8
        L_CHAR = 256
        L_SUB = 128

        def _linear(x, W, b):
            return jnp.einsum('blh,oh->blo', x, W) + b

        def _interp_linear(x, out_len):
            L_in = x.shape[1]
            pos = (jnp.arange(out_len, dtype=x.dtype) + 0.5) * (L_in / out_len) - 0.5
            pos = jnp.clip(pos, 0.0, L_in - 1)
            lo = jnp.floor(pos).astype(jnp.int32)
            hi = jnp.minimum(lo + 1, L_in - 1)
            w = (pos - lo.astype(x.dtype))[None, :, None]
            return x[:, lo] * (1 - w) + x[:, hi] * w
        h = char_emb.shape[-1]
        scale = 1.0 / jnp.sqrt(jnp.asarray(h, char_emb.dtype))
        Q_char = _linear(char_emb, Wq_c, bq_c)
        K_sub = _linear(subword_emb, Wk_s, bk_s)
        V_sub = _linear(subword_emb, Wv_s, bv_s)
        scores = jnp.einsum('bqh,bkh->bqk', Q_char, K_sub) * scale
        char2sub = jnp.einsum('bqk,bkh->bqh', jax.nn.softmax(scores, axis=-1), V_sub)
        Q_sub = _linear(subword_emb, Wq_s, bq_s)
        K_char = _linear(char_emb, Wk_c, bk_c)
        V_char = _linear(char_emb, Wv_c, bv_c)
        scores2 = jnp.einsum('bqh,bkh->bqk', Q_sub, K_char) * scale
        sub2char = jnp.einsum('bqk,bkh->bqh', jax.nn.softmax(scores2, axis=-1), V_char)
        L_char = char_emb.shape[1]
        if sub2char.shape[1] != L_char:
            sub2char = _interp_linear(sub2char, L_char)
        gate_in = jnp.concatenate([char2sub, sub2char], axis=-1)
        gate = jax.nn.sigmoid(jnp.einsum('blh,oh->blo', gate_in, Wg) + bg)
        return gate * char2sub + (1 - gate) * sub2char

    def _L0_ffn_ref(x, wqkv, q_scale, k_scale, wo, ln_g, ln_b, w1, b1, w2, b2):
        import jax, jax.numpy as jnp
        import numpy as np
        DIM = 128
        DEPTH = 2
        HEADS = 8
        DIM_HEAD = 64
        WINDOW = 64
        INNER = HEADS * DIM_HEAD
        HID = int(DIM * 4 * 2 / 3)
        B, N = (2, 1024)
        QK_SCALE = 8.0

        def shift_token(t):
            t1, t2 = jnp.split(t, 2, axis=-1)
            t2 = jnp.pad(t2, ((0, 0), (1, 0), (0, 0)))[:, :-1]
            return jnp.concatenate([t1, t2], axis=-1)

        def l2norm(t):
            return t / jnp.clip(jnp.linalg.norm(t, axis=-1, keepdims=True), 1e-12)

        def rotate_half(x):
            x1, x2 = jnp.split(x, 2, axis=-1)
            return jnp.concatenate([-x2, x1], axis=-1)

        def rotary_xpos(q, k):
            n = q.shape[-2]
            half_idx = jnp.arange(0, DIM_HEAD, 2, dtype=jnp.float32)
            inv_freq = 1.0 / 10000.0 ** (half_idx / DIM_HEAD)
            t = jnp.arange(n, dtype=jnp.float32)
            freqs = t[:, None] * inv_freq[None, :]
            freqs = jnp.concatenate([freqs, freqs], axis=-1)
            base = (half_idx + 0.4 * DIM_HEAD) / (1.4 * DIM_HEAD)
            power = (t - n // 2) / float(WINDOW // 2)
            scale = base[None, :] ** power[:, None]
            scale = jnp.concatenate([scale, scale], axis=-1)
            cos, sin = (jnp.cos(freqs), jnp.sin(freqs))
            q = q * cos * scale + rotate_half(q) * sin * scale
            k = k * cos / scale + rotate_half(k) * sin / scale
            return (q, k)

        def local_attention(q, k, v):
            b, h, n, d = q.shape
            w = n // WINDOW
            bq = q.reshape(b, h, w, WINDOW, d) * QK_SCALE
            bk = k.reshape(b, h, w, WINDOW, d)
            bv = v.reshape(b, h, w, WINDOW, d)

            def look_around(t):
                p = jnp.pad(t, ((0, 0), (0, 0), (1, 0), (0, 0), (0, 0)))
                return jnp.concatenate([p[:, :, :w], p[:, :, 1:]], axis=3)
            bk, bv = (look_around(bk), look_around(bv))
            bt = jnp.arange(n).reshape(w, WINDOW)
            btp = jnp.pad(bt, ((1, 0), (0, 0)), constant_values=-1)
            btk = jnp.concatenate([btp[:w], btp[1:]], axis=1)
            sim = jnp.einsum('bhwid,bhwjd->bhwij', bq, bk)
            i = bt[:, :, None]
            j = btk[:, None, :]
            mask = (i < j) | (i > j + WINDOW) | (j == -1)
            sim = jnp.where(mask, -jnp.finfo(sim.dtype).max, sim)
            attn = jax.nn.softmax(sim, axis=-1)
            out = jnp.einsum('bhwij,bhwjd->bhwid', attn, bv)
            return out.reshape(b, h, n, d)

        def _layer(x, wqkv, qs, ksc, wo, lg, lb, w1, b1, w2, b2):
            b, n, _ = x.shape
            h = shift_token(x)
            qkv = h @ wqkv
            q, k, v = jnp.split(qkv, 3, axis=-1)
            to_heads = lambda t: t.reshape(b, n, HEADS, DIM_HEAD).transpose(0, 2, 1, 3)
            q, k, v = (to_heads(q), to_heads(k), to_heads(v))
            q = l2norm(q) * qs
            k = l2norm(k) * ksc
            q, k = rotary_xpos(q, k)
            o = local_attention(q, k, v)
            o = o.transpose(0, 2, 1, 3).reshape(b, n, INNER)
            x = x + o @ wo
            h = shift_token(x)
            mu = h.mean(-1, keepdims=True)
            var = h.var(-1, keepdims=True)
            h = (h - mu) / jnp.sqrt(var + 1e-05) * lg + lb
            h = h @ w1 + b1
            a, g = jnp.split(h, 2, axis=-1)
            h = a * jax.nn.gelu(g, approximate=False)
            x = x + h @ w2 + b2
            return x
        for l in range(DEPTH):
            x = _layer(x, wqkv[l], q_scale[l], k_scale[l], wo[l], ln_g[l], ln_b[l], w1[l], b1[l], w2[l], b2[l])
        return x

    def _L1_attn_ref(x, wq, w_kv_down, w_k_up, w_v_up, wo):
        import jax, jax.numpy as jnp
        import numpy as np
        N_HEADS = 16
        HEAD_DIM = 64
        ROPE_THETA = 10000.0

        def _rope_cos_sin(seq_len, dim, theta):
            inv_freq = 1.0 / theta ** (jnp.arange(0, dim, 2, dtype=jnp.float32) / dim)
            pos = jnp.arange(seq_len, dtype=jnp.float32)
            freqs = pos[:, None] * inv_freq[None, :]
            emb = jnp.concatenate([freqs, freqs], axis=-1)
            return (jnp.cos(emb), jnp.sin(emb))

        def _rotate_half(x):
            d = x.shape[-1] // 2
            return jnp.concatenate([-x[..., d:], x[..., :d]], axis=-1)
        B, S, _ = x.shape
        H, D = (N_HEADS, HEAD_DIM)
        q = jnp.einsum('bsd,qd->bsq', x, wq).reshape(B, S, H, D).transpose(0, 2, 1, 3)
        kv_latent = jnp.einsum('bsd,ld->bsl', x, w_kv_down)
        k = jnp.einsum('bsl,ql->bsq', kv_latent, w_k_up).reshape(B, S, H, D).transpose(0, 2, 1, 3)
        v = jnp.einsum('bsl,ql->bsq', kv_latent, w_v_up).reshape(B, S, H, D).transpose(0, 2, 1, 3)
        cos, sin = _rope_cos_sin(S, D, ROPE_THETA)
        cos = cos[None, None]
        sin = sin[None, None]
        q = q * cos + _rotate_half(q) * sin
        k = k * cos + _rotate_half(k) * sin
        scores = jnp.einsum('bhsd,bhtd->bhst', q, k) / jnp.sqrt(jnp.float32(D))
        causal = jnp.triu(jnp.full((S, S), -jnp.inf, dtype=jnp.float32), k=1)
        scores = scores + causal[None, None]
        probs = jax.nn.softmax(scores.astype(jnp.float32), axis=-1).astype(q.dtype)
        out = jnp.einsum('bhst,bhtd->bhsd', probs, v)
        out = out.transpose(0, 2, 1, 3).reshape(B, S, H * D)
        return jnp.einsum('bsq,dq->bsd', out, wo)

    def _L1_xattn_ref(key, query, value, Wq, Wk, Wv, Wo, bo, mask):
        import jax, jax.numpy as jnp
        import numpy as np
        EMBED_DIM = 128
        HEADS = 16
        D_K = EMBED_DIM // HEADS
        B, S = (2, 256)

        def _split_heads(x):
            b, s, _ = x.shape
            return x.reshape(b, s, HEADS, D_K).transpose(0, 2, 1, 3)
        b, q_len = (query.shape[0], query.shape[1])
        k = _split_heads(key @ Wk.T)
        q = _split_heads(query @ Wq.T)
        v = _split_heads(value @ Wv.T)
        scores = jnp.einsum('bhqd,bhkd->bhqk', q, k) / np.sqrt(D_K)
        scores = jnp.where(mask, scores, jnp.float32(-1e+20))
        attn = jax.nn.softmax(scores, axis=-1)
        out = jnp.einsum('bhqk,bhkd->bhqd', attn, v)
        out = out.transpose(0, 2, 1, 3).reshape(b, q_len, HEADS * D_K)
        return out @ Wo.T + bo

    def _L1_ffn_ref(x, Wr, br, W1, b1, W2, b2):
        import jax, jax.numpy as jnp
        import numpy as np
        D_MODEL, D_FF, N_EXP = (128, 512, 8)
        B, S, D = x.shape
        xf = x.reshape(-1, D)
        logits = xf @ Wr.T + br
        expert_idx = jnp.argmax(logits, axis=-1)
        h = jax.nn.relu(jnp.einsum('td,efd->etf', xf, W1) + b1[:, None, :])
        y = jnp.einsum('etf,edf->etd', h, W2) + b2[:, None, :]
        out = y[expert_idx, jnp.arange(xf.shape[0])]
        return out.reshape(B, S, D)

    def _L2_attn_ref(x, Wq, bq, Wk, bk, Wv, bv, Wo, bo):
        import math
        import jax, jax.numpy as jnp
        import numpy as np
        D_MODEL = 128
        N_HEADS = 16
        D_HEAD = D_MODEL // N_HEADS

        def get_alibi_slopes(n_heads: int) -> np.ndarray:

            def pow2_slopes(n):
                start = 2 ** (-2 ** (-(math.log2(n) - 3)))
                return np.array([start * start ** i for i in range(n)], dtype=np.float32)
            if math.log2(n_heads).is_integer():
                return pow2_slopes(n_heads)
            closest = 2 ** math.floor(math.log2(n_heads))
            slopes = pow2_slopes(closest)
            extra = pow2_slopes(2 * closest)[0::2][:n_heads - closest]
            return np.concatenate([slopes, extra], axis=0)
        B, S, D = x.shape
        H, Dh = (N_HEADS, D_HEAD)
        q = (x @ Wq.T + bq).reshape(B, S, H, Dh).transpose(0, 2, 1, 3)
        k = (x @ Wk.T + bk).reshape(B, S, H, Dh).transpose(0, 2, 1, 3)
        v = (x @ Wv.T + bv).reshape(B, S, H, Dh).transpose(0, 2, 1, 3)
        scores = jnp.einsum('bhqd,bhkd->bhqk', q, k) / math.sqrt(Dh)
        slopes = jnp.asarray(get_alibi_slopes(H), dtype=scores.dtype)
        pos = jnp.arange(S, dtype=scores.dtype)
        pos_diff = pos[None, :] - pos[:, None]
        alibi = slopes[:, None, None] * pos_diff[None, :, :]
        scores = scores + alibi[None]
        causal = jnp.tril(jnp.ones((S, S), dtype=bool))
        scores = jnp.where(causal[None, None], scores, -jnp.inf)
        weights = jax.nn.softmax(scores, axis=-1)
        y = jnp.einsum('bhqk,bhkd->bhqd', weights, v)
        y = y.transpose(0, 2, 1, 3).reshape(B, S, D)
        return y @ Wo.T + bo

    def _L2_xattn_ref(q, k, v, Wq, bq, Wk, bk, Wv, bv, Wo, bo):
        import jax, jax.numpy as jnp
        import numpy as np
        D_MODEL = 128
        NHEAD = 16
        HEAD_DIM = D_MODEL // NHEAD
        B, S, D = q.shape
        H, Hd = (NHEAD, HEAD_DIM)
        qh = (q @ Wq.T + bq).reshape(B, S, H, Hd).transpose(0, 2, 1, 3)
        kh = (k @ Wk.T + bk).reshape(B, S, H, Hd).transpose(0, 2, 1, 3)
        vh = (v @ Wv.T + bv).reshape(B, S, H, Hd).transpose(0, 2, 1, 3)
        scores = jnp.einsum('bhqd,bhkd->bhqk', qh, kh) / jnp.sqrt(jnp.float32(Hd))
        attn = jax.nn.softmax(scores, axis=-1)
        out = jnp.einsum('bhqk,bhkd->bhqd', attn, vh)
        out = out.transpose(0, 2, 1, 3).reshape(B, S, D)
        return out @ Wo.T + bo

    def _L2_ffn_ref(inputs, gate_w, gate_b, w1, b1, w2, b2):
        import jax, jax.numpy as jnp
        import numpy as np
        NUM_EXPERTS = 8
        CAPACITY = 80
        D = inputs.shape[-1]
        tokens = inputs.reshape(-1, D)
        logits = tokens @ gate_w + gate_b
        probs = jax.nn.softmax(logits, axis=-1)
        expert_idx = jnp.argmax(probs, axis=-1)
        mask1 = jax.nn.one_hot(expert_idx, NUM_EXPERTS, dtype=jnp.float32)
        pos = jnp.sum(jnp.cumsum(mask1, axis=0) * mask1, axis=-1) - 1.0
        pos = pos.astype(jnp.int32)
        keep = (pos < CAPACITY).astype(jnp.float32)
        gate_prob = jnp.sum(probs * mask1, axis=-1)
        pos_oh = jax.nn.one_hot(pos, CAPACITY, dtype=jnp.float32)
        sec_mask = mask1[:, :, None] * pos_oh[:, None, :] * keep[:, None, None]
        combine_weights = sec_mask * gate_prob[:, None, None]
        dispatch = jnp.einsum('nec,nd->ecd', sec_mask, tokens)
        h = jax.nn.gelu(jnp.einsum('ecd,edf->ecf', dispatch, w1) + b1[:, None, :])
        expert_out = jnp.einsum('ecf,efd->ecd', h, w2) + b2[:, None, :]
        out = jnp.einsum('nec,ecd->nd', combine_weights, expert_out)
        return out.reshape(inputs.shape)

    def _L3_attn_ref(x, Wq, bq, Wk, bk, Wv, bv, Wo, bo, token_positions):
        import jax, jax.numpy as jnp
        import numpy as np
        D_MODEL = 128
        NUM_HEADS = 16
        D_K = D_MODEL // NUM_HEADS
        THETA = 10000.0
        NEG_INF = -1000000000.0

        def _rope(x, positions):
            half = D_K // 2
            inv_freq = 1.0 / THETA ** (jnp.arange(0, D_K, 2, dtype=jnp.float32) / D_K)
            angles = positions.astype(jnp.float32)[:, None] * inv_freq
            cos, sin = (jnp.cos(angles), jnp.sin(angles))
            xe = x[..., 0::2]
            xo = x[..., 1::2]
            re = xe * cos - xo * sin
            ro = xe * sin + xo * cos
            return jnp.stack([re, ro], axis=-1).reshape(x.shape).astype(x.dtype)
        B, S, D = x.shape
        Q = x @ Wq.T + bq
        K = x @ Wk.T + bk
        V = x @ Wv.T + bv

        def split_heads(t):
            return t.reshape(B, S, NUM_HEADS, D_K).transpose(0, 2, 1, 3)
        Q, K, V = (split_heads(Q), split_heads(K), split_heads(V))
        pos = jnp.arange(S)
        Q = _rope(Q, pos)
        K = _rope(K, pos)
        scale = 1.0 / jnp.sqrt(jnp.float32(D_K))
        scores = jnp.einsum('bhqd,bhkd->bhqk', Q, K) * scale
        causal = jnp.tril(jnp.ones((S, S), dtype=bool))
        scores = jnp.where(causal, scores, NEG_INF)
        weights = jax.nn.softmax(scores, axis=-1)
        attn = jnp.einsum('bhqk,bhkd->bhqd', weights, V)
        concat = attn.transpose(0, 2, 1, 3).reshape(B, S, D)
        return concat @ Wo.T + bo

    def _L3_xattn_ref(query, key, value, pad_mask, subsq_mask, Wq, bq, Wk, bk, Wv, bv):
        import jax, jax.numpy as jnp
        import numpy as np
        E, H = (128, 16)
        N, S, T = (2, 256, 256)
        n, s, e = query.shape
        t = value.shape[1]
        d = e // H
        q = (query @ Wq.T + bq).reshape(n, s, H, d).transpose(0, 2, 1, 3)
        k = (key @ Wk.T + bk).reshape(n, t, H, d).transpose(0, 2, 1, 3)
        v = (value @ Wv.T + bv).reshape(n, t, H, d).transpose(0, 2, 1, 3)
        att = jnp.einsum('bhsd,bhtd->bhst', q, k) / jnp.sqrt(jnp.float32(d))
        att = jnp.where(pad_mask == 0, jnp.float32(-1000000000.0), att)
        att = jnp.where(subsq_mask == 0, jnp.float32(-1000000000.0), att)
        prob = jax.nn.softmax(att, axis=-1)
        out = jnp.einsum('bhst,bhtd->bhsd', prob, v)
        return out.transpose(0, 2, 1, 3).reshape(n, s, e)

    def _L3_ffn_ref(x, kernel, input_scale, kernel_scale, bias):
        import jax, jax.numpy as jnp
        import numpy as np
        FEATURES = 128
        D_IN = 128

        def fp8_gemm_optimized(x, input_scale, kernel, kernel_scale):
            s_in = input_scale[0]
            s_k = kernel_scale[0]
            x_q = (x.astype(jnp.float32) / s_in).astype(jnp.float8_e4m3fn)
            k_q = (kernel.astype(jnp.float32) / s_k).astype(jnp.float8_e4m3fn)
            y = jnp.dot(x_q.astype(jnp.float32), k_q.astype(jnp.float32), preferred_element_type=jnp.float32)
            return y * (s_in * s_k)
        dtype = jnp.bfloat16
        x = x.astype(dtype)
        orig_shape = x.shape
        x2 = x.reshape(-1, x.shape[-1])
        y = fp8_gemm_optimized(x2, input_scale, kernel, kernel_scale)
        y = y.astype(dtype) + bias
        return y.reshape(orig_shape[:-1] + (FEATURES,))
    x = _layernorm(x + _L0_attn_ref(x, L0_attn_wq, L0_attn_bq, L0_attn_wk, L0_attn_bk, L0_attn_wv, L0_attn_bv, L0_attn_wo, L0_attn_bo), axis=-1)
    x = _layernorm(x + _L0_xattn_ref(x, ctx_1024, L0_xattn_Wq_c, L0_xattn_bq_c, L0_xattn_Wk_s, L0_xattn_bk_s, L0_xattn_Wv_s, L0_xattn_bv_s, L0_xattn_Wq_s, L0_xattn_bq_s, L0_xattn_Wk_c, L0_xattn_bk_c, L0_xattn_Wv_c, L0_xattn_bv_c, L0_xattn_Wg, L0_xattn_bg), axis=-1)
    x = _layernorm(x + _L0_ffn_ref(x, L0_ffn_wqkv, L0_ffn_q_scale, L0_ffn_k_scale, L0_ffn_wo, L0_ffn_ln_g, L0_ffn_ln_b, L0_ffn_w1, L0_ffn_b1, L0_ffn_w2, L0_ffn_b2), axis=-1)
    x = _layernorm(x + _L1_attn_ref(x, L1_attn_wq, L1_attn_w_kv_down, L1_attn_w_k_up, L1_attn_w_v_up, L1_attn_wo), axis=-1)
    x = _layernorm(x + _L1_xattn_ref(ctx_1024, x, ctx_1024, L1_xattn_Wq, L1_xattn_Wk, L1_xattn_Wv, L1_xattn_Wo, L1_xattn_bo, mask_1x1xSxS2_bk0), axis=-1)
    x = _layernorm(x + _L1_ffn_ref(x, L1_ffn_Wr, L1_ffn_br, L1_ffn_W1, L1_ffn_b1, L1_ffn_W2, L1_ffn_b2), axis=-1)
    x = _layernorm(x + _L2_attn_ref(x, L2_attn_Wq, L2_attn_bq, L2_attn_Wk, L2_attn_bk, L2_attn_Wv, L2_attn_bv, L2_attn_Wo, L2_attn_bo), axis=-1)
    x = _layernorm(x + _L2_xattn_ref(x, ctx_1024, ctx_1024, L2_xattn_Wq, L2_xattn_bq, L2_xattn_Wk, L2_xattn_bk, L2_xattn_Wv, L2_xattn_bv, L2_xattn_Wo, L2_xattn_bo), axis=-1)
    x = _layernorm(x + _L2_ffn_ref(x, L2_ffn_gate_w, L2_ffn_gate_b, L2_ffn_w1, L2_ffn_b1, L2_ffn_w2, L2_ffn_b2), axis=-1)
    x = _layernorm(x + _L3_attn_ref(x, L3_attn_Wq, L3_attn_bq, L3_attn_Wk, L3_attn_bk, L3_attn_Wv, L3_attn_bv, L3_attn_Wo, L3_attn_bo, L3_attn_token_positions), axis=-1)
    x = _layernorm(x + _L3_xattn_ref(x, ctx_1024, ctx_1024, mask_Bx1x1xS2_ik0, mask_1x1xSxS2_ik0, L3_xattn_Wq, L3_xattn_bq, L3_xattn_Wk, L3_xattn_bk, L3_xattn_Wv, L3_xattn_bv), axis=-1)
    x = _layernorm(x + _L3_ffn_ref(x, L3_ffn_kernel, L3_ffn_input_scale, L3_ffn_kernel_scale, L3_ffn_bias), axis=-1)
    return x

_drawn_inputs = setup_inputs


def setup_inputs(seed=0):
    import zlib

    import numpy as np

    out = dict(_drawn_inputs(seed))
    spreads = {'L0_attn_bq': (0.0, 0.1),
     'L0_attn_bk': (0.0, 0.33),
     'L0_attn_bv': (0.0, 0.1),
     'L0_attn_bo': (0.0, 0.1),
     'L0_ffn_q_scale': (1.0, 0.6),
     'L0_ffn_k_scale': (1.0, 0.6),
     'L0_ffn_ln_g': (1.0, 0.6),
     'L0_ffn_ln_b': (0.0, 0.8),
     'L0_ffn_b1': (0.0, 0.691),
     'L0_ffn_b2': (0.0, 0.1),
     'L2_attn_bq': (0.0, 0.505),
     'L2_attn_bk': (0.0, 0.8),
     'L2_attn_bv': (0.0, 0.1),
     'L2_attn_bo': (0.0, 0.1),
     'L2_xattn_bq': (0.0, 0.359),
     'L2_xattn_bk': (0.0, 0.8),
     'L2_xattn_bv': (0.0, 0.1),
     'L2_xattn_bo': (0.0, 0.1),
     'L2_ffn_gate_b': (0.0, 0.624),
     'L2_ffn_b1': (0.0, 0.8),
     'L2_ffn_b2': (0.0, 0.702),
     'L3_attn_bq': (0.0, 0.561),
     'L3_attn_bk': (0.0, 0.674),
     'L3_attn_bv': (0.0, 0.1),
     'L3_attn_bo': (0.0, 0.1),
     'L3_xattn_bq': (0.0, 0.1),
     'L3_xattn_bk': (0.0, 0.8),
     'L3_xattn_bv': (0.0, 0.1)}
    factors = {'L0_xattn_Wq_c': 8.0,
     'L0_xattn_bq_c': 8.0,
     'L0_xattn_Wk_s': 7.692,
     'L0_xattn_bk_s': 8.0,
     'L0_xattn_Wq_s': 8.0,
     'L0_xattn_bq_s': 8.0,
     'L0_xattn_Wk_c': 7.966,
     'L0_xattn_bk_c': 8.0,
     'L0_xattn_Wg': 8.0,
     'L0_xattn_bg': 8.0,
     'L0_ffn_w1': 3.973,
     'L0_ffn_w2': 3.904,
     'L1_ffn_b1': 3.368,
     'L2_ffn_gate_w': 5.185,
     'L2_ffn_w1': 8.0,
     'L2_ffn_w2': 8.0}
    for name, (base, spread) in spreads.items():
        noise = np.random.default_rng([zlib.crc32(name.encode()), seed]).standard_normal(out[name].shape)
        drawn = base * np.exp(spread * noise) if base else spread * noise
        out[name] = jnp.asarray(drawn.astype(out[name].dtype))
    for name, factor in factors.items():
        out[name] = (out[name] * factor).astype(out[name].dtype)
    return out
```

```python
from contextlib import ExitStack

import numpy as np

import concourse.bass as bass
from concourse import mybir

F32 = mybir.dt.float32
BF16 = mybir.dt.bfloat16
FP8 = mybir.dt.float8e4
U8 = mybir.dt.uint8
I32 = mybir.dt.int32
ALU = mybir.AluOpType
ACT = mybir.ActivationFunctionType
X_AXIS = mybir.AxisListType.X
ds = bass.ds

P = 128
B, S, D = 32, 64, 128
TILES = B * S // P
SEQS = P // S
STREAMS = (0, 1)
TURNS = TILES // 2
GROUPS = TILES // 4
GT = 512
H8, HD8 = 16, 8
HID = 341
HCH = [128, 128, 85]
EXP = 8
FF = 512
FCH = FF // P
CAP = 80
EPS = 1e-5
NEG = -1e30
OFF = -1e20
BLOCKS = 12

(L0_ATTN, L0_CROSS, F0_ATTN, F0_GLU, F1_ATTN, F1_GLU, L1_ATTN, L1_CROSS, L1_MOE,
 L2_ATTN, L2_CROSS, L2_MOE, L3_ATTN, L3_CROSS, L3_FP8) = range(15)
PHASES = [1, 2, 6, 7, 8, 9, 10, 11, 12, 13, 14, 15][BLOCKS - 1]

NARROW = (L0_ATTN, L1_CROSS, L2_ATTN, L2_CROSS, L3_ATTN, L3_CROSS)
ROPED = (L0_ATTN, L3_ATTN)
GIVEN_CTX = (L0_CROSS, L1_CROSS, L2_CROSS, L3_CROSS)
PREFIX = {L0_ATTN: "a0", L0_CROSS: "x0", L1_CROSS: "x1", L2_ATTN: "a2", L2_CROSS: "x2", L3_ATTN: "a3", L3_CROSS: "x3"}
WIDE = (F0_ATTN, F1_ATTN, L1_ATTN)
GLU = (F0_GLU, F1_GLU)
ATTN = NARROW + WIDE
TILED = NARROW + WIDE + GLU + (L0_CROSS,)
FINISHED = TILED + (L2_MOE,)
PIPED = NARROW
KEPT = (F0_ATTN, F0_GLU, F1_ATTN)

HAS_OUT = tuple(p for p in ATTN if p != L3_CROSS) + (L0_CROSS,)

FIRES = {
    "x_staged": FINISHED, "x_turned": TILED, "xT_ready": TILED,
    "projected": NARROW + (L0_CROSS,), "rope_biased": ROPED, "rope_scaled": ROPED,
    "qk_ready": NARROW + (L0_CROSS,), "values_ready": ATTN + (L0_CROSS,), "keys_spread": NARROW,
    "scores_ready": ATTN + (L0_CROSS,), "max_ready": ATTN + (L0_CROSS,), "scores_shifted": ATTN + (L0_CROSS,),
    "probs_ready": ATTN + (L0_CROSS,), "probs_turned": ATTN + (L0_CROSS,), "probsT_ready": ATTN + (L0_CROSS,),
    "mixed": ATTN + (L0_CROSS,), "sums_inverted": ATTN + (L0_CROSS,), "heads_normal": ATTN + (L0_CROSS,),
    "heads_turned": HAS_OUT, "headsT_ready": HAS_OUT, "y_ready": tuple(p for p in FINISHED if p != L3_CROSS),
    "sums_ready": (L0_CROSS,), "gate_exp": (L0_CROSS,), "gate_den": (L0_CROSS,), "gate_ready": (L0_CROSS,),
    "paths_diff": (L0_CROSS,), "diff_gated": (L0_CROSS,), "y_mixed": (L0_CROSS,), "biased": (L0_CROSS,),
    "q_projected": WIDE, "k_projected": (L1_ATTN,), "latent_projected": (L1_ATTN,), "latent_ready": (L1_ATTN,),
    "squares": (F0_ATTN, F1_ATTN), "norms_sq": (F0_ATTN, F1_ATTN), "norms_floor": (F0_ATTN, F1_ATTN),
    "norms_inv": (F0_ATTN, F1_ATTN), "unit_ready": (F0_ATTN, F1_ATTN),
    "dispatched_made": (L2_MOE,), "dispatch_turned": (L2_MOE,), "dispatchT_ready": (L2_MOE,),
    "q_parts": WIDE, "q_rotated": WIDE, "q_turned": WIDE, "qT_ready": WIDE,
    "k_parts": (L1_ATTN,), "k_rotated": (L1_ATTN,), "k_turned": (L1_ATTN,), "kT_ready": (L1_ATTN,),
    "v_projected": WIDE,
    "h_turned": GLU, "h_stats": GLU, "h_mean": GLU, "h_var": GLU, "h_rstd": GLU, "h_normal": GLU,
    "hn_turned": GLU, "hnT_ready": GLU, "up_ready": GLU, "gelu_ready": GLU, "gated_ready": GLU,
    "outer_sum": (F1_GLU,), "res_sum": tuple(p for p in FINISHED if p not in KEPT),
    "ln_stats": tuple(p for p in FINISHED if p not in KEPT),
}
for _n in ("ln_mean", "ln_var", "ln_rstd"):
    FIRES[_n] = FIRES["ln_stats"]


def program(nc, packs, dram, out):
    with ExitStack() as ctx:
        def sb(name, shape, dt=F32):
            return ctx.enter_context(nc.sbuf_tensor(name, shape, dt))

        def sem(name):
            return ctx.enter_context(nc.semaphore(name))

        state = sb("state", [P, TILES, D])
        inner = sb("inner", [P, TILES, D])
        ctxT = sb("ctxT", [P, TILES, P])
        weights = {n: sb("w_" + n, [P if n == "scales" else ap.shape[0], ap.shape[1]]) for n, (ap, _) in packs.items()
                   if n not in ("moe1", "moe2", "alibi", "a2", "a3", "x3", "x1", "x2", "m2rows", "scales")}
        experts = sb("experts", [P, packs["moe1"][0].shape[1]])
        weights["moe1"] = weights["moe2"] = experts
        LATE = {"fa0": ("a2", "a3", "x3"), "fa1": ("x1", "x2"), "x0": ("m2rows",)}
        for early, late in LATE.items():
            first = 0
            for n in late:
                rows, cols = packs[n][0].shape
                weights[n] = weights[early][0:rows, first:first + cols]
                first += cols

        def part(pack, name):
            first, cols = packs[pack][1][name]
            return weights[pack][:, first:first + cols]

        ident = part("const", "ident")
        ones_row = sb("ones_row", [1, P])
        ident16 = sb("ident16", [P, P], BF16)
        causal16 = sb("causal16", [P, S], BF16)
        alibi16 = inner[:, 0:12, :].rearrange("p a n -> p (a n)").bitcast(BF16).rearrange("p (n k) -> p n k", n=3)
        rope_f = [sb(f"rope_f{l}", [P, 4 * 64]) for l in range(2)]
        seq_add = sb("seq_add", [P, S], BF16)
        own16 = sb("own16", [P, S], BF16)
        pads16 = sb("pads16", [P, TILES, S], BF16)
        pads_tile = [sb(f"pads_tile{s}", [P, S], BF16) for s in STREAMS]
        minus_half = sb("minus_half", [P, 16])

        BIG = 1024
        VALUES64 = SEQS * 8 * 2 * 65
        SCRATCH = 7 * BIG + VALUES64
        arena = sb("arena", [P, 2 * SCRATCH])

        pads_int = arena[:, 0:TILES * S].bitcast(I32).rearrange("p (t k) -> p t k", t=TILES)

        mask_int = arena[:, 1024:1024 + S].bitcast(I32)
        own_u8 = arena[:, 1088:1088 + S // 4].bitcast(U8)
        weights["scales"] = arena[:, 1152:1152 + 512]

        def big(s, k, cols=1024):
            at0 = s * SCRATCH + k * BIG
            return arena[:, at0:at0 + cols]

        xs = [sb(f"xs{s}", [P, D]) for s in STREAMS]
        cs = [sb(f"cs{s}", [P, P]) for s in STREAMS]
        xT = [sb(f"xT{s}", [P, P]) for s in STREAMS]
        shT = [sb(f"shT{s}", [P, P]) for s in STREAMS]
        total = [sb(f"total{s}", [P, D]) for s in STREAMS]
        stats = [sb(f"stats{s}", [P, 6]) for s in STREAMS]
        moments = [sb(f"moments{s}", [P, 2]) for s in STREAMS]
        var_eps = [sb(f"var_eps{s}", [P, 1]) for s in STREAMS]
        rstd = [sb(f"rstd{s}", [P, 1]) for s in STREAMS]
        maxima = [sb(f"maxima{s}", [P, 16]) for s in STREAMS]
        inv_sum = [sb(f"inv_sum{s}", [P, 16]) for s in STREAMS]
        sq_sum = [sb(f"sq_sum{s}", [P, 16]) for s in STREAMS]
        sq_floor = [sb(f"sq_floor{s}", [P, 16]) for s in STREAMS]
        inv_norm = [sb(f"inv_norm{s}", [P, 16]) for s in STREAMS]
        values8 = [sb(f"values8_{s}", [P, H8 // 2, SEQS, 2, HD8 + 1]) for s in STREAMS]
        heads_out = [sb(f"heads_out{s}", [P, D]) for s in STREAMS]
        outT = [sb(f"outT{s}", [P, 2, P]) for s in STREAMS]
        gate = [sb(f"gate{s}", [P, D]) for s in STREAMS]
        latentT = [big(s, 6, P)[0:S, :] for s in STREAMS]

        ps = [ctx.enter_context(nc.psum_tensor(f"ps{s}", [P, 4, 512], F32)) for s in STREAMS]

        def bank(s, b, lo=0, hi=512):
            return ps[s][:, b, lo:hi]

        def pair(s, b):
            return ps[s][:, b:b + 2, :].rearrange("p a n -> p (a n)")

        signal = {n: sem(n) for n in FIRES}
        tile_done = sem("tile_done")
        setup_done = sem("setup_done")
        x_loaded, ctx_loaded, out_stored = sem("x_loaded"), sem("ctx_loaded"), sem("out_stored")
        loaded = {n: sem("loaded_" + n) for n in packs}
        masks_loaded = sem("masks_loaded")
        tables_ready = sem("tables_ready")
        moe_sems = {n: sem(n) for n in (
            "g_staged", "g_turned", "g_xT", "g_logits", "g_top", "g_eq", "g_rank", "g_first", "g_onehot",
            "g_oneturned", "g_onehotT", "g_bias", "h_done", "relu_done", "ye_done", "acc_done",
            "g_sum", "g_stats", "g_mean", "g_var", "g_rstd")}
        gate_sems = {n: sem(n) for n in (
            "c_logits", "c_chain", "c_shifted", "c_exp", "c_onehot", "c_counts", "c_staged", "c_made", "c_slot",
            "c_dispatched", "c_slotsT", "c_up", "c_gelu", "c_down", "c_out")}
        fp_sems = {n: sem(n) for n in ("f_once", "f_chain", "f_rounded", "f_turned", "f_turned_copy", "f_y")}
        loaded8 = sem("loaded8")

        def at(name, ph, v, s):
            fires = sorted(FIRES[name])
            return 16 * fires.index(ph) + s + 1 + v

        def tiles_done(ph, v, s):
            return 16 * ph + s + 1 + v

        class Turn:

            def __init__(self, eng, ph, turn):
                self.eng, self.ph = eng, ph
                self.v = turn * 2

            def wait(self, name, s, alone=False):
                self.eng.wait_ge(signal[name], at(name, self.ph, self.v, s))
                if alone:
                    self.eng.nop(nofuse=True)

            def tile(self, s):
                return self.v + s

        def piped(eng, ph, body):
            body(None, Turn(eng, ph, 0))
            with eng.Fori(0, TURNS - 1) as turn:
                body(Turn(eng, ph, turn), Turn(eng, ph, turn + 1))
            body(Turn(eng, ph, TURNS - 1), None)

        def turns(eng, ph, body):
            with eng.Fori(0, TURNS) as turn:
                body(Turn(eng, ph, turn))

        def mm(o, lhsT, rhs, start=True, stop=True):
            return nc.tensor.matmul(o, lhsT, rhs, start=start, stop=stop, skip_group_check=True)

        def tile_of(x, t, s):
            return x[:, ds(t.tile(s), 1), :].rearrange("p a n -> p (a n)")

        def stage_pool(t, s, src, context=False):
            if t.ph not in PIPED:
                t.eng.wait_ge(tile_done, tiles_done(t.ph, t.v, s))
            if context:
                nc.gpsimd.tensor_copy(cs[s][:, :], tile_of(ctxT, t, s))
            if t.ph == L3_CROSS:
                nc.gpsimd.tensor_copy(pads_tile[s][:, :], tile_of(pads16, t, s))
            nc.gpsimd.tensor_copy(xs[s][:, :], tile_of(src, t, s))\
                .then_inc(signal["x_staged"], 1)

        def turn_x_pe(t, s):
            t.wait("x_staged", s)
            nc.tensor.transpose(bank(s, 0, 0, P), xs[s][:, :], ident).then_inc(signal["x_turned"], 1)

        def turn_x_act(t, s, shifted):
            t.wait("x_turned", s)
            if not shifted:
                nc.scalar.copy(xT[s][:, :], bank(s, 0, 0, P)).then_inc(signal["xT_ready"], 1)
                return
            nc.scalar.copy(shT[s][0:S, :], ps[s][0:S, 0, 0:P])
            up = shT[s][S:P, :].rearrange("p (b t) -> p b t", b=SEQS)
            nc.scalar.copy(up[:, :, 1:S], ps[s][S:P, 0, 0:P].rearrange("p (b t) -> p b t", b=SEQS)[:, :, 0:S - 1])\
                .then_inc(signal["xT_ready"], 1)

        def norm_pool(t, s):
            t.wait("ln_var", s)
            nc.gpsimd.tensor_tensor(rstd[s][:, :], var_eps[s][:, :], minus_half[:, 0:1], ALU.pow)\
                .then_inc(signal["ln_rstd"], 1)

        def finish_vector(t, y, dst, ready="y_ready", outer=False, src=None):
            kept = t.ph in KEPT
            src = src if src is not None else state
            for s in STREAMS:
                t.wait(ready, s)
                if kept:
                    nc.vector.tensor_tensor(tile_of(dst, t, s), tile_of(src, t, s), y(s), ALU.add)\
                        .then_inc(tile_done, 1)
                elif outer:
                    nc.vector.tensor_tensor(total[s][:, :], tile_of(src, t, s), y(s), ALU.add)\
                        .then_inc(signal["outer_sum"], 1)
                    t.wait("outer_sum", s)
                    nc.vector.tensor_tensor(total[s][:, :], total[s][:, :], tile_of(state, t, s), ALU.add)\
                        .then_inc(signal["res_sum"], 1)
                else:
                    nc.vector.tensor_tensor(total[s][:, :], tile_of(src, t, s), y(s), ALU.add)\
                        .then_inc(signal["res_sum"], 1)
            if kept:
                return
            for s in STREAMS:
                t.wait("res_sum", s)
                nc.vector.bn_stats(stats[s][:, :], total[s][:, :]).then_inc(signal["ln_stats"], 1)
            for s in STREAMS:
                t.wait("ln_stats", s, alone=True)
                nc.vector.bn_aggr(moments[s][:, :], stats[s][:, :]).then_inc(signal["ln_mean"], 1)
            for s in STREAMS:
                t.wait("ln_mean", s)
                nc.vector.tensor_scalar(var_eps[s][:, :], moments[s][:, 1:2], EPS, None, ALU.add)\
                    .then_inc(signal["ln_var"], 1)
            for s in STREAMS:
                t.wait("ln_rstd", s)
                nc.vector.tensor_scalar(tile_of(dst, t, s), total[s][:, :],
                                        moments[s][:, 0:1], rstd[s][:, 0:1], ALU.subtract, ALU.mult)\
                    .then_inc(tile_done, 1)

        def softmax_vector(t, heads):
            half = heads // 2
            for s in STREAMS:
                t.wait("scores_ready", s)
                sc = ps[s][:, 2:4, 0:half * S].rearrange("p a (h k) -> p a h k", h=half)
                mx = maxima[s][:, 0:heads].rearrange("p (a h) -> p a h", a=2)
                nc.vector.reduce_max(mx, sc, X_AXIS).then_inc(signal["max_ready"], 1)
                t.wait("max_ready", s)
                nc.vector.tensor_tensor(probs(s)[:, 0:heads * S].rearrange("p (a h k) -> p a h k", a=2, h=half), sc,
                                        mx.unsqueeze(3).broadcast_to([P, 2, half, S]),
                                        ALU.subtract).then_inc(signal["scores_shifted"], 1)

        def exp_scalar(t, heads, scale):
            n = heads * S
            for s in STREAMS:
                t.wait("scores_shifted", s)
                nc.scalar.activation(probs(s)[:, 0:n], probs(s)[:, 0:n], ACT.Exp, scale=scale)\
                    .then_inc(signal["probs_ready"], 1)

        def probsT_scalar(t, heads):
            n = heads * S
            for s in STREAMS:
                t.wait("probs_turned", s)
                nc.scalar.copy(probsT(s)[:, 0:n], pair(s, 2)[:, 0:n]).then_inc(signal["probsT_ready"], 1)

        def softmax_scalar(t, heads, scale):
            exp_scalar(t, heads, scale)
            probsT_scalar(t, heads)

        def turn_probs_pe(t, heads):
            for s in STREAMS:
                t.wait("probs_ready", s)
                for j in range(heads // 2):
                    last = nc.tensor.transpose(pair(s, 2)[:, j * P:(j + 1) * P], probs(s)[:, j * P:(j + 1) * P], ident)
                last.then_inc(signal["probs_turned"], 1)

        def roped(s):
            return big(s, 0)

        def query8(s):
            return big(s, 1, 256).rearrange("p (h b t) -> p h b t", h=2, b=SEQS)

        def key8(s):
            return big(s, 1)[:, 256:384]

        def keys_wide(s):
            return big(s, 2)

        def probs(s):
            return big(s, 5)

        def probsT(s):
            return big(s, 6)

        VAL = H8 // 2 * 4 * (HD8 + 1)

        def narrow_pool(pool):
            def run(ph):
                if ph in GIVEN_CTX:
                    pool.wait_ge(ctx_loaded, 16)
                pool.wait_ge(tile_done, 2 + 16 * ph)
                for s in STREAMS:
                    nc.gpsimd.memset(big(s, 1, 256), 0.0)

                def body(back, front):
                    if front:
                        for s in STREAMS:
                            if back:
                                back.wait("scores_ready", s)
                            stage_pool(front, s, state, context=ph in GIVEN_CTX)
                        for s in STREAMS:
                            front.wait("qk_ready", s)
                            nc.gpsimd.tensor_tensor(
                                keys_wide(s).rearrange("p (a h t) -> p a h t", a=2, h=8),
                                key8(s).rearrange("p (a t) -> p a t", a=2).unsqueeze(2).broadcast_to([P, 2, 8, S]),
                                part("const", "own_head").unsqueeze(1).unsqueeze(3).broadcast_to([P, 2, 8, S]),
                                ALU.mult).then_inc(signal["keys_spread"], 1)
                    if back:
                        for s in STREAMS:
                            norm_pool(back, s)
                piped(pool, ph, body)
            return run

        def narrow_tensor(pe):
            def run(ph):
                w = PREFIX[ph]
                has_out = ph != L3_CROSS
                pe.wait_ge(loaded[w], 16)
                if ph == L2_ATTN:
                    pe.wait_ge(loaded["alibi"], 16)

                def project(t, s):
                    src = cs[s] if ph in GIVEN_CTX else xT[s]
                    kinds = [("wq", xT[s]), ("wk", src)]
                    if ph in ROPED:
                        kinds += [("wq_swapped", xT[s]), ("wk_swapped", src)]
                    for n, (name, rhs) in enumerate(kinds):
                        for half in range(2):
                            for b in range(SEQS):
                                mm(ps[s][b * S:(b + 1) * S, 0, n * P + half * S:n * P + (half + 1) * S],
                                   part(w, name)[:, half * S:(half + 1) * S], rhs[:, b * S:(b + 1) * S])
                    for par in range(2):
                        for b in range(SEQS):
                            o = ps[s][par * S:(par + 1) * S, 1, b * S:(b + 1) * S]
                            last = mm(o, src[:, b * S:(b + 1) * S], part(w, "wv")[:, par * S:(par + 1) * S],
                                      stop=has_out)
                            if not has_out:
                                last = mm(o, ones_row[:, 0:S], part("rows", "x3_bv")[:, par * S:(par + 1) * S],
                                          start=False)
                    last.then_inc(signal["projected"], 1)

                def score(t, s):
                    opened = ph != L2_CROSS
                    for half in range(2):
                        if ph == L2_ATTN:
                            for n in range(3):
                                mm(bank(s, 2 + half), ident16[:, :], alibi16[:, n, half * 512:(half + 1) * 512],
                                   start=(n == 0), stop=False)
                        elif opened:
                            table = {L1_CROSS: own16, L3_CROSS: pads_tile[s]}.get(ph, causal16)
                            mm(bank(s, 2 + half), ident16[:, :], table[:, :].unsqueeze(1).broadcast_to([P, 8, S]),
                               stop=False)
                        last = mm(bank(s, 2 + half), query8(s)[:, half, :, :].rearrange("p b t -> p (b t)"),
                                  keys_wide(s)[:, half * 512:(half + 1) * 512], start=not opened)
                    last.then_inc(signal["scores_ready"], 1)

                def body(back, front):
                    if back:
                        for s in STREAMS:
                            back.wait("keys_spread", s)
                            score(back, s)
                    if front:
                        for s in STREAMS:
                            if back:
                                back.wait("values_ready", s)
                            front.wait("x_staged", s)
                            nc.tensor.transpose(bank(s, 1, 0, P), xs[s][:, :], ident)\
                                .then_inc(signal["x_turned"], 1)
                    if back:
                        turn_probs_pe(back, H8)
                    if front:
                        for s in STREAMS:
                            front.wait("xT_ready", s)
                            project(front, s)
                    if back:
                        for s in STREAMS:
                            back.wait("probsT_ready", s)
                            back.wait("values_ready", s)
                            for j in range(H8 // 2):
                                last = mm(bank(s, 2, j * 36, (j + 1) * 36), probsT(s)[:, j * P:(j + 1) * P],
                                          values8[s][:, j, :, :, :].rearrange("p b a d -> p (b a d)"))
                            last.then_inc(signal["mixed"], 1)
                        if has_out:
                            for s in STREAMS:
                                back.wait("heads_normal", s)
                                nc.tensor.transpose(bank(s, 3, 0, P), heads_out[s][:, :], ident)\
                                    .then_inc(signal["heads_turned"], 1)
                            for s in STREAMS:
                                back.wait("headsT_ready", s)
                                mm(bank(s, 3, 0, P), outT[s][:, 0, :], part(w, "wo"), stop=False)
                                mm(bank(s, 3, 0, P), ones_row[:, :], part("rows", w + "_bo"), start=False)\
                                    .then_inc(signal["y_ready"], 1)
                        for s in STREAMS:
                            back.wait("res_sum" if has_out else "heads_normal", s)
                piped(pe, ph, body)
            return run

        def narrow_scalar(act):
            def run(ph):
                w = PREFIX[ph]
                has_out = ph != L3_CROSS
                act.wait_ge(loaded[w], 16)
                scale = float(1.0 / np.sqrt(np.float32(HD8)))

                def body(back, front):
                    if back:
                        exp_scalar(back, H8, scale)
                    if front:
                        for s in STREAMS:
                            front.wait("x_turned", s)
                            nc.scalar.copy(xT[s][:, :], bank(s, 1, 0, P)).then_inc(signal["xT_ready"], 1)
                    if back:
                        probsT_scalar(back, H8)
                        if has_out:
                            for s in STREAMS:
                                back.wait("heads_turned", s)
                                if ph == L1_CROSS:
                                    nc.scalar.copy(outT[s][:, 0, :], bank(s, 3, 0, P))\
                                        .then_inc(signal["headsT_ready"], 1)
                                else:
                                    nc.scalar.activation(outT[s][:, 0, :], bank(s, 3, 0, P), ACT.Identity,
                                                         bias=part(w, "bv")[:, 0:1]).then_inc(signal["headsT_ready"], 1)
                    if front:
                        for s in STREAMS:
                            front.wait("projected", s)
                            if back:
                                back.wait("mixed", s)
                            for par in range(2):
                                rows = slice(par * S, (par + 1) * S)
                                for b in range(SEQS):
                                    last = nc.scalar.copy(
                                        values8[s][rows, :, b, par, 0:HD8],
                                        ps[s][rows, 1, b * S:(b + 1) * S].rearrange("p (j d) -> p j d", j=8))
                            last.then_inc(signal["values_ready"], 1)
                piped(act, ph, body)
            return run

        def narrow_vector(dve):
            def run(ph):
                w = PREFIX[ph]
                dve.wait_ge(loaded[w], 16)

                def spread_query(s, make):
                    for b in range(SEQS):
                        make(query8(s)[b * S:(b + 1) * S, :, b, :], slice(b * S, (b + 1) * S))

                def queries_and_keys(t, s):
                    def halves(x):
                        return x.rearrange("p (h t) -> p h t", h=2)
                    t.wait("projected", s)
                    if ph in ROPED:
                        n8 = roped(s)[:, 0:512].rearrange("p (n t) -> p n t", n=8)
                        nc.vector.tensor_tensor(n8, bank(s, 0).rearrange("p (n t) -> p n t", n=8),
                                                part(w, "bias").unsqueeze(2).broadcast_to([P, 8, S]), ALU.add)\
                            .then_inc(signal["rope_biased"], 1)
                        t.wait("rope_biased", s)
                        f4 = roped(s)[:, 0:512].rearrange("p (f n t) -> p f n t", f=2, n=4)
                        table = part("const", "rope8").rearrange("p (f t) -> p f t", f=2)
                        nc.vector.tensor_tensor(f4, f4, table.unsqueeze(2).broadcast_to([P, 2, 4, S]), ALU.mult)\
                            .then_inc(signal["rope_scaled"], 1)
                        t.wait("rope_scaled", s)
                        spread_query(s, lambda o, r: nc.vector.tensor_tensor(
                            o, halves(roped(s)[r, 0:128]), halves(roped(s)[r, 256:384]), ALU.add))
                        nc.vector.tensor_tensor(key8(s), roped(s)[:, 128:256], roped(s)[:, 384:512], ALU.add)\
                            .then_inc(signal["qk_ready"], 1)
                    elif ph == L1_CROSS:
                        spread_query(s, lambda o, r: nc.vector.tensor_copy(o, halves(ps[s][r, 0, 0:128])))
                        nc.vector.tensor_copy(key8(s), bank(s, 0, 128, 256)).then_inc(signal["qk_ready"], 1)
                    else:
                        spread_query(s, lambda o, r: nc.vector.tensor_tensor(
                            o, halves(ps[s][r, 0, 0:128]),
                            part(w, "bias")[r, 0:2].unsqueeze(2).broadcast_to([S, 2, S]), ALU.add))
                        nc.vector.tensor_tensor(halves(key8(s)), halves(bank(s, 0, 128, 256)),
                                                part(w, "bias")[:, 2:4].unsqueeze(2).broadcast_to([P, 2, S]), ALU.add)\
                            .then_inc(signal["qk_ready"], 1)

                dve.wait_ge(tile_done, 2 + 16 * ph)

                def body(back, front):
                    if back:
                        softmax_vector(back, H8)
                    if front:
                        for s in STREAMS:
                            queries_and_keys(front, s)
                    if back:
                        for s in STREAMS:
                            back.wait("mixed", s)
                            for b in range(SEQS):
                                rows = slice(b * S, (b + 1) * S)
                                sums = ps[s][rows, 2, 0:VAL].rearrange("p (j b n d) -> p j b n d", j=8, b=SEQS, n=2)
                                last = nc.vector.reciprocal(inv_sum[s][rows, :].rearrange("p (j n) -> p j n", n=2),
                                                            sums[:, :, b, :, HD8])
                            last.then_inc(signal["sums_inverted"], 1)
                            back.wait("sums_inverted", s)
                            for b in range(SEQS):
                                rows = slice(b * S, (b + 1) * S)
                                mix = ps[s][rows, 2, 0:VAL].rearrange("p (j b n d) -> p j b n d", j=8, b=SEQS, n=2)
                                last = nc.vector.tensor_tensor(
                                    heads_out[s][rows, :].rearrange("p (j n d) -> p j n d", j=8, n=2),
                                    mix[:, :, b, :, 0:HD8],
                                    inv_sum[s][rows, :].rearrange("p (j n) -> p j n", n=2).unsqueeze(3)
                                    .broadcast_to([S, 8, 2, HD8]), ALU.mult)
                            last.then_inc(signal["heads_normal"], 1)
                        if ph == L3_CROSS:
                            finish_vector(back, lambda s: heads_out[s][:, :], state, ready="heads_normal")
                        else:
                            finish_vector(back, lambda s: bank(s, 3, 0, P), state)
                piped(dve, ph, body)
            return run

        def wide_heads(ph):
            return 16 if ph == L1_ATTN else 8

        def wide_pack(ph):
            return {F0_ATTN: "fa0", F1_ATTN: "fa1", L1_ATTN: "a1"}[ph]

        def key_rotated(s):
            return big(s, 1)

        def rope_swapped(s):
            return big(s, 2)

        def queryT(s):
            return big(s, 3)

        def keyT(s):
            return big(s, 4)

        def mixed_heads(s):
            return big(s, 0)

        def values64(s):
            return big(s, 7, VALUES64).rearrange("p (b c a d) -> p b c a d", b=SEQS, c=8, a=2)

        def mix_place(s, c):
            return c // 3, (c % 3) * 130

        def mix_banks(heads):
            pairs = heads // 2
            return [(k, 6 * k, 2 * min(3, pairs - 3 * k)) for k in range((pairs + 2) // 3)]

        def wide_pool(pool):
            def run(ph):
                src = state if ph in (F0_ATTN, L1_ATTN) else inner

                def body(t):
                    for s in STREAMS:
                        stage_pool(t, s, src)
                    if ph != L1_ATTN:
                        for s in STREAMS:
                            t.wait("norms_floor", s)
                            nc.gpsimd.tensor_tensor(inv_norm[s][:, :], sq_floor[s][:, :], minus_half[:, :], ALU.pow)\
                                .then_inc(signal["norms_inv"], 1)
                    for s in STREAMS:
                        t.wait("q_parts", s)
                        nc.gpsimd.tensor_tensor(roped(s), roped(s), rope_swapped(s), ALU.add)\
                            .then_inc(signal["q_rotated"], 1)
                    if ph == L1_ATTN:
                        for s in STREAMS:
                            t.wait("k_parts", s)
                            nc.gpsimd.tensor_tensor(key_rotated(s), key_rotated(s), probs(s), ALU.add)\
                                .then_inc(signal["k_rotated"], 1)
                        for s in STREAMS:
                            norm_pool(t, s)
                turns(pool, ph, body)
            return run

        def wide_tensor(pe):
            def run(ph):
                heads, w = wide_heads(ph), wide_pack(ph)
                half, n = heads // 2, heads * S
                pe.wait_ge(loaded[w], 16)

                def body(t):
                    for s in STREAMS:
                        turn_x_pe(t, s)
                    for s in STREAMS:
                        t.wait("xT_ready", s)
                        if ph == L1_ATTN:
                            mm(ps[s][0:S, 1, 0:P], part(w, "down"), xT[s][:, :]).then_inc(signal["latent_projected"], 1)
                        rows = xT[s] if ph == L1_ATTN else shT[s]
                        wq = part(w, "wqk")
                        for k in range(2):
                            last = mm(bank(s, 2 + k), rows[:, :], wq[:, k * 512:(k + 1) * 512])
                        last.then_inc(signal["q_projected"], 1)
                    if ph == L1_ATTN:
                        for s in STREAMS:
                            t.wait("latent_ready", s)
                            for k in range(2):
                                last = mm(bank(s, k), latentT[s], part(w, "k_up")[0:S, k * 512:(k + 1) * 512])
                            last.then_inc(signal["k_projected"], 1)
                    for s in STREAMS:
                        t.wait("q_rotated", s)
                        for j in range(8):
                            last = nc.tensor.transpose(pair(s, 2)[:, j * P:(j + 1) * P], roped(s)[:, j * P:(j + 1) * P],
                                                       ident)
                        last.then_inc(signal["q_turned"], 1)
                    if ph == L1_ATTN:
                        for s in STREAMS:
                            t.wait("k_rotated", s)
                            for j in range(8):
                                last = nc.tensor.transpose(pair(s, 0)[:, j * P:(j + 1) * P],
                                                           key_rotated(s)[:, j * P:(j + 1) * P], ident)
                            last.then_inc(signal["k_turned"], 1)
                    for s in STREAMS:
                        if ph == L1_ATTN:
                            t.wait("kT_ready", s, alone=True)
                        for par in range(2):
                            for b in range(SEQS):
                                o = pair(s, 0)[par * S:(par + 1) * S, b * half * S:(b + 1) * half * S]
                                wv = part(w, "wv")[:, par * half * S:(par + 1) * half * S]
                                if ph == L1_ATTN:
                                    last = mm(o, latentT[s][:, b * S:(b + 1) * S], wv[0:S, :])
                                else:
                                    last = mm(o, shT[s][:, b * S:(b + 1) * S], wv)
                        last.then_inc(signal["v_projected"], 1)
                    for s in STREAMS:
                        t.wait("qT_ready", s)
                        for k in range(2):
                            mm(bank(s, 2 + k, 0, half * S), ident16[:, :],
                               causal16[:, :].unsqueeze(1).broadcast_to([P, half, S]), stop=False)
                        keys = keyT(s) if ph == L1_ATTN else queryT(s)[:, 512:1024]
                        for par in range(2):
                            rows = slice(par * S, (par + 1) * S)
                            for b in range(SEQS):
                                for j in range(half):
                                    cols = slice(j * P + b * S, j * P + (b + 1) * S)
                                    last = mm(ps[s][b * S:(b + 1) * S, 2 + par, j * S:(j + 1) * S],
                                              queryT(s)[rows, cols], keys[rows, cols], start=False)
                        last.then_inc(signal["scores_ready"], 1)
                    turn_probs_pe(t, heads)
                    for s in STREAMS:
                        t.wait("probsT_ready", s)
                        t.wait("values_ready", s)
                        for c in range(half):
                            bk, col = mix_place(s, c)
                            for b in range(SEQS):
                                last = mm(ps[s][b * S:(b + 1) * S, bk, col:col + 130],
                                          probsT(s)[:, c * P + b * S:c * P + (b + 1) * S],
                                          values64(s)[:, b, c, :, :].rearrange("p a d -> p (a d)"))
                        last.then_inc(signal["mixed"], 1)
                    for s in STREAMS:
                        t.wait("heads_normal", s)
                        for j in range(half):
                            last = nc.tensor.transpose(pair(s, 0)[:, j * P:(j + 1) * P],
                                                       mixed_heads(s)[:, j * P:(j + 1) * P], ident)
                        last.then_inc(signal["heads_turned"], 1)
                    for s in STREAMS:
                        t.wait("headsT_ready", s)
                        for j in range(half):
                            last = mm(bank(s, 2, 0, P), queryT(s)[:, j * P:(j + 1) * P],
                                      part(w, "wo")[:, j * D:(j + 1) * D], start=(j == 0), stop=(j == half - 1))
                        last.then_inc(signal["y_ready"], 1)
                turns(pe, ph, body)
            return run

        def wide_scalar(act):
            def run(ph):
                heads = wide_heads(ph)
                half = heads // 2

                def body(t):
                    for s in STREAMS:
                        turn_x_act(t, s, shifted=ph != L1_ATTN)
                    if ph == L1_ATTN:
                        for s in STREAMS:
                            t.wait("latent_projected", s)
                            nc.scalar.copy(latentT[s], ps[s][0:S, 1, 0:P]).then_inc(signal["latent_ready"], 1)
                    else:
                        for s in STREAMS:
                            t.wait("q_projected", s)
                            nc.scalar.activation(rope_swapped(s), pair(s, 2), ACT.Square)\
                                .then_inc(signal["squares"], 1)
                    for s in STREAMS:
                        t.wait("q_turned", s)
                        nc.scalar.copy(queryT(s), pair(s, 2)).then_inc(signal["qT_ready"], 1)
                    if ph == L1_ATTN:
                        for s in STREAMS:
                            t.wait("k_turned", s)
                            nc.scalar.copy(keyT(s), pair(s, 0)).then_inc(signal["kT_ready"], 1)
                    for s in STREAMS:
                        t.wait("v_projected", s)
                        for par in range(2):
                            rows = slice(par * S, (par + 1) * S)
                            last = nc.scalar.copy(values64(s)[rows, :, 0:half, par, 0:64],
                                                  pair(s, 0)[rows, 0:SEQS * half * S]
                                                  .rearrange("p (b c d) -> p b c d", b=SEQS, c=half))
                        last.then_inc(signal["values_ready"], 1)
                    softmax_scalar(t, heads, 0.125 if ph == L1_ATTN else 8.0)
                    for s in STREAMS:
                        t.wait("heads_turned", s)
                        nc.scalar.copy(queryT(s)[:, 0:half * P], pair(s, 0)[:, 0:half * P])\
                            .then_inc(signal["headsT_ready"], 1)
                turns(act, ph, body)
            return run

        def wide_vector(dve):
            def run(ph):
                heads = wide_heads(ph)
                tables = {F0_ATTN: rope_f[0], F1_ATTN: rope_f[1]}.get(ph)
                tables = part("const", "rope64") if tables is None else tables[:, :]
                tables = tables.rearrange("p (f n d) -> p f n d", f=2, n=2)

                def rotate(x, straight, swapped):
                    def table(f, lo, hi):
                        return tables[:, f, :, lo:hi].unsqueeze(2).broadcast_to([P, 2, 8, hi - lo])
                    nc.vector.tensor_tensor(straight, x, table(0, 0, 64), ALU.mult)
                    nc.vector.tensor_tensor(swapped[:, :, :, 0:32], x[:, :, :, 32:64], table(1, 0, 32), ALU.mult)
                    return nc.vector.tensor_tensor(swapped[:, :, :, 32:64], x[:, :, :, 0:32], table(1, 32, 64), ALU.mult)

                def blocks(x):
                    return x.rearrange("p (n h d) -> p n h d", n=2, h=8)

                def body(t):
                    if ph == L1_ATTN:
                        for s in STREAMS:
                            t.wait("q_projected", s)
                            rotate(blocks(pair(s, 2)), blocks(roped(s)), blocks(rope_swapped(s)))\
                                .then_inc(signal["q_parts"], 1)
                        for s in STREAMS:
                            t.wait("k_projected", s)
                            rotate(blocks(pair(s, 0)), blocks(key_rotated(s)), blocks(probs(s)))\
                                .then_inc(signal["k_parts"], 1)
                    else:
                        for s in STREAMS:
                            t.wait("squares", s)
                            nc.vector.reduce_sum(sq_sum[s][:, :], rope_swapped(s).rearrange("p (h d) -> p h d", h=16),
                                                 X_AXIS).then_inc(signal["norms_sq"], 1)
                        for s in STREAMS:
                            t.wait("norms_sq", s)
                            nc.vector.tensor_scalar(sq_floor[s][:, :], sq_sum[s][:, :], 1e-24, None, ALU.max)\
                                .then_inc(signal["norms_floor"], 1)
                        for s in STREAMS:
                            t.wait("norms_inv", s)
                            nc.vector.tensor_tensor(key_rotated(s).rearrange("p (h d) -> p h d", h=16),
                                                    pair(s, 2).rearrange("p (h d) -> p h d", h=16),
                                                    inv_norm[s][:, :].unsqueeze(2).broadcast_to([P, 16, 64]),
                                                    ALU.mult).then_inc(signal["unit_ready"], 1)
                        for s in STREAMS:
                            t.wait("unit_ready", s)
                            rotate(blocks(key_rotated(s)), blocks(roped(s)), blocks(rope_swapped(s)))\
                                .then_inc(signal["q_parts"], 1)
                    softmax_vector(t, heads)
                    for s in STREAMS:
                        t.wait("mixed", s)
                        for bk, m, k in mix_banks(heads):
                            mix = bank(s, bk, 0, k * 65).rearrange("p (h d) -> p h d", h=k)
                            last = nc.vector.reciprocal(inv_sum[s][:, m:m + k], mix[:, :, 64:65]
                                                        .rearrange("p h d -> p (h d)"))
                        last.then_inc(signal["sums_inverted"], 1)
                        t.wait("sums_inverted", s)
                        for bk, m, k in mix_banks(heads):
                            mix = bank(s, bk, 0, k * 65).rearrange("p (h d) -> p h d", h=k)
                            last = nc.vector.tensor_tensor(
                                mixed_heads(s)[:, m * 64:(m + k) * 64].rearrange("p (h d) -> p h d", h=k),
                                mix[:, :, 0:64], inv_sum[s][:, m:m + k].unsqueeze(2).broadcast_to([P, k, 64]), ALU.mult)
                        last.then_inc(signal["heads_normal"], 1)
                    finish_vector(t, lambda s: bank(s, 2, 0, P), state if ph == L1_ATTN else inner,
                                  src=inner if ph == F1_ATTN else state)
                turns(dve, ph, body)
            return run

        def glu_pack(ph):
            return {F0_GLU: "fg0", F1_GLU: "fg1"}[ph]

        def normal_h(s):
            return heads_out[s]

        def gelu_out(s):
            return big(s, 0, 3 * P)

        def gated_out(s):
            return big(s, 1, 3 * P)

        def glu_pool(pool):
            def run(ph):
                def body(t):
                    for s in STREAMS:
                        stage_pool(t, s, inner)
                    for s in STREAMS:
                        t.wait("h_var", s)
                        nc.gpsimd.tensor_tensor(rstd[s][:, :], var_eps[s][:, :], minus_half[:, 0:1], ALU.pow)\
                            .then_inc(signal["h_rstd"], 1)
                    if ph == F1_GLU:
                        for s in STREAMS:
                            norm_pool(t, s)
                turns(pool, ph, body)
            return run

        def glu_tensor(pe):
            def run(ph):
                w = glu_pack(ph)
                pe.wait_ge(loaded[w], 16)

                def body(t):
                    for s in STREAMS:
                        turn_x_pe(t, s)
                    for s in STREAMS:
                        t.wait("xT_ready", s)
                        nc.tensor.transpose(bank(s, 0, P, 2 * P), shT[s][:, :], ident).then_inc(signal["h_turned"], 1)
                    for s in STREAMS:
                        t.wait("h_normal", s)
                        nc.tensor.transpose(bank(s, 0, 2 * P, 3 * P), normal_h(s)[:, :], ident)\
                            .then_inc(signal["hn_turned"], 1)
                    for s in STREAMS:
                        t.wait("hnT_ready", s)
                        for side in range(2):
                            first = 0 if side else HID
                            for n, k in enumerate(HCH):
                                last = mm(ps[s][0:k, 1 + side, n * P:(n + 1) * P],
                                          part(w, "w1")[:, first + n * P:first + n * P + k], xT[s][:, :])
                        last.then_inc(signal["up_ready"], 1)
                    for s in STREAMS:
                        t.wait("gated_ready", s)
                        for n, k in enumerate(HCH):
                            mm(bank(s, 3, 0, P), gated_out(s)[0:k, n * P:(n + 1) * P],
                               part(w, "w2")[0:k, n * D:(n + 1) * D], start=(n == 0), stop=False)
                        mm(bank(s, 3, 0, P), ones_row[:, :], part("rows", w + "_b2"), start=False)\
                            .then_inc(signal["y_ready"], 1)
                turns(pe, ph, body)
            return run

        def glu_scalar(act):
            def run(ph):
                w = glu_pack(ph)
                act.wait_ge(loaded[w], 16)

                def body(t):
                    for s in STREAMS:
                        turn_x_act(t, s, True)
                    for s in STREAMS:
                        t.wait("hn_turned", s)
                        nc.scalar.activation(xT[s][:, :], bank(s, 0, 2 * P, 3 * P), ACT.Identity,
                                             bias=part(w, "ln")[:, 1:2], scale=part(w, "ln")[:, 0:1])\
                            .then_inc(signal["hnT_ready"], 1)
                    for s in STREAMS:
                        t.wait("up_ready", s)
                        for n, k in enumerate(HCH):
                            last = nc.scalar.activation(gelu_out(s)[0:k, n * P:(n + 1) * P],
                                                        ps[s][0:k, 1, n * P:(n + 1) * P], ACT.Gelu,
                                                        bias=part(w, "b1")[0:k, 3 + n:4 + n])
                        last.then_inc(signal["gelu_ready"], 1)
                turns(act, ph, body)
            return run

        def glu_vector(dve):
            def run(ph):
                w = glu_pack(ph)
                dve.wait_ge(loaded[w], 16)

                def body(t):
                    for s in STREAMS:
                        t.wait("h_turned", s)
                        nc.vector.bn_stats(stats[s][:, :], bank(s, 0, P, 2 * P)).then_inc(signal["h_stats"], 1)
                    for s in STREAMS:
                        t.wait("h_stats", s, alone=True)
                        nc.vector.bn_aggr(moments[s][:, :], stats[s][:, :]).then_inc(signal["h_mean"], 1)
                    for s in STREAMS:
                        t.wait("h_mean", s)
                        nc.vector.tensor_scalar(var_eps[s][:, :], moments[s][:, 1:2], EPS, None, ALU.add)\
                            .then_inc(signal["h_var"], 1)
                    for s in STREAMS:
                        t.wait("h_rstd", s)
                        nc.vector.tensor_scalar(normal_h(s)[:, :], bank(s, 0, P, 2 * P), moments[s][:, 0:1],
                                                rstd[s][:, 0:1], ALU.subtract, ALU.mult)\
                            .then_inc(signal["h_normal"], 1)
                    for s in STREAMS:
                        t.wait("gelu_ready", s)
                        for n, k in enumerate(HCH):
                            last = nc.vector.scalar_tensor_tensor(
                                out=gated_out(s)[0:k, n * P:(n + 1) * P], in0=ps[s][0:k, 2, n * P:(n + 1) * P],
                                scalar=part(w, "b1")[0:k, n:n + 1], in1=gelu_out(s)[0:k, n * P:(n + 1) * P],
                                op0=ALU.add, op1=ALU.mult)
                        last.then_inc(signal["gated_ready"], 1)
                    finish_vector(t, lambda s: bank(s, 3, 0, P), inner if ph == F0_GLU else state, outer=ph == F1_GLU,
                                  src=inner)
                turns(dve, ph, body)
            return run

        def both_qk(s):
            return big(s, 0, 512)

        def both_values(s):
            return big(s, 1, SEQS * D)

        def both_probs(s):
            return big(s, 2, 2 * S)

        def both_probsT(s):
            return big(s, 3, P)

        def both_mixed(s):
            return big(s, 4, 2 * D)

        def cross0_pool(pool):
            def run(ph):
                pool.wait_ge(ctx_loaded, 16)

                def body(t):
                    for s in STREAMS:
                        stage_pool(t, s, state, context=True)
                    for s in STREAMS:
                        norm_pool(t, s)
                turns(pool, ph, body)
            return run

        def cross0_tensor(pe):
            def run(ph):
                pe.wait_ge(loaded["x0"], 16)

                def body(t):
                    for s in STREAMS:
                        turn_x_pe(t, s)
                    for s in STREAMS:
                        t.wait("xT_ready", s)
                        for n, (name, src) in enumerate((("wq_c", xT[s]), ("wk_s", cs[s]), ("wq_s", cs[s]),
                                                         ("wk_c", xT[s]))):
                            mm(bank(s, 1, n * P, (n + 1) * P), part("x0", name), src[:, :])
                        for way, (name, src) in enumerate((("wv_s", cs[s]), ("wv_c", xT[s]))):
                            for b in range(SEQS):
                                o = ps[s][way * S:(way + 1) * S, 0, (1 + b) * P:(2 + b) * P]
                                mm(o, src[:, b * S:(b + 1) * S], part("x0", name), stop=False)
                                last = mm(o, ones_row[:, 0:S], part("rows", "x0_b" + name[1:]), start=False)
                        last.then_inc(signal["projected"], 1)
                    for s in STREAMS:
                        t.wait("qk_ready", s)
                        for way in range(2):
                            for b in range(SEQS):
                                q, k = (both_qk(s)[:, (2 * way + n) * P + b * S:(2 * way + n) * P + (b + 1) * S]
                                        for n in range(2))
                                last = mm(ps[s][b * S:(b + 1) * S, 2, way * S:(way + 1) * S], q, k)
                        last.then_inc(signal["scores_ready"], 1)
                    for s in STREAMS:
                        t.wait("probs_ready", s)
                        nc.tensor.transpose(bank(s, 3, 0, P), both_probs(s), ident).then_inc(signal["probs_turned"], 1)
                    for s in STREAMS:
                        t.wait("probsT_ready", s, alone=True)
                        t.wait("values_ready", s, alone=True)
                        for way in range(2):
                            rows = slice(way * S, (way + 1) * S)
                            for b in range(SEQS):
                                last = mm(ps[s][b * S:(b + 1) * S, 1 + way, 0:D],
                                          both_probsT(s)[rows, b * S:(b + 1) * S],
                                          both_values(s)[rows, b * D:(b + 1) * D])
                        last.then_inc(signal["mixed"], 1)
                    for s in STREAMS:
                        t.wait("heads_normal", s)
                        for way in range(2):
                            last = nc.tensor.transpose(bank(s, 3, (1 + way) * P, (2 + way) * P),
                                                       both_mixed(s)[:, way * D:(way + 1) * D], ident)
                        last.then_inc(signal["heads_turned"], 1)
                    for s in STREAMS:
                        t.wait("headsT_ready", s)
                        for way in range(2):
                            mm(bank(s, 0, 0, P), outT[s][:, way, :], part("x0", f"wg{way}"), start=(way == 0),
                               stop=False)
                        mm(bank(s, 0, 0, P), ones_row[:, :], part("rows", "x0_bg"), start=False)\
                            .then_inc(signal["y_ready"], 1)
                turns(pe, ph, body)
            return run

        def cross0_scalar(act):
            def run(ph):
                def body(t):
                    for s in STREAMS:
                        turn_x_act(t, s, False)
                    for s in STREAMS:
                        t.wait("projected", s)
                        nc.scalar.copy(both_values(s), bank(s, 0, P, 3 * P)).then_inc(signal["values_ready"], 1)
                    for s in STREAMS:
                        t.wait("scores_shifted", s)
                        nc.scalar.activation(both_probs(s), both_probs(s), ACT.Exp, scale=float(D) ** -0.5)\
                            .then_inc(signal["probs_ready"], 1)
                    for s in STREAMS:
                        t.wait("probs_turned", s)
                        nc.scalar.copy(both_probsT(s), bank(s, 3, 0, P)).then_inc(signal["probsT_ready"], 1)
                    for s in STREAMS:
                        t.wait("heads_turned", s)
                        nc.scalar.copy(outT[s][:, :, :].rearrange("p w t -> p (w t)"), bank(s, 3, P, 3 * P))\
                            .then_inc(signal["headsT_ready"], 1)
                    for s in STREAMS:
                        t.wait("y_ready", s)
                        nc.scalar.activation(gate[s][:, :], bank(s, 0, 0, P), ACT.Exp, scale=-1.0)\
                            .then_inc(signal["gate_exp"], 1)
                turns(act, ph, body)
            return run

        def cross0_vector(dve):
            def run(ph):
                dve.wait_ge(loaded["x0"], 16)

                def body(t):
                    for s in STREAMS:
                        t.wait("projected", s)
                        nc.vector.tensor_tensor(both_qk(s).rearrange("p (n t) -> p n t", n=4),
                                                bank(s, 1).rearrange("p (n t) -> p n t", n=4),
                                                part("x0", "bias").unsqueeze(2).broadcast_to([P, 4, P]), ALU.add)\
                            .then_inc(signal["qk_ready"], 1)
                    for s in STREAMS:
                        t.wait("scores_ready", s)
                        sc = bank(s, 2, 0, 2 * S).rearrange("p (w k) -> p w k", w=2)
                        nc.vector.reduce_max(maxima[s][:, 0:2], sc, X_AXIS).then_inc(signal["max_ready"], 1)
                        t.wait("max_ready", s)
                        nc.vector.tensor_tensor(both_probs(s).rearrange("p (w k) -> p w k", w=2), sc,
                                                maxima[s][:, 0:2].unsqueeze(2).broadcast_to([P, 2, S]),
                                                ALU.subtract).then_inc(signal["scores_shifted"], 1)
                    for s in STREAMS:
                        t.wait("probs_ready", s)
                        nc.vector.reduce_sum(sq_sum[s][:, 0:2], both_probs(s).rearrange("p (w k) -> p w k", w=2),
                                             X_AXIS).then_inc(signal["sums_ready"], 1)
                    for s in STREAMS:
                        t.wait("sums_ready", s)
                        nc.vector.reciprocal(inv_sum[s][:, 0:2], sq_sum[s][:, 0:2]).then_inc(signal["sums_inverted"], 1)
                    for s in STREAMS:
                        t.wait("mixed", s)
                        t.wait("sums_inverted", s)
                        nc.vector.tensor_tensor(both_mixed(s).rearrange("p (w d) -> p w d", w=2), ps[s][:, 1:3, 0:D],
                                                inv_sum[s][:, 0:2].unsqueeze(2).broadcast_to([P, 2, D]), ALU.mult)\
                            .then_inc(signal["heads_normal"], 1)
                    for s in STREAMS:
                        t.wait("heads_normal", s)
                        nc.vector.tensor_tensor(heads_out[s][:, :], both_mixed(s)[:, 0:D], both_mixed(s)[:, D:2 * D],
                                                ALU.subtract).then_inc(signal["paths_diff"], 1)
                    for s in STREAMS:
                        t.wait("gate_exp", s)
                        nc.vector.tensor_scalar(gate[s][:, :], gate[s][:, :], 1.0, None, ALU.add)\
                            .then_inc(signal["gate_den"], 1)
                    for s in STREAMS:
                        t.wait("gate_den", s)
                        nc.vector.reciprocal(gate[s][:, :], gate[s][:, :]).then_inc(signal["gate_ready"], 1)
                    for s in STREAMS:
                        t.wait("gate_ready", s)
                        t.wait("paths_diff", s)
                        nc.vector.tensor_tensor(heads_out[s][:, :], heads_out[s][:, :], gate[s][:, :], ALU.mult)\
                            .then_inc(signal["diff_gated"], 1)
                    for s in STREAMS:
                        t.wait("diff_gated", s)
                        nc.vector.tensor_tensor(heads_out[s][:, :], heads_out[s][:, :], both_mixed(s)[:, D:2 * D],
                                                ALU.add).then_inc(signal["y_mixed"], 1)
                    finish_vector(t, lambda s: heads_out[s][:, :], state, ready="y_mixed")
                turns(dve, ph, body)
            return run

        def carver():
            used = [0]

            def carve(cols, rows=P, dt=F32):
                words = cols if dt == F32 else -(-cols // (2 if dt == BF16 else 4))
                used[0] += words
                assert used[0] <= 2 * SCRATCH
                view = arena[0:rows, used[0] - words:used[0]]
                return view if dt == F32 else view.bitcast(dt)
            return carve

        def group_of(x, g):
            return x[:, ds(g * 4, 4), :].rearrange("p a n -> p (a n)")

        carve = carver()
        g_x, g_xT, g_acc = carve(GT), carve(GT), carve(GT)
        g_hidden = [carve(GT) for _ in range(2 * FCH)]
        g_onehotT = carve(GT, rows=EXP)
        g_eq, g_onehot = carve(4 * EXP), carve(4 * EXP)
        g_max, g_first = carve(4), carve(4)
        g_stats, g_moments, g_var, g_rstd = carve(24), carve(8), carve(4), carve(4)
        gs = moe_sems

        def group_stage_pool(pool, ph, use, g):
            pool.wait_ge(tile_done, 2 + 16 * ph + g * 4)
            nc.gpsimd.tensor_copy(g_x, group_of(state, g)).then_inc(gs["g_staged"], 1)

        def group_norm_pool(pool, use, g):
            pool.wait_ge(gs["g_var"], 4 * use + 1 + g)
            nc.gpsimd.tensor_tensor(g_rstd, g_var, minus_half[:, 0:4], ALU.pow).then_inc(gs["g_rstd"], 1)

        def group_norm_vector(dve, use, g):
            for tt in range(4):
                last = nc.vector.bn_stats(g_stats[:, 6 * tt:6 * tt + 6], g_acc[:, tt * D:(tt + 1) * D])
            last.then_inc(gs["g_stats"], 1)
            dve.wait_ge(gs["g_stats"], 4 * use + 1 + g)
            dve.nop(nofuse=True)
            for tt in range(4):
                last = nc.vector.bn_aggr(g_moments[:, 2 * tt:2 * tt + 2], g_stats[:, 6 * tt:6 * tt + 6])
            last.then_inc(gs["g_mean"], 1)
            dve.wait_ge(gs["g_mean"], 4 * use + 1 + g)
            nc.vector.tensor_scalar(g_var, g_moments.rearrange("p (t m) -> p t m", m=2)[:, :, 1:2]
                                    .rearrange("p t m -> p (t m)"), EPS, None, ALU.add).then_inc(gs["g_var"], 1)
            dve.wait_ge(gs["g_rstd"], 4 * use + 1 + g)
            for tt in range(4):
                nc.vector.tensor_scalar(state[:, ds(g * 4 + tt, 1), :].rearrange("p a n -> p (a n)"),
                                        g_acc[:, tt * D:(tt + 1) * D], g_moments[:, 2 * tt:2 * tt + 1],
                                        g_rstd[:, tt:tt + 1], ALU.subtract, ALU.mult).then_inc(tile_done, 1)

        def group_turn_tensor(pe, use, g, pack, bias):
            pe.wait_ge(gs["g_staged"], 4 * use + 1 + g)
            for tt in range(4):
                last = nc.tensor.transpose(bank(1, 2, tt * P, (tt + 1) * P), g_x[:, tt * D:(tt + 1) * D], ident)
            last.then_inc(gs["g_turned"], 1)
            pe.wait_ge(gs["g_xT"], 4 * use + 1 + g)
            for tt in range(4):
                o = bank(1, 3, tt * EXP, (tt + 1) * EXP)
                mm(o, g_xT[:, tt * P:(tt + 1) * P], part(pack, "wr"), stop=False)
                last = mm(o, ones_row[:, :], part("rows", bias), start=False)
            last.then_inc(gs["g_logits"], 1)

        def group_turn_scalar(act, use, g):
            act.wait_ge(gs["g_turned"], 4 * use + 1 + g)
            nc.scalar.copy(g_xT, bank(1, 2)).then_inc(gs["g_xT"], 1)

        def moe1_pool(ph):
            with pool_engine.Fori(0, GROUPS) as g:
                group_stage_pool(pool_engine, ph, 0, g)
                group_norm_pool(pool_engine, 0, g)

        def moe1_tensor(ph):
            pe = tensor_engine
            pe.wait_ge(loaded["moe1"], 16)

            def up(g, e):
                for f in range(FCH):
                    if e:
                        pe.wait_ge(gs["relu_done"], g * 32 + 4 * (e - 1) + f + 1)
                    mm(bank(0, f), part("moe1", "w1")[:, (e * FCH + f) * P:(e * FCH + f + 1) * P], g_xT)\
                        .then_inc(gs["h_done"], 1)

            def down(g, e):
                pe.wait_ge(gs["relu_done"], g * 32 + 4 * e + 4)
                if e >= 2:
                    pe.wait_ge(gs["acc_done"], g * 8 + e - 1)
                for tt in range(4):
                    for f in range(FCH):
                        last = mm(bank(1, e % 2, tt * D, (tt + 1) * D),
                                  g_hidden[(e % 2) * FCH + f][:, tt * P:(tt + 1) * P],
                                  part("moe1", "w2")[:, (e * FCH + f) * D:(e * FCH + f + 1) * D],
                                  start=(f == 0), stop=(f == FCH - 1))
                last.then_inc(gs["ye_done"], 1)

            with pe.Fori(0, GROUPS) as g:
                group_turn_tensor(pe, 0, g, "moe1", "m1_br")
                pe.wait_ge(gs["g_onehot"], 1 + g)
                for tt in range(4):
                    last = nc.tensor.transpose(ps[1][0:EXP, 3, tt * P:(tt + 1) * P],
                                               g_onehot[:, tt * EXP:(tt + 1) * EXP], ident)
                last.then_inc(gs["g_oneturned"], 1)
                up(g, 0)
                pe.wait_ge(gs["g_onehotT"], 1 + g)
                for tt in range(4):
                    last = mm(bank(1, 3, tt * D, (tt + 1) * D), g_onehotT[:, tt * P:(tt + 1) * P],
                              part("moe1", "b2")[0:EXP, :])
                last.then_inc(gs["g_bias"], 1)
                for e in range(EXP):
                    if e + 1 < EXP:
                        up(g, e + 1)
                    down(g, e)

        def moe1_scalar(ph):
            act = scalar_engine
            act.wait_ge(loaded["moe1"], 16)
            with act.Fori(0, GROUPS) as g:
                group_turn_scalar(act, 0, g)
                act.wait_ge(gs["g_oneturned"], 1 + g)
                nc.scalar.copy(g_onehotT, ps[1][0:EXP, 3, :]).then_inc(gs["g_onehotT"], 1)
                for e in range(EXP):
                    if e >= 2:
                        act.wait_ge(gs["ye_done"], g * 8 + e - 1)
                    for f in range(FCH):
                        act.wait_ge(gs["h_done"], g * 32 + 4 * e + f + 1)
                        nc.scalar.activation(g_hidden[(e % 2) * FCH + f], bank(0, f), ACT.Relu,
                                             bias=part("moe1", "b1")[:, e * FCH + f:e * FCH + f + 1])\
                            .then_inc(gs["relu_done"], 1)

        def moe1_vector(ph):
            dve = vector_engine

            def four(x):
                return x.rearrange("p (t e) -> p t e", t=4)

            def wide4(x):
                return x.unsqueeze(2).broadcast_to([P, 4, EXP])

            with dve.Fori(0, GROUPS) as g:
                dve.wait_ge(gs["g_logits"], 1 + g)
                logits = four(bank(1, 3, 0, 4 * EXP))
                nc.vector.reduce_max(g_max, logits, X_AXIS).then_inc(gs["g_top"], 1)
                dve.wait_ge(gs["g_top"], 1 + g)
                nc.vector.tensor_tensor(four(g_eq), logits, wide4(g_max), ALU.is_equal).then_inc(gs["g_eq"], 1)
                dve.wait_ge(gs["g_eq"], 1 + g)
                nc.vector.tensor_tensor(four(g_eq), four(g_eq), part("const", "falling").unsqueeze(1)
                                        .broadcast_to([P, 4, EXP]), ALU.mult).then_inc(gs["g_rank"], 1)
                dve.wait_ge(gs["g_rank"], 1 + g)
                nc.vector.reduce_max(g_first, four(g_eq), X_AXIS).then_inc(gs["g_first"], 1)
                dve.wait_ge(gs["g_first"], 1 + g)
                nc.vector.tensor_tensor(four(g_onehot), four(g_eq), wide4(g_first), ALU.is_equal)\
                    .then_inc(gs["g_onehot"], 1)
                dve.wait_ge(gs["g_bias"], 1 + g)
                nc.vector.tensor_tensor(g_acc, g_x, bank(1, 3), ALU.add).then_inc(gs["g_sum"], 1)
                dve.wait_ge(gs["g_sum"], 1 + g)
                for e in range(EXP):
                    dve.wait_ge(gs["ye_done"], g * 8 + e + 1)
                    if e:
                        dve.wait_ge(gs["acc_done"], g * 8 + e)
                    for tt in range(4):
                        cols = slice(tt * D, (tt + 1) * D)
                        last = nc.vector.scalar_tensor_tensor(
                            out=g_acc[:, cols], in0=bank(1, e % 2)[:, cols],
                            scalar=g_onehot[:, tt * EXP + e:tt * EXP + e + 1], in1=g_acc[:, cols],
                            op0=ALU.mult, op1=ALU.add)
                    last.then_inc(gs["acc_done"], 1)
                dve.wait_ge(gs["acc_done"], g * 8 + EXP)
                group_norm_vector(dve, 0, g)

        carve = carver()
        carve(2 * GT)
        NT8 = TILES * EXP
        logits_all, probs_all, rank_all, onehot_all, weighted_all, count_all = (carve(NT8) for _ in range(6))
        top_all, sum_all, inv_all, best_all, first_all, slot_all = (carve(TILES) for _ in range(6))
        onehot16, upto16, ones16 = carve(NT8, dt=BF16), carve(P, dt=BF16), carve(P, dt=BF16)
        zero512 = carve(512)
        at_slot = [carve(CAP) for _ in STREAMS]
        dispatch = [carve(EXP * CAP) for _ in STREAMS]
        dispatchT = [carve(EXP * P, rows=CAP) for _ in STREAMS]
        slotsT = carve(EXP * CAP)
        hidden80 = [carve(FCH * CAP) for _ in range(2)]
        expert_out = carve(EXP * D, rows=CAP)
        cm = gate_sems

        def moe2_pool(ph):
            pool = pool_engine
            for g in range(GROUPS):
                if g:
                    pool.wait_ge(cm["c_logits"], g)
                group_stage_pool(pool, ph, 1, 0) if g == 0 else \
                    nc.gpsimd.tensor_copy(g_x, state[:, 4 * g:4 * g + 4, :].rearrange("p a n -> p (a n)"))\
                    .then_inc(gs["g_staged"], 1)
            with pool.Fori(0, TURNS) as turn:
                for s in STREAMS:
                    pool.wait_ge(cm["c_dispatched"], turn * 2 + s + 1)
                    nc.gpsimd.tensor_copy(xs[s][:, :], state[:, ds(turn * 2 + s, 1), :].rearrange("p a n -> p (a n)"))\
                        .then_inc(cm["c_staged"], 1)
            pool.wait_ge(cm["c_dispatched"], 2 + TILES)

            def body(t):
                for s in STREAMS:
                    stage_pool(t, s, state)
                for s in STREAMS:
                    norm_pool(t, s)
            turns(pool, ph, body)

        def moe2_tensor(ph):
            pe = tensor_engine
            pe.wait_ge(loaded["moe2"], 16)
            pe.wait_ge(loaded["m2rows"], 16)
            for g in range(GROUPS):
                if g:
                    pe.wait_ge(cm["c_logits"], g)
                group_turn_tensor(pe, 1, g, "moe2", "m2_bg")
            pe.wait_ge(cm["c_onehot"], 1)
            count = bank(0, 2, 0, NT8)
            mm(count, upto16, onehot16, stop=False)
            for t in range(TILES - 1):
                last = mm(count[:, (t + 1) * EXP:], ones16, onehot16[:, t * EXP:(t + 1) * EXP].unsqueeze(1)
                          .broadcast_to([P, TILES - 1 - t, EXP]), start=False)
            last.then_inc(cm["c_counts"], 1)
            for half in range(2):
                last = mm(bank(0, half, 0, 320), zero512[:, 0:P], zero512[:, 0:320], stop=False)
            last.then_inc(cm["c_dispatched"], 2)
            with pe.Fori(0, TURNS) as turn:
                for s in STREAMS:
                    pe.wait_ge(cm["c_staged"], turn * 2 + s + 1)
                    pe.wait_ge(cm["c_made"], turn * 2 + s + 1)
                    for half in range(2):
                        last = mm(bank(0, half, 0, 320), xs[s][:, :], dispatch[s][:, half * 320:(half + 1) * 320],
                                  start=False)
                    last.then_inc(cm["c_dispatched"], 1)

            def up(e):
                if e >= 2:
                    pe.wait_ge(cm["c_gelu"], e - 1)
                for f in range(FCH):
                    last = mm(bank(0, 2 + e % 2, f * CAP, (f + 1) * CAP),
                              part("moe2", "w1")[:, (e * FCH + f) * P:(e * FCH + f + 1) * P],
                              slotsT[:, e * CAP:(e + 1) * CAP])
                last.then_inc(cm["c_up"], 1)

            pe.wait_ge(cm["c_slotsT"], 1)
            up(0)
            for e in range(EXP):
                if e + 1 < EXP:
                    up(e + 1)
                pe.wait_ge(cm["c_gelu"], e + 1)
                o = ps[1][0:CAP, e // 4, (e % 4) * D:(e % 4 + 1) * D]
                for f in range(FCH):
                    mm(o, hidden80[e % 2][:, f * CAP:(f + 1) * CAP],
                       part("moe2", "w2")[:, (e * FCH + f) * D:(e * FCH + f + 1) * D], start=(f == 0), stop=False)
                mm(o, ones_row[:, 0:CAP], part("m2rows", "b2")[:, e * D:(e + 1) * D], start=False)\
                    .then_inc(cm["c_down"], 1)
            pe.wait_ge(cm["c_out"], 1)

            def body(t):
                for s in STREAMS:
                    t.wait("dispatched_made", s)
                    for e in range(EXP):
                        last = nc.tensor.transpose(pair(s, 2)[0:CAP, e * P:(e + 1) * P],
                                                   dispatch[s][:, e * CAP:(e + 1) * CAP], ident)
                    last.then_inc(signal["dispatch_turned"], 1)
                for s in STREAMS:
                    t.wait("dispatchT_ready", s)
                    for e in range(EXP):
                        last = mm(bank(s, 0, 0, D), dispatchT[s][:, e * P:(e + 1) * P],
                                  expert_out[:, e * D:(e + 1) * D], start=(e == 0), stop=(e == EXP - 1))
                    last.then_inc(signal["y_ready"], 1)
            turns(pe, ph, body)

        def moe2_scalar(ph):
            act = scalar_engine
            act.wait_ge(loaded["moe2"], 16)
            for g in range(GROUPS):
                group_turn_scalar(act, 1, g)
            act.wait_ge(cm["c_shifted"], 1)
            nc.scalar.activation(probs_all, probs_all, ACT.Exp).then_inc(cm["c_exp"], 1)
            act.wait_ge(cm["c_dispatched"], 2 + TILES)
            nc.scalar.copy(slotsT.rearrange("p (a n) -> p a n", a=2), ps[0][:, 0:2, 0:320]).then_inc(cm["c_slotsT"], 1)
            for e in range(EXP):
                act.wait_ge(cm["c_up"], e + 1)
                if e >= 2:
                    act.wait_ge(cm["c_down"], e - 1)
                for f in range(FCH):
                    last = nc.scalar.activation(hidden80[e % 2][:, f * CAP:(f + 1) * CAP],
                                                bank(0, 2 + e % 2, f * CAP, (f + 1) * CAP), ACT.Gelu_apprx_tanh,
                                                bias=part("moe2", "b1")[:, e * FCH + f:e * FCH + f + 1])
                last.then_inc(cm["c_gelu"], 1)
            act.wait_ge(cm["c_down"], EXP)
            nc.scalar.copy(expert_out, pair(1, 0)[0:CAP, :]).then_inc(cm["c_out"], 1)

            def body(t):
                for s in STREAMS:
                    t.wait("dispatch_turned", s)
                    nc.scalar.copy(dispatchT[s], pair(s, 2)[0:CAP, :]).then_inc(signal["dispatchT_ready"], 1)
            turns(act, ph, body)

        def moe2_vector(ph):
            dve = vector_engine
            steps = [0]

            def then(ins):
                steps[0] += 1
                ins.then_inc(cm["c_chain"], 1)
                dve.wait_ge(cm["c_chain"], steps[0])

            def tiled(x):
                return x.rearrange("p (t e) -> p t e", t=TILES)

            def spread(x):
                return x.unsqueeze(2).broadcast_to([P, TILES, EXP])

            def make_dispatch(tile, s, count, chosen):
                nc.vector.tensor_tensor(at_slot[s], part("const", "slot"),
                                        slot_all[:, ds(tile, 1)].broadcast_to([P, CAP]), ALU.is_equal)\
                    .then_inc(cm["c_slot"], 1)
                dve.wait_ge(cm["c_slot"], count)
                return nc.vector.tensor_tensor(
                    dispatch[s].rearrange("p (e c) -> p e c", e=EXP),
                    chosen[:, ds(tile * EXP, EXP)].unsqueeze(2).broadcast_to([P, EXP, CAP]),
                    at_slot[s].unsqueeze(1).broadcast_to([P, EXP, CAP]), ALU.mult)

            for g in range(GROUPS):
                dve.wait_ge(gs["g_logits"], 4 + g + 1)
                nc.vector.tensor_copy(logits_all[:, g * 4 * EXP:(g + 1) * 4 * EXP], bank(1, 3, 0, 4 * EXP))\
                    .then_inc(cm["c_logits"], 1)
            dve.wait_ge(cm["c_logits"], GROUPS)
            nc.vector.memset(zero512, 0.0)
            nc.vector.memset(ones16, 1.0)
            nc.vector.tensor_copy(upto16, part("const", "upto"))
            then(nc.vector.reduce_max(top_all, tiled(logits_all), X_AXIS))
            nc.vector.tensor_tensor(tiled(probs_all), tiled(logits_all), spread(top_all), ALU.subtract)\
                .then_inc(cm["c_shifted"], 1)
            dve.wait_ge(cm["c_exp"], 1)
            then(nc.vector.reduce_sum(sum_all, tiled(probs_all), X_AXIS))
            then(nc.vector.reciprocal(inv_all, sum_all))
            then(nc.vector.tensor_tensor(tiled(probs_all), tiled(probs_all), spread(inv_all), ALU.mult))
            then(nc.vector.reduce_max(best_all, tiled(probs_all), X_AXIS))
            then(nc.vector.tensor_tensor(tiled(rank_all), tiled(probs_all), spread(best_all), ALU.is_equal))
            then(nc.vector.tensor_tensor(tiled(rank_all), tiled(rank_all), part("const", "falling").unsqueeze(1)
                                         .broadcast_to([P, TILES, EXP]), ALU.mult))
            then(nc.vector.reduce_max(first_all, tiled(rank_all), X_AXIS))
            then(nc.vector.tensor_tensor(tiled(onehot_all), tiled(rank_all), spread(first_all), ALU.is_equal))
            nc.vector.tensor_copy(onehot16, onehot_all).then_inc(cm["c_onehot"], 1)
            nc.vector.tensor_tensor(tiled(weighted_all), tiled(onehot_all), spread(best_all), ALU.mult)
            dve.wait_ge(cm["c_counts"], 1)
            then(nc.vector.tensor_tensor(count_all, bank(0, 2, 0, NT8), onehot_all, ALU.mult))
            then(nc.vector.reduce_sum(slot_all, tiled(count_all), X_AXIS))
            then(nc.vector.tensor_scalar(slot_all, slot_all, -1.0, None, ALU.add))
            with dve.Fori(0, TURNS) as turn:
                for s in STREAMS:
                    dve.wait_ge(cm["c_dispatched"], turn * 2 + s + 1)
                    make_dispatch(turn * 2 + s, s, turn * 2 + s + 1, onehot_all).then_inc(cm["c_made"], 1)
            dve.wait_ge(cm["c_dispatched"], 2 + TILES)

            def body(t):
                for s in STREAMS:
                    t.wait("x_staged", s)
                    make_dispatch(t.tile(s), s, t.v + TILES + s + 1, weighted_all)\
                        .then_inc(signal["dispatched_made"], 1)
                finish_vector(t, lambda s: bank(s, 0, 0, D), state)
            turns(dve, ph, body)

        carve = carver()
        carve(3 * GT)
        q_in, q_abs, q_bad = carve(GT), carve(GT), carve(GT)
        q_small8, q_large8 = carve(GT, dt=FP8), carve(GT, dt=FP8)
        q_large = carve(GT)
        q_mask = carve(GT, dt=U8)
        q_x = carve(GT, dt=BF16)
        q_xT = carve(GT, dt=BF16)
        x16, y16, sum16 = carve(GT, dt=BF16), carve(GT, dt=BF16), carve(GT, dt=BF16)
        f_stats_end = carve(GT * 8)
        q_w = carve(P, dt=BF16)
        w16 = carve(D, dt=BF16)
        bias8 = carve(D, dt=BF16)
        scale8, inv8, scale_both = carve(2), carve(2), carve(1)
        fs = fp_sems

        def fp8_pool(ph):
            with pool_engine.Fori(0, GROUPS) as g:
                group_stage_pool(pool_engine, ph, 2, g)
                group_norm_pool(pool_engine, 1, g)

        def fp8_tensor(ph):
            pe = tensor_engine
            turned = ps[0][:, 0, :].bitcast(BF16)
            with pe.Fori(0, GROUPS) as g:
                pe.wait_ge(fs["f_rounded"], g + 1)
                for tt in range(4):
                    last = nc.tensor.transpose(turned[:, tt * P:(tt + 1) * P], q_x[:, tt * P:(tt + 1) * P],
                                               ident16[:, :])
                last.then_inc(fs["f_turned"], 1)
                pe.wait_ge(fs["f_turned_copy"], g + 1)
                for tt in range(4):
                    last = mm(bank(0, 1, tt * D, (tt + 1) * D), q_xT[:, tt * P:(tt + 1) * P], q_w)
                last.then_inc(fs["f_y"], 1)

        def fp8_scalar(ph):
            act = scalar_engine
            with act.Fori(0, GROUPS) as g:
                act.wait_ge(fs["f_turned"], g + 1)
                nc.scalar.copy(q_xT, ps[0][:, 0, :].bitcast(BF16)[:, 0:GT]).then_inc(fs["f_turned_copy"], 1)

        def fp8_vector(ph):
            dve = vector_engine
            per_group = 13

            def rounded(n, src, scale, dst, then):
                small8, large8, large, mask = q_small8[:, 0:n], q_large8[:, 0:n], q_large[:, 0:n], q_mask[:, 0:n]
                x, size, bad = q_in[:, 0:n], q_abs[:, 0:n], q_bad[:, 0:n]
                then(nc.vector.tensor_scalar(x, src, scale, None, ALU.mult), alone=True)
                nc.vector.tensor_scalar(large8, x, 0.5, None, ALU.mult, saturate=False)
                nc.vector.tensor_tensor(size, x, x, ALU.mult)
                then(nc.vector.tensor_scalar(small8, x, 192.0, -192.0, ALU.min, ALU.max, saturate=False),
                     alone=True)
                nc.vector.tensor_copy(dst, small8)
                nc.vector.tensor_scalar(mask, size, 128.0 ** 2, None, ALU.is_ge)
                then(nc.vector.tensor_scalar(large, large8, 2.0, None, ALU.mult))
                then(nc.vector.tensor_tensor(size, large, large, ALU.mult))
                then(nc.vector.tensor_scalar(bad, size, 480.0 ** 2, 3e38, ALU.is_ge, ALU.mult))
                then(nc.vector.tensor_scalar(bad, bad, 10.0, None, ALU.mult))
                then(nc.vector.tensor_tensor(size, bad, bad, ALU.subtract))
                then(nc.vector.tensor_tensor(large, large, size, ALU.add), alone=True)
                then(nc.vector.copy_predicated(dst, mask, large))

            steps = [0]

            def once(ins, alone=False):
                steps[0] += 1
                ins.then_inc(fs["f_once"], 1)
                dve.wait_ge(fs["f_once"], steps[0])

            dve.wait_ge(loaded8, 3 * 16)
            once(nc.vector.tensor_tensor(scale_both, scale8[:, 0:1], scale8[:, 1:2], ALU.mult))
            once(nc.vector.reciprocal(inv8, scale8))
            rounded(P, w16, inv8[:, 1:2], q_w, once)
            with dve.Fori(0, GROUPS) as g:
                steps_in = [0]

                def then(ins, alone=False):
                    steps_in[0] += 1
                    ins.then_inc(fs["f_chain"], 1)
                    dve.wait_ge(fs["f_chain"], g * per_group + steps_in[0])
                    if alone:
                        dve.nop(nofuse=True)

                dve.wait_ge(gs["g_staged"], 4 + 4 + 1 + g)
                then(nc.vector.tensor_copy(x16, g_x))
                rounded(GT, x16, inv8[:, 0:1], q_x, then)
                nc.vector.nop().then_inc(fs["f_rounded"], 1)
                dve.wait_ge(fs["f_y"], g + 1)
                then(nc.vector.tensor_scalar(y16, bank(0, 1), scale_both[:, 0:1], None, ALU.mult))
                then(nc.vector.tensor_tensor(sum16.rearrange("p (t d) -> p t d", t=4),
                                             y16.rearrange("p (t d) -> p t d", t=4),
                                             bias8.unsqueeze(1).broadcast_to([P, 4, D]), ALU.add))
                then(nc.vector.tensor_tensor(g_acc, g_x, sum16, ALU.add))
                assert steps_in[0] == per_group
                group_norm_vector(dve, 1, g)

        pool_engine, tensor_engine, scalar_engine, vector_engine = nc.gpsimd, nc.tensor, nc.scalar, nc.vector
        block = ctx.enter_context(nc.Block())

        @block.sync
        def _(sp):
            sp.dma_start(weights["const"][:, :], packs["const"][0]).then_inc(loaded["const"], 16)
            sp.dma_start(weights["a0"][:, :], packs["a0"][0]).then_inc(loaded["a0"], 16)
            sp.dma_start(state[:, :, :], dram["x"].rearrange("(t p) d -> p t d", p=P)).then_inc(x_loaded, 16)
            sp.dma_start(weights["rows"][:, :], packs["rows"][0]).then_inc(loaded["rows"], 16)
            sp.dma_start(weights["scales"][:, :], packs["scales"][0][0].partition_broadcast(P))\
                .then_inc(loaded["scales"], 16)
            sp.dma_start(own_u8[:, :], dram["own"].unsqueeze(0).broadcast_to([SEQS, S, S])).then_inc(masks_loaded, 16)
            sp.dma_start(mask_int[:, :], dram["seq"].unsqueeze(0).broadcast_to([SEQS, S, S])).then_inc(masks_loaded, 16)
            for b in range(SEQS):
                sp.dma_start(pads_int[b * S:(b + 1) * S, :, :], dram["pads"][:, b, :].partition_broadcast(S))\
                    .then_inc(masks_loaded, 16)
            sp.dma_start(ctxT[:, :, :], dram["ctxT"].rearrange("d (t p) -> d t p", p=P)).then_inc(ctx_loaded, 16)
            for n in ("x0", "fa0", "fg0", "fa1", "fg1", "a1", "moe1"):
                sp.dma_start(weights[n][:, :], packs[n][0]).then_inc(loaded[n], 16)
            for early, done in (("x0", L0_CROSS), ("fa0", F0_ATTN), ("fa1", F1_ATTN)):
                if PHASES > done + 1:
                    sp.wait_ge(tile_done, 2 + 16 * (done + 1))
                    for n in LATE[early]:
                        sp.dma_start(weights[n], packs[n][0]).then_inc(loaded[n], 16)
                        sp.wait_ge(loaded[n], 16)
            if PHASES > F1_GLU + 1:
                sp.wait_ge(tile_done, 2 + 16 * (F1_GLU + 1))
                sp.dma_start(alibi16.rearrange("p n k -> p (n k)"), packs["alibi"][0]).then_inc(loaded["alibi"], 16)
                sp.wait_ge(loaded["alibi"], 16)
            if PHASES > L1_MOE + 1:
                sp.wait_ge(tile_done, 2 + 16 * (L1_MOE + 1))
                sp.dma_start(experts[:, :], packs["moe2"][0]).then_inc(loaded["moe2"], 16)
                sp.wait_ge(loaded["moe2"], 16)
            if PHASES > L3_CROSS + 1:
                sp.wait_ge(tile_done, 2 + 16 * (L3_CROSS + 1))
                sp.dma_start(w16, dram["kernel8"]).then_inc(loaded8, 16)
                sp.dma_start(bias8, dram["bias8"][0].partition_broadcast(P)).then_inc(loaded8, 16)
                sp.dma_start(scale8, dram["scales8"][0].partition_broadcast(P)).then_inc(loaded8, 16)
            sp.wait_ge(tile_done, 2 + 16 * PHASES)
            sp.dma_start(out.rearrange("(t p) d -> p t d", p=P), state[:, :, :]).then_inc(out_stored, 16)
            sp.wait_ge(out_stored, 16)

        @block.gpsimd
        def _(pool):
            pool.wait_ge(x_loaded, 16)
            pool.wait_ge(tables_ready, 1)
            narrow, wide, glu = narrow_pool(pool), wide_pool(pool), glu_pool(pool)
            cross0 = cross0_pool(pool)
            for run, ph in zip((narrow, cross0, wide, glu, wide, glu, wide, narrow, moe1_pool, narrow, narrow, moe2_pool,
                                narrow, narrow, fp8_pool), range(PHASES)):
                run(ph)

        @block.tensor
        def _(pe):
            pe.wait_ge(loaded["const"], 16)
            pe.wait_ge(loaded["rows"], 16)
            pe.wait_ge(tables_ready, 1)
            narrow, wide, glu = narrow_tensor(pe), wide_tensor(pe), glu_tensor(pe)
            cross0 = cross0_tensor(pe)
            for run, ph in zip((narrow, cross0, wide, glu, wide, glu, wide, narrow, moe1_tensor, narrow, narrow,
                                moe2_tensor, narrow, narrow, fp8_tensor), range(PHASES)):
                run(ph)

        @block.scalar
        def _(act):
            act.wait_ge(tables_ready, 1)
            narrow, wide, glu = narrow_scalar(act), wide_scalar(act), glu_scalar(act)
            cross0 = cross0_scalar(act)
            for run, ph in zip((narrow, cross0, wide, glu, wide, glu, wide, narrow, moe1_scalar, narrow, narrow,
                                moe2_scalar, narrow, narrow, fp8_scalar), range(PHASES)):
                run(ph)

        @block.vector
        def _(dve):
            dve.wait_ge(loaded["const"], 16)
            dve.wait_ge(loaded["scales"], 16)
            dve.wait_ge(masks_loaded, 4 * 16)
            nc.vector.memset(ones_row[:, :], 1.0)
            nc.vector.memset(minus_half[:, :], -0.5)
            for s in STREAMS:
                nc.vector.memset(values8[s][:, :, :, :, :].rearrange("p j b a d -> p (j b a d)"), 0.0)
                nc.vector.memset(shT[s][:, :], 0.0)
                nc.vector.memset(values64(s).rearrange("p b c a d -> p (b c a d)"), 0.0)
            nc.vector.tensor_copy(ident16[:, :], ident)
            for l in range(2):
                nc.vector.tensor_tensor(rope_f[l][:, :], part("const", "rope_xpos"),
                                        weights["scales"][:, l * 256:(l + 1) * 256], ALU.mult)
            nc.vector.tensor_scalar(own16[:, :], own_u8[:, :], 0.0, OFF, ALU.is_equal, ALU.mult)
            nc.vector.tensor_scalar(seq_add[:, :], mask_int[:, :], 0.0, OFF, ALU.is_equal, ALU.mult)
            nc.vector.tensor_scalar(pads16[:, :, :], pads_int, 0.0, OFF, ALU.is_equal, ALU.mult)
            nc.vector.tensor_copy(causal16[:, :], part("const", "causal")).then_inc(setup_done, 1)
            dve.wait_ge(setup_done, 1)
            nc.vector.tensor_tensor(pads16[:, :, :], pads16[:, :, :],
                                    seq_add[:, :].unsqueeze(1).broadcast_to([P, TILES, S]), ALU.min)
            for s in STREAMS:
                for par in range(2):
                    rows = slice(par * S, (par + 1) * S)
                    nc.vector.memset(values8[s][rows, :, :, par, HD8:HD8 + 1], 1.0)
                    last = nc.vector.memset(values64(s)[rows, :, :, par, 64:65], 1.0)
            last.then_inc(tables_ready, 1)
            dve.wait_ge(tables_ready, 1)
            nc.vector.memset(stats[0][:, :], 0.0).then_inc(tile_done, 2)
            narrow, wide, glu = narrow_vector(dve), wide_vector(dve), glu_vector(dve)
            cross0 = cross0_vector(dve)
            for run, ph in zip((narrow, cross0, wide, glu, wide, glu, wide, narrow, moe1_vector, narrow, narrow,
                                moe2_vector, narrow, narrow, fp8_vector), range(PHASES)):
                run(ph)


def rope8_table():
    f = np.arange(P) % HD8
    theta = np.arange(S, dtype=np.float32)[None, :] / np.exp(
        2.0 * (f // 2).astype(np.float32) / HD8 * np.log(10000.0)).astype(np.float32)[:, None]
    cos, sin = np.cos(theta), np.sin(theta)
    sign = np.where(f % 2 == 0, -1.0, 1.0)[:, None]
    return np.concatenate([cos, sin * sign], axis=1).astype(np.float32)


def rope64_table(xpos):
    half = np.arange(0, 64, 2, dtype=np.float32)
    t = (np.arange(P) % S).astype(np.float32)
    freqs = np.tile(t[:, None] * (1.0 / 10000.0 ** (half / 64)).astype(np.float32)[None, :], (1, 2))
    cos, sin = np.cos(freqs), np.sin(freqs)
    sin = np.concatenate([-sin[:, :32], sin[:, 32:]], axis=1)
    scale = 1.0
    if xpos:
        base = (half + 0.4 * 64) / (1.4 * 64)
        scale = np.tile(base[None, :] ** ((t - S // 2) / 32.0)[:, None], (1, 2))
    return np.concatenate([cos * scale, cos / scale, sin * scale, sin / scale], axis=1).astype(np.float32)


def alibi_table():
    slopes = (2.0 ** -0.5) ** np.arange(1, H8 + 1)
    diff = np.arange(S)[None, :] - (np.arange(P) % S)[:, None]
    full = slopes[None, :, None] * diff[:, None, :] * np.sqrt(HD8)
    rest = full.reshape(P, H8 * S).astype(np.float32)
    parts = []
    for _ in range(3):
        top = (rest.view(np.uint32) & 0xFFFF0000).view(np.float32)
        parts.append(top)
        rest = rest - top
    future = np.broadcast_to((diff > 0)[:, None, :], (P, H8, S)).reshape(P, H8 * S)
    parts[0] = np.where(future, np.float32(NEG), parts[0]).astype(np.float32)
    return np.concatenate(parts, axis=1)


def constants():
    p = np.arange(P)
    causal = np.where(np.arange(S)[None, :] <= (p % S)[:, None], 0.0, NEG).astype(np.float32)
    own_head = (((p // HD8) % 8)[:, None] == np.arange(8)[None, :]).astype(np.float32)
    return {"ident": np.eye(P, dtype=np.float32), "causal": causal, "own_head": own_head, "rope8": rope8_table(),
            "rope64": rope64_table(False), "rope_xpos": rope64_table(True),
            "falling": np.tile(np.arange(EXP, 0, -1, dtype=np.float32), (P, 1)),
            "slot": np.tile(np.arange(CAP, dtype=np.float32), (P, 1)),
            "upto": (p[:, None] <= p[None, :]).astype(np.float32)}


def by_parity(w, heads, d):
    return w.reshape(w.shape[0], heads // 2, 2, d).transpose(0, 2, 1, 3).reshape(w.shape[0], heads * d)


def chunked(w):
    n = w.shape[0] // P
    return w.reshape(n, P, w.shape[1]).transpose(1, 0, 2).reshape(P, n * w.shape[1])


def rows_to(a, n):
    out = np.zeros((n,) + a.shape[1:], a.dtype)
    out[:a.shape[0]] = a
    return out


def layout(i):
    swap = np.arange(D) ^ 1

    def narrow(wq, wk, wv, wo=None, bq=None, bk=None, bv=None, rope=False):
        out = {"wq": wq.T, "wk": wk.T, "wv": by_parity(wv.T, H8, HD8)}
        if wo is not None:
            out["wo"] = wo.T
        if bq is not None:
            out["bv"] = bv[:, None]
            rows = [bq, bk]
            if rope:
                out |= {"wq_swapped": wq[swap].T, "wk_swapped": wk[swap].T}
                rows += [bq[swap], bk[swap]]
            out["bias"] = np.concatenate([np.stack([r[h * S:(h + 1) * S] for r in rows for h in range(2)], axis=1)] * 2)
        return out

    def named(prefix, names):
        return [i[prefix + n] for n in names.split()]

    packs = {"const": constants()}
    packs["a0"] = narrow(*named("L0_attn_", "wq wk wv wo bq bk bv"), rope=True)
    x0 = {n: i["L0_xattn_" + n] for n in ("Wq_c", "Wk_s", "Wv_s", "Wq_s", "Wk_c", "Wv_c", "Wg")}
    packs["rows"] = {"a0_bo": i["L0_attn_bo"], "x0_bv_s": i["L0_xattn_bv_s"], "x0_bv_c": i["L0_xattn_bv_c"],
                     "x0_bg": i["L0_xattn_bg"], "fg0_b2": i["L0_ffn_b2"][0], "fg1_b2": i["L0_ffn_b2"][1],
                     "x1_bo": i["L1_xattn_bo"], "a2_bo": i["L2_attn_bo"], "x2_bo": i["L2_xattn_bo"],
                     "a3_bo": i["L3_attn_bo"], "x3_bv": by_parity(i["L3_xattn_bv"][None], H8, HD8)[0],
                     "m1_br": i["L1_ffn_br"], "m2_bg": i["L2_ffn_gate_b"], }
    packs["rows"] = {n: a[None] for n, a in packs["rows"].items()}
    packs["m2rows"] = {"b2": i["L2_ffn_b2"].reshape(1, -1)}
    packs["scales"] = {}
    for l in range(2):
        q, k = i["L0_ffn_q_scale"][l], i["L0_ffn_k_scale"][l]
        for n, a in (("q", q), ("k", k), ("q_turned", np.roll(q, 32)), ("k_turned", np.roll(k, 32))):
            packs["scales"][f"{n}{l}"] = a[None]
    packs["x0"] = {"wq_c": x0["Wq_c"].T, "wk_s": x0["Wk_s"].T, "wq_s": x0["Wq_s"].T, "wk_c": x0["Wk_c"].T,
                   "wv_s": x0["Wv_s"].T, "wv_c": x0["Wv_c"].T, "wg0": x0["Wg"][:, :D].T, "wg1": x0["Wg"][:, D:].T,
                   "bias": np.stack(named("L0_xattn_", "bq_c bk_s bq_s bk_c"), axis=1)}
    for l in range(2):
        wqkv, wo = i["L0_ffn_wqkv"][l], i["L0_ffn_wo"][l]
        packs[f"fa{l}"] = {"wqk": wqkv[:, :1024], "wv": by_parity(by_parity(wqkv[:, 1024:], 8, 64), 8, 64),
                           "wo": chunked(by_parity(wo.T, 8, 64).T)}
        b1 = i["L0_ffn_b1"][l]
        w2 = rows_to(i["L0_ffn_w2"][l], 3 * P)
        packs[f"fg{l}"] = {"w1": i["L0_ffn_w1"][l], "w2": chunked(w2),
                           "b1": np.concatenate([rows_to(b1[:HID], 3 * P).reshape(3, P),
                                                 rows_to(b1[HID:], 3 * P).reshape(3, P)]).T,
                           "ln": np.stack([i["L0_ffn_ln_g"][l], i["L0_ffn_ln_b"][l]], axis=1)}
    packs["a1"] = {"wqk": i["L1_attn_wq"].T, "down": i["L1_attn_w_kv_down"].T,
                   "k_up": rows_to(i["L1_attn_w_k_up"].T, P), "wv": rows_to(by_parity(by_parity(i["L1_attn_w_v_up"].T, 16, 64), 16, 64), P),
                   "wo": chunked(by_parity(i["L1_attn_wo"], 16, 64).T)}
    packs["x1"] = narrow(*named("L1_xattn_", "Wq Wk Wv Wo"))
    packs["moe1"] = {"w1": i["L1_ffn_W1"].transpose(2, 0, 1).reshape(D, EXP * FF),
                     "w2": i["L1_ffn_W2"].reshape(EXP, D, FCH, P).transpose(3, 0, 2, 1).reshape(P, EXP * FCH * D),
                     "b1": i["L1_ffn_b1"].reshape(EXP * FCH, P).T, "wr": i["L1_ffn_Wr"].T,
                     "b2": rows_to(i["L1_ffn_b2"], P)}
    packs["a2"] = narrow(*named("L2_attn_", "Wq Wk Wv Wo bq bk bv"))
    packs["x2"] = narrow(*named("L2_xattn_", "Wq Wk Wv Wo bq bk bv"))
    packs["moe2"] = {"w1": i["L2_ffn_w1"].transpose(1, 0, 2).reshape(D, EXP * FF),
                     "w2": i["L2_ffn_w2"].reshape(EXP, FCH, P, D).transpose(2, 0, 1, 3).reshape(P, EXP * FCH * D),
                     "b1": i["L2_ffn_b1"].reshape(EXP * FCH, P).T, "wr": i["L2_ffn_gate_w"],
                     "pad": np.zeros((P, D), np.float32)}
    packs["a3"] = narrow(*named("L3_attn_", "Wq Wk Wv Wo bq bk bv"), rope=True)
    x3 = i["L3_xattn_Wv"]
    packs["x3"] = narrow(i["L3_xattn_Wq"], i["L3_xattn_Wk"], x3, None, *named("L3_xattn_", "bq bk bv"))
    packs["alibi"] = {"alibi": alibi_table()}
    return packs


def kernel(**inputs):
    import concourse.bacc as bacc
    from concourse.bass_utils import run_bass_kernel_spmd

    i = {n: np.asarray(a) for n, a in inputs.items()}
    nc = bacc.Bacc("TRN2", target_bir_lowering=False, num_devices=1)
    arrays, dram, packs = {}, {}, {}

    def declare(name, a):
        a = np.ascontiguousarray(a)
        arrays["in_" + name] = a
        return nc.dram_tensor("in_" + name, a.shape, mybir.dt.from_np(a.dtype), kind="ExternalInput").ap()

    for name, parts in layout(i).items():
        where, first = {}, 0
        for part, a in parts.items():
            where[part] = (first, a.shape[1])
            first += a.shape[1]
        whole = np.concatenate(list(parts.values()), axis=1)
        if name == "alibi":
            whole = whole.astype(i["L3_ffn_kernel"].dtype)
        packs[name] = (declare("pack_" + name, whole), where)
    dram["x"] = declare("x", i["x"].reshape(B * S, D))
    dram["ctxT"] = declare("ctxT", i["ctx_1024"].reshape(B * S, D).T)
    dram["own"] = declare("own", i["mask_1x1xSxS2_bk0"].reshape(S, S))
    dram["seq"] = declare("seq", i["mask_1x1xSxS2_ik0"].reshape(S, S))
    dram["pads"] = declare("pads", i["mask_Bx1x1xS2_ik0"].reshape(TILES, SEQS, S))
    dram["kernel8"] = declare("kernel8", i["L3_ffn_kernel"])
    dram["bias8"] = declare("bias8", i["L3_ffn_bias"][None])
    dram["scales8"] = declare("scales8", np.stack([i["L3_ffn_input_scale"], i["L3_ffn_kernel_scale"]], axis=1))
    out = nc.dram_tensor("out", (B * S, D), F32, kind="ExternalOutput").ap()
    program(nc, packs, dram, out)
    r = run_bass_kernel_spmd(nc, [arrays], core_ids=[0])
    return r.results[0]["out"].reshape(B, S, D)
```

```python
from contextlib import ExitStack

import numpy as np

import concourse.bass as bass
from concourse import mybir

F32 = mybir.dt.float32
BF16 = mybir.dt.bfloat16
FP8 = mybir.dt.float8e4
U8 = mybir.dt.uint8
I32 = mybir.dt.int32
ALU = mybir.AluOpType
ACT = mybir.ActivationFunctionType
X_AXIS = mybir.AxisListType.X
ds = bass.ds

P = 128
B, S, D = 32, 64, 128
TILES = B * S // P
SEQS = P // S
STREAMS = (0, 1)
TURNS = TILES // 2
GROUPS = TILES // 4
GT = 512
H8, HD8 = 16, 8
HID = 341
HCH = [128, 128, 85]
EXP = 8
FF = 512
FCH = FF // P
CAP = 80
EPS = 1e-5
NEG = -1e30
OFF = -1e20
BLOCKS = 12

(L0_ATTN, L0_CROSS, F0_ATTN, F0_GLU, F1_ATTN, F1_GLU, L1_ATTN, L1_CROSS, L1_MOE,
 L2_ATTN, L2_CROSS, L2_MOE, L3_ATTN, L3_CROSS, L3_FP8) = range(15)
PHASES = [1, 2, 6, 7, 8, 9, 10, 11, 12, 13, 14, 15][BLOCKS - 1]

NARROW = (L0_ATTN, L1_CROSS, L2_ATTN, L2_CROSS, L3_ATTN, L3_CROSS)
ROPED = (L0_ATTN, L3_ATTN)
GIVEN_CTX = (L0_CROSS, L1_CROSS, L2_CROSS, L3_CROSS)
PREFIX = {L0_ATTN: "a0", L0_CROSS: "x0", L1_CROSS: "x1", L2_ATTN: "a2", L2_CROSS: "x2", L3_ATTN: "a3", L3_CROSS: "x3"}
WIDE = (F0_ATTN, F1_ATTN, L1_ATTN)
GLU = (F0_GLU, F1_GLU)
ATTN = NARROW + WIDE
TILED = NARROW + WIDE + GLU + (L0_CROSS,)
FINISHED = TILED + (L2_MOE,)
PIPED = TILED
KEPT = (F0_ATTN, F0_GLU, F1_ATTN)

HAS_OUT = tuple(p for p in ATTN if p != L3_CROSS) + (L0_CROSS,)

FIRES = {
    "x_staged": FINISHED, "x_turned": TILED, "xT_ready": TILED,
    "projected": NARROW + (L0_CROSS,), "rope_biased": ROPED, "rope_scaled": ROPED,
    "qk_ready": NARROW + (L0_CROSS,), "values_ready": ATTN + (L0_CROSS,), "keys_spread": NARROW,
    "scores_ready": ATTN + (L0_CROSS,), "max_ready": ATTN + (L0_CROSS,), "scores_shifted": ATTN + (L0_CROSS,),
    "probs_ready": ATTN + (L0_CROSS,), "probs_turned": ATTN + (L0_CROSS,), "probsT_ready": ATTN + (L0_CROSS,),
    "mixed": ATTN + (L0_CROSS,), "sums_inverted": ATTN + (L0_CROSS,), "heads_normal": ATTN + (L0_CROSS,),
    "heads_turned": HAS_OUT, "headsT_ready": HAS_OUT, "y_ready": tuple(p for p in FINISHED if p != L3_CROSS),
    "sums_ready": WIDE + (L0_CROSS,), "gate_exp": (L0_CROSS,), "gate_den": (L0_CROSS,), "gate_ready": (L0_CROSS,),
    "paths_diff": (L0_CROSS,), "diff_gated": (L0_CROSS,), "y_mixed": (L0_CROSS,), "biased": (L0_CROSS,),
    "q_projected": WIDE, "k_projected": (L1_ATTN,), "latent_projected": (L1_ATTN,), "latent_ready": (L1_ATTN,),
    "squares": (F0_ATTN, F1_ATTN), "norms_sq": (F0_ATTN, F1_ATTN), "norms_floor": (F0_ATTN, F1_ATTN),
    "norms_inv": (F0_ATTN, F1_ATTN), "unit_ready": (F0_ATTN, F1_ATTN),
    "dispatched_made": (L2_MOE,), "dispatch_turned": (L2_MOE,), "dispatchT_ready": (L2_MOE,),
    "q_parts": WIDE, "q_rotated": WIDE, "q_turned": WIDE, "qT_ready": WIDE,
    "k_parts": (L1_ATTN,), "k_rotated": (L1_ATTN,), "k_turned": (L1_ATTN,), "kT_ready": (L1_ATTN,),
    "v_projected": WIDE + NARROW,
    "h_turned": GLU, "h_stats": GLU, "h_mean": GLU, "h_var": GLU, "h_rstd": GLU, "h_normal": GLU,
    "hn_turned": GLU, "hnT_ready": GLU, "up_ready": GLU, "gelu_ready": GLU, "gated_ready": GLU,
    "outer_sum": (F1_GLU,), "res_sum": tuple(p for p in FINISHED if p not in KEPT),
    "ln_stats": tuple(p for p in FINISHED if p not in KEPT),
}
for _n in ("ln_mean", "ln_var", "ln_rstd"):
    FIRES[_n] = FIRES["ln_stats"]


def program(nc, packs, dram, out):
    with ExitStack() as ctx:
        def sb(name, shape, dt=F32):
            return ctx.enter_context(nc.sbuf_tensor(name, shape, dt))

        def sem(name):
            return ctx.enter_context(nc.semaphore(name))

        state = sb("state", [P, TILES, D])
        inner = sb("inner", [P, TILES, D])
        ctxT = sb("ctxT", [P, TILES, P])
        weights = {n: sb("w_" + n, [P if n == "scales" else ap.shape[0], ap.shape[1]]) for n, (ap, _) in packs.items()
                   if n not in ("moe1", "moe2", "alibi", "a2", "a3", "x3", "x1", "x2", "m2rows", "scales")}
        experts = sb("experts", [P, packs["moe1"][0].shape[1]])
        weights["moe1"] = weights["moe2"] = experts
        LATE = {"fa0": ("a2", "a3", "x3"), "fa1": ("x1", "x2"), "x0": ("m2rows",)}
        for early, late in LATE.items():
            first = 0
            for n in late:
                rows, cols = packs[n][0].shape
                weights[n] = weights[early][0:rows, first:first + cols]
                first += cols

        def part(pack, name):
            first, cols = packs[pack][1][name]
            return weights[pack][:, first:first + cols]

        ident = part("const", "ident")
        ones_row = sb("ones_row", [1, P])
        ident16 = sb("ident16", [P, P], BF16)
        causal16 = sb("causal16", [P, S], BF16)
        alibi16 = inner[:, 0:12, :].rearrange("p a n -> p (a n)").bitcast(BF16).rearrange("p (n k) -> p n k", n=3)
        rope_f = [sb(f"rope_f{l}", [P, 4 * 64]) for l in range(2)]
        seq_add = sb("seq_add", [P, S], BF16)
        own16 = sb("own16", [P, S], BF16)
        pads16 = sb("pads16", [P, TILES, S], BF16)
        pads_tile = [sb(f"pads_tile{s}", [P, S], BF16) for s in STREAMS]
        minus_half = sb("minus_half", [P, 16])

        BIG = 1024
        VALUES64 = SEQS * 8 * 2 * 64
        SCRATCH = 7 * BIG + VALUES64
        arena = sb("arena", [P, 2 * SCRATCH])

        pads_int = arena[:, 0:TILES * S].bitcast(I32).rearrange("p (t k) -> p t k", t=TILES)

        mask_int = arena[:, 1024:1024 + S].bitcast(I32)
        own_u8 = arena[:, 1088:1088 + S // 4].bitcast(U8)
        weights["scales"] = arena[:, 1152:1152 + 512]

        def big(s, k, cols=1024):
            at0 = s * SCRATCH + k * BIG
            return arena[:, at0:at0 + cols]

        xs = [sb(f"xs{s}", [P, D]) for s in STREAMS]
        cs = [sb(f"cs{s}", [P, P]) for s in STREAMS]
        xT = [sb(f"xT{s}", [P, P]) for s in STREAMS]
        shT = [sb(f"shT{s}", [P, P]) for s in STREAMS]
        total = [sb(f"total{s}", [P, D]) for s in STREAMS]
        stats = [sb(f"stats{s}", [P, 6]) for s in STREAMS]
        moments = [sb(f"moments{s}", [P, 2]) for s in STREAMS]
        var_eps = [sb(f"var_eps{s}", [P, 1]) for s in STREAMS]
        rstd = [sb(f"rstd{s}", [P, 1]) for s in STREAMS]
        maxima = [sb(f"maxima{s}", [P, 16]) for s in STREAMS]
        row_sum = [sb(f"row_sum{s}", [P, 16]) for s in STREAMS]
        inv_sum = [sb(f"inv_sum{s}", [P, 16]) for s in STREAMS]
        sq_sum = [sb(f"sq_sum{s}", [P, 16]) for s in STREAMS]
        sq_floor = [sb(f"sq_floor{s}", [P, 16]) for s in STREAMS]
        inv_norm = [sb(f"inv_norm{s}", [P, 16]) for s in STREAMS]
        values8 = [sb(f"values8_{s}", [P, H8 // 2, SEQS, 2, HD8 + 1]) for s in STREAMS]
        heads_out = [sb(f"heads_out{s}", [P, D]) for s in STREAMS]
        outT = [sb(f"outT{s}", [P, 2, P]) for s in STREAMS]
        gate = [sb(f"gate{s}", [P, D]) for s in STREAMS]
        latentT = [shT[s][0:S, :] for s in STREAMS]
        h_stats = [sb(f"h_stats{s}", [P, 6]) for s in STREAMS]
        h_moments = [sb(f"h_moments{s}", [P, 2]) for s in STREAMS]
        h_var = [sb(f"h_var{s}", [P, 1]) for s in STREAMS]
        h_rstd = [sb(f"h_rstd{s}", [P, 1]) for s in STREAMS]

        ps = [ctx.enter_context(nc.psum_tensor(f"ps{s}", [P, 4, 512], F32)) for s in STREAMS]

        def bank(s, b, lo=0, hi=512):
            return ps[s][:, b, lo:hi]

        def pair(s, b):
            return ps[s][:, b:b + 2, :].rearrange("p a n -> p (a n)")

        signal = {n: sem(n) for n in FIRES}
        tile_done = sem("tile_done")
        setup_done = sem("setup_done")
        x_loaded, ctx_loaded, out_stored = sem("x_loaded"), sem("ctx_loaded"), sem("out_stored")
        loaded = {n: sem("loaded_" + n) for n in packs}
        masks_loaded = sem("masks_loaded")
        tables_ready = sem("tables_ready")
        moe_sems = {n: sem(n) for n in (
            "g_staged", "g_turned", "g_xT", "g_logits", "g_top", "g_eq", "g_rank", "g_first", "g_onehot",
            "g_oneturned", "g_onehotT", "g_bias", "h_done", "relu_done", "ye_done", "acc_done",
            "g_sum", "g_stats", "g_mean", "g_var", "g_rstd")}
        gate_sems = {n: sem(n) for n in (
            "c_logits", "c_chain", "c_shifted", "c_exp", "c_onehot", "c_counts", "c_staged", "c_made", "c_slot",
            "c_dispatched", "c_slotsT", "c_up", "c_gelu", "c_down", "c_out")}
        fp_sems = {n: sem(n) for n in ("f_once", "f_chain", "f_rounded", "f_turned", "f_turned_copy", "f_y")}
        loaded8 = sem("loaded8")

        def at(name, ph, v, s):
            fires = sorted(FIRES[name])
            return 16 * fires.index(ph) + s + 1 + v

        def tiles_done(ph, v, s):
            return 16 * ph + s + 1 + v

        class Turn:

            def __init__(self, eng, ph, turn):
                self.eng, self.ph = eng, ph
                self.v = turn * 2

            def wait(self, name, s, alone=False):
                self.eng.wait_ge(signal[name], at(name, self.ph, self.v, s))
                if alone:
                    self.eng.nop(nofuse=True)

            def tile(self, s):
                return self.v + s

            def wait_last(self, s):
                self.eng.wait_ge(tile_done, tiles_done(self.ph, self.v, s))

        def piped(eng, ph, body):
            body(None, Turn(eng, ph, 0))
            with eng.Fori(0, TURNS - 1) as turn:
                body(Turn(eng, ph, turn), Turn(eng, ph, turn + 1))
            body(Turn(eng, ph, TURNS - 1), None)

        def piped3(eng, ph, body):
            body(None, None, Turn(eng, ph, 0))
            body(None, Turn(eng, ph, 0), Turn(eng, ph, 1))
            with eng.Fori(0, TURNS - 2) as turn:
                body(Turn(eng, ph, turn), Turn(eng, ph, turn + 1), Turn(eng, ph, turn + 2))
            body(Turn(eng, ph, TURNS - 2), Turn(eng, ph, TURNS - 1), None)
            body(Turn(eng, ph, TURNS - 1), None, None)

        def turns(eng, ph, body):
            with eng.Fori(0, TURNS) as turn:
                body(Turn(eng, ph, turn))

        def mm(o, lhsT, rhs, start=True, stop=True):
            return nc.tensor.matmul(o, lhsT, rhs, start=start, stop=stop, skip_group_check=True)

        def tile_of(x, t, s):
            return x[:, ds(t.tile(s), 1), :].rearrange("p a n -> p (a n)")

        def stage_pool(t, s, src, context=False):
            if t.ph not in PIPED:
                t.eng.wait_ge(tile_done, tiles_done(t.ph, t.v, s))
            if context:
                nc.gpsimd.tensor_copy(cs[s][:, :], tile_of(ctxT, t, s))
            if t.ph == L3_CROSS:
                nc.gpsimd.tensor_copy(pads_tile[s][:, :], tile_of(pads16, t, s))
            nc.gpsimd.tensor_copy(xs[s][:, :], tile_of(src, t, s))\
                .then_inc(signal["x_staged"], 1)

        def turn_x_pe(t, s):
            t.wait("x_staged", s)
            nc.tensor.transpose(bank(s, 0, 0, P), xs[s][:, :], ident).then_inc(signal["x_turned"], 1)

        def turn_x_act(t, s, shifted):
            t.wait("x_turned", s)
            if not shifted:
                nc.scalar.copy(xT[s][:, :], bank(s, 0, 0, P)).then_inc(signal["xT_ready"], 1)
                return
            nc.scalar.copy(shT[s][0:S, :], ps[s][0:S, 0, 0:P])
            up = shT[s][S:P, :].rearrange("p (b t) -> p b t", b=SEQS)
            nc.scalar.copy(up[:, :, 1:S], ps[s][S:P, 0, 0:P].rearrange("p (b t) -> p b t", b=SEQS)[:, :, 0:S - 1])\
                .then_inc(signal["xT_ready"], 1)

        def norm_pool(t, s):
            t.wait("ln_var", s)
            nc.gpsimd.tensor_tensor(rstd[s][:, :], var_eps[s][:, :], minus_half[:, 0:1], ALU.pow)\
                .then_inc(signal["ln_rstd"], 1)

        def finish_vector(t, y, dst, ready="y_ready", outer=False, src=None):
            sum_vector(t, y, dst, ready, outer, src)
            if t.ph not in KEPT:
                norm_vector(t, dst)

        def sum_vector(t, y, dst, ready="y_ready", outer=False, src=None):
            kept = t.ph in KEPT
            src = src if src is not None else state
            for s in STREAMS:
                t.wait(ready, s)
                if kept:
                    nc.vector.tensor_tensor(tile_of(dst, t, s), tile_of(src, t, s), y(s), ALU.add)\
                        .then_inc(tile_done, 1)
                elif outer:
                    nc.vector.tensor_tensor(total[s][:, :], tile_of(src, t, s), y(s), ALU.add)\
                        .then_inc(signal["outer_sum"], 1)
                    t.wait("outer_sum", s)
                    nc.vector.tensor_tensor(total[s][:, :], total[s][:, :], tile_of(state, t, s), ALU.add)\
                        .then_inc(signal["res_sum"], 1)
                else:
                    nc.vector.tensor_tensor(total[s][:, :], tile_of(src, t, s), y(s), ALU.add)\
                        .then_inc(signal["res_sum"], 1)
            if kept:
                return
            for s in STREAMS:
                t.wait("res_sum", s)
                nc.vector.bn_stats(stats[s][:, :], total[s][:, :]).then_inc(signal["ln_stats"], 1)
            for s in STREAMS:
                t.wait("ln_stats", s, alone=True)
                nc.vector.bn_aggr(moments[s][:, :], stats[s][:, :]).then_inc(signal["ln_mean"], 1)
            for s in STREAMS:
                t.wait("ln_mean", s)
                nc.vector.tensor_scalar(var_eps[s][:, :], moments[s][:, 1:2], EPS, None, ALU.add)\
                    .then_inc(signal["ln_var"], 1)

        def norm_vector(t, dst):
            for s in STREAMS:
                t.wait("ln_rstd", s)
                nc.vector.tensor_scalar(tile_of(dst, t, s), total[s][:, :],
                                        moments[s][:, 0:1], rstd[s][:, 0:1], ALU.subtract, ALU.mult)\
                    .then_inc(tile_done, 1)

        def softmax_vector(t, heads, streams=STREAMS):
            half = heads // 2
            for s in streams:
                t.wait("scores_ready", s)
                sc = ps[s][:, 2:4, 0:half * S].rearrange("p a (h k) -> p a h k", h=half)
                mx = maxima[s][:, 0:heads].rearrange("p (a h) -> p a h", a=2)
                nc.vector.reduce_max(mx, sc, X_AXIS).then_inc(signal["max_ready"], 1)
                t.wait("max_ready", s)
                nc.vector.tensor_tensor(probs(s)[:, 0:heads * S].rearrange("p (a h k) -> p a h k", a=2, h=half), sc,
                                        mx.unsqueeze(3).broadcast_to([P, 2, half, S]),
                                        ALU.subtract).then_inc(signal["scores_shifted"], 1)

        def exp_scalar(t, heads, scale, streams=STREAMS):
            n = heads * S
            for s in streams:
                t.wait("scores_shifted", s)
                nc.scalar.activation(probs(s)[:, 0:n], probs(s)[:, 0:n], ACT.Exp, scale=scale)\
                    .then_inc(signal["probs_ready"], 1)

        def probsT_scalar(t, heads):
            n = heads * S
            for s in STREAMS:
                t.wait("probs_turned", s)
                nc.scalar.copy(probsT(s)[:, 0:n], pair(s, 2)[:, 0:n]).then_inc(signal["probsT_ready"], 1)

        def turn_probs_pe(t, heads, streams=STREAMS):
            for s in streams:
                t.wait("probs_ready", s)
                for j in range(heads // 2):
                    last = nc.tensor.transpose(pair(s, 2)[:, j * P:(j + 1) * P], probs(s)[:, j * P:(j + 1) * P], ident)
                last.then_inc(signal["probs_turned"], 1)

        def roped(s):
            return big(s, 0)

        def query8(s):
            return big(s, 1, 256).rearrange("p (h b t) -> p h b t", h=2, b=SEQS)

        def key8(s):
            return big(s, 1)[:, 256:384]

        def keys_wide(s):
            return big(s, 2)

        def probs(s):
            return big(s, 5)

        def probsT(s):
            return big(s, 6)

        VAL = H8 // 2 * 4 * (HD8 + 1)

        def narrow_pool(pool):
            def run(ph):
                if ph in GIVEN_CTX:
                    pool.wait_ge(ctx_loaded, 16)
                pool.wait_ge(tile_done, 2 + 16 * ph)
                for s in STREAMS:
                    nc.gpsimd.memset(big(s, 1, 256), 0.0)

                def body(tail, middle, front):
                    if front:
                        for s in STREAMS:
                            if middle:
                                middle.wait("v_projected", s)
                            stage_pool(front, s, state, context=ph in GIVEN_CTX)
                    if tail:
                        for s in STREAMS:
                            norm_pool(tail, s)
                    if front:
                        for s in STREAMS:
                            front.wait("qk_ready", s)
                            nc.gpsimd.tensor_tensor(
                                keys_wide(s).rearrange("p (a h t) -> p a h t", a=2, h=8),
                                key8(s).rearrange("p (a t) -> p a t", a=2).unsqueeze(2).broadcast_to([P, 2, 8, S]),
                                part("const", "own_head").unsqueeze(1).unsqueeze(3).broadcast_to([P, 2, 8, S]),
                                ALU.mult).then_inc(signal["keys_spread"], 1)
                piped3(pool, ph, body)
            return run

        def narrow_tensor(pe):
            def run(ph):
                w = PREFIX[ph]
                has_out = ph != L3_CROSS
                pe.wait_ge(loaded[w], 16)
                if ph == L2_ATTN:
                    pe.wait_ge(loaded["alibi"], 16)

                def project(t, s):
                    src = cs[s] if ph in GIVEN_CTX else xT[s]
                    kinds = [("wq", xT[s]), ("wk", src)]
                    if ph in ROPED:
                        kinds += [("wq_swapped", xT[s]), ("wk_swapped", src)]
                    for n, (name, rhs) in enumerate(kinds):
                        for half in range(2):
                            for b in range(SEQS):
                                last = mm(ps[s][b * S:(b + 1) * S, 0, n * P + half * S:n * P + (half + 1) * S],
                                          part(w, name)[:, half * S:(half + 1) * S], rhs[:, b * S:(b + 1) * S])
                    last.then_inc(signal["projected"], 1)

                def project_values(t, s):
                    src = cs[s] if ph in GIVEN_CTX else xT[s]
                    for par in range(2):
                        for b in range(SEQS):
                            o = ps[s][par * S:(par + 1) * S, 0, b * S:(b + 1) * S]
                            last = mm(o, src[:, b * S:(b + 1) * S], part(w, "wv")[:, par * S:(par + 1) * S],
                                      stop=has_out)
                            if not has_out:
                                last = mm(o, ones_row[:, 0:S], part("rows", "x3_bv")[:, par * S:(par + 1) * S],
                                          start=False)
                    last.then_inc(signal["v_projected"], 1)

                def score(t, s):
                    opened = ph != L2_CROSS
                    for half in range(2):
                        if ph == L2_ATTN:
                            for n in range(3):
                                mm(bank(s, 2 + half), ident16[:, :], alibi16[:, n, half * 512:(half + 1) * 512],
                                   start=(n == 0), stop=False)
                        elif opened:
                            table = {L1_CROSS: own16, L3_CROSS: pads_tile[s]}.get(ph, causal16)
                            mm(bank(s, 2 + half), ident16[:, :], table[:, :].unsqueeze(1).broadcast_to([P, 8, S]),
                               stop=False)
                        last = mm(bank(s, 2 + half), query8(s)[:, half, :, :].rearrange("p b t -> p (b t)"),
                                  keys_wide(s)[:, half * 512:(half + 1) * 512], start=not opened)
                    last.then_inc(signal["scores_ready"], 1)

                def mix(t, s):
                    t.wait("values_ready", s)
                    for j in range(H8 // 2):
                        last = mm(bank(s, 1, j * 36, (j + 1) * 36), probsT(s)[:, j * P:(j + 1) * P],
                                  values8[s][:, j, :, :, :].rearrange("p b a d -> p (b a d)"))
                    last.then_inc(signal["mixed"], 1)

                def body(tail, middle, front):
                    for s in STREAMS:
                        if tail:
                            tail.wait("probsT_ready", s)
                            mix(tail, s)
                        if middle:
                            middle.wait("keys_spread", s)
                            score(middle, s)
                    if middle:
                        for s in STREAMS:
                            project_values(middle, s)
                    for s in STREAMS:
                        if tail and has_out:
                            tail.wait("heads_normal", s)
                            nc.tensor.transpose(bank(s, 1, VAL, VAL + P), heads_out[s][:, :], ident)\
                                .then_inc(signal["heads_turned"], 1)
                        if front:
                            if middle:
                                middle.wait("values_ready", s)
                            turn_x_pe(front, s)
                    if tail and has_out:
                        for s in STREAMS:
                            tail.wait("headsT_ready", s)
                            mm(bank(s, 1, 0, P), outT[s][:, 0, :], part(w, "wo"), stop=False)
                            mm(bank(s, 1, 0, P), ones_row[:, :], part("rows", w + "_bo"), start=False)\
                                .then_inc(signal["y_ready"], 1)
                    for s in STREAMS:
                        if front:
                            front.wait("xT_ready", s)
                            project(front, s)
                        if middle:
                            turn_probs_pe(middle, H8, streams=(s,))
                    if tail:
                        for s in STREAMS:
                            tail.wait("res_sum" if has_out else "heads_normal", s)
                piped3(pe, ph, body)
            return run

        def narrow_scalar(act):
            def run(ph):
                w = PREFIX[ph]
                has_out = ph != L3_CROSS
                act.wait_ge(loaded[w], 16)
                scale = float(1.0 / np.sqrt(np.float32(HD8)))

                def body(tail, middle, front):
                    if middle:
                        for s in STREAMS:
                            middle.wait("v_projected", s)
                            if tail:
                                tail.wait("mixed", s)
                            for par in range(2):
                                rows = slice(par * S, (par + 1) * S)
                                for b in range(SEQS):
                                    last = nc.scalar.copy(
                                        values8[s][rows, :, b, par, 0:HD8],
                                        ps[s][rows, 0, b * S:(b + 1) * S].rearrange("p (j d) -> p j d", j=8))
                            last.then_inc(signal["values_ready"], 1)
                    if front:
                        for s in STREAMS:
                            turn_x_act(front, s, False)
                    if tail and has_out:
                        for s in STREAMS:
                            tail.wait("heads_turned", s)
                            if ph == L1_CROSS:
                                nc.scalar.copy(outT[s][:, 0, :], bank(s, 1, VAL, VAL + P))\
                                    .then_inc(signal["headsT_ready"], 1)
                            else:
                                nc.scalar.activation(outT[s][:, 0, :], bank(s, 1, VAL, VAL + P), ACT.Identity,
                                                     bias=part(w, "bv")[:, 0:1]).then_inc(signal["headsT_ready"], 1)
                    if middle:
                        exp_scalar(middle, H8, scale)
                        probsT_scalar(middle, H8)
                piped3(act, ph, body)
            return run

        def narrow_vector(dve):
            def run(ph):
                w = PREFIX[ph]
                dve.wait_ge(loaded[w], 16)

                def spread_query(s, make):
                    for b in range(SEQS):
                        make(query8(s)[b * S:(b + 1) * S, :, b, :], slice(b * S, (b + 1) * S))

                def queries_and_keys(t, s):
                    def halves(x):
                        return x.rearrange("p (h t) -> p h t", h=2)
                    t.wait("projected", s)
                    if ph in ROPED:
                        n8 = roped(s)[:, 0:512].rearrange("p (n t) -> p n t", n=8)
                        nc.vector.tensor_tensor(n8, bank(s, 0).rearrange("p (n t) -> p n t", n=8),
                                                part(w, "bias").unsqueeze(2).broadcast_to([P, 8, S]), ALU.add)\
                            .then_inc(signal["rope_biased"], 1)
                        t.wait("rope_biased", s)
                        f4 = roped(s)[:, 0:512].rearrange("p (f n t) -> p f n t", f=2, n=4)
                        table = part("const", "rope8").rearrange("p (f t) -> p f t", f=2)
                        nc.vector.tensor_tensor(f4, f4, table.unsqueeze(2).broadcast_to([P, 2, 4, S]), ALU.mult)\
                            .then_inc(signal["rope_scaled"], 1)
                        t.wait("rope_scaled", s)
                        spread_query(s, lambda o, r: nc.vector.tensor_tensor(
                            o, halves(roped(s)[r, 0:128]), halves(roped(s)[r, 256:384]), ALU.add))
                        nc.vector.tensor_tensor(key8(s), roped(s)[:, 128:256], roped(s)[:, 384:512], ALU.add)\
                            .then_inc(signal["qk_ready"], 1)
                    elif ph == L1_CROSS:
                        spread_query(s, lambda o, r: nc.vector.tensor_copy(o, halves(ps[s][r, 0, 0:128])))
                        nc.vector.tensor_copy(key8(s), bank(s, 0, 128, 256)).then_inc(signal["qk_ready"], 1)
                    else:
                        spread_query(s, lambda o, r: nc.vector.tensor_tensor(
                            o, halves(ps[s][r, 0, 0:128]),
                            part(w, "bias")[r, 0:2].unsqueeze(2).broadcast_to([S, 2, S]), ALU.add))
                        nc.vector.tensor_tensor(halves(key8(s)), halves(bank(s, 0, 128, 256)),
                                                part(w, "bias")[:, 2:4].unsqueeze(2).broadcast_to([P, 2, S]), ALU.add)\
                            .then_inc(signal["qk_ready"], 1)

                dve.wait_ge(tile_done, 2 + 16 * ph)

                def normal_heads(t, s):
                    t.wait("mixed", s)
                    for b in range(SEQS):
                        rows = slice(b * S, (b + 1) * S)
                        sums = ps[s][rows, 1, 0:VAL].rearrange("p (j b n d) -> p j b n d", j=8, b=SEQS, n=2)
                        last = nc.vector.reciprocal(inv_sum[s][rows, :].rearrange("p (j n) -> p j n", n=2),
                                                    sums[:, :, b, :, HD8])
                    last.then_inc(signal["sums_inverted"], 1)
                    t.wait("sums_inverted", s)
                    for b in range(SEQS):
                        rows = slice(b * S, (b + 1) * S)
                        mix = ps[s][rows, 1, 0:VAL].rearrange("p (j b n d) -> p j b n d", j=8, b=SEQS, n=2)
                        last = nc.vector.tensor_tensor(
                            heads_out[s][rows, :].rearrange("p (j n d) -> p j n d", j=8, n=2),
                            mix[:, :, b, :, 0:HD8],
                            inv_sum[s][rows, :].rearrange("p (j n) -> p j n", n=2).unsqueeze(3)
                            .broadcast_to([S, 8, 2, HD8]), ALU.mult)
                    last.then_inc(signal["heads_normal"], 1)

                def body(tail, middle, front):
                    for s in STREAMS:
                        if tail:
                            normal_heads(tail, s)
                        if middle:
                            softmax_vector(middle, H8, streams=(s,))
                    if tail:
                        if ph == L3_CROSS:
                            sum_vector(tail, lambda s: heads_out[s][:, :], state, ready="heads_normal")
                        else:
                            sum_vector(tail, lambda s: bank(s, 1, 0, P), state)
                    if front:
                        for s in STREAMS:
                            queries_and_keys(front, s)
                    if tail:
                        norm_vector(tail, state)
                piped3(dve, ph, body)
            return run

        def wide_heads(ph):
            return 16 if ph == L1_ATTN else 8

        def wide_pack(ph):
            return {F0_ATTN: "fa0", F1_ATTN: "fa1", L1_ATTN: "a1"}[ph]

        def key_rotated(s):
            return big(s, 1)

        def rope_swapped(s):
            return big(s, 2)

        def queryT(s):
            return big(s, 3)

        def keyT(s):
            return big(s, 4)

        def mixed_heads(s):
            return probs(s)

        def headsT(s):
            return probsT(s)

        def values64(s):
            return big(s, 7, VALUES64).rearrange("p (b c a d) -> p b c a d", b=SEQS, c=8, a=2)

        def wide_pool(pool):
            def run(ph):
                src = state if ph in (F0_ATTN, L1_ATTN) else inner
                pool.wait_ge(tile_done, 2 + 16 * ph)

                def body(back, front):
                    if front:
                        for s in STREAMS:
                            if back:
                                back.wait("x_turned", s)
                            stage_pool(front, s, src)
                        if ph != L1_ATTN:
                            for s in STREAMS:
                                front.wait("norms_floor", s)
                                nc.gpsimd.tensor_tensor(inv_norm[s][:, :], sq_floor[s][:, :], minus_half[:, :],
                                                        ALU.pow).then_inc(signal["norms_inv"], 1)
                        for s in STREAMS:
                            front.wait("q_parts", s)
                            nc.gpsimd.tensor_tensor(roped(s), roped(s), rope_swapped(s), ALU.add)\
                                .then_inc(signal["q_rotated"], 1)
                        if ph == L1_ATTN:
                            for s in STREAMS:
                                front.wait("k_parts", s)
                                nc.gpsimd.tensor_tensor(key_rotated(s), key_rotated(s), rope_swapped(s), ALU.add)\
                                    .then_inc(signal["k_rotated"], 1)
                    if back and ph == L1_ATTN:
                        for s in STREAMS:
                            norm_pool(back, s)
                piped(pool, ph, body)
            return run

        def wide_tensor(pe):
            def run(ph):
                heads, w = wide_heads(ph), wide_pack(ph)
                half = heads // 2
                pe.wait_ge(loaded[w], 16)

                def score(t, s):
                    t.wait_last(s)
                    t.wait("kT_ready" if ph == L1_ATTN else "qT_ready", s)
                    for k in range(2):
                        mm(bank(s, 2 + k, 0, half * S), ident16[:, :],
                           causal16[:, :].unsqueeze(1).broadcast_to([P, half, S]), stop=False)
                    keys = keyT(s) if ph == L1_ATTN else queryT(s)[:, 512:1024]
                    for par in range(2):
                        rows = slice(par * S, (par + 1) * S)
                        for b in range(SEQS):
                            for j in range(half):
                                cols = slice(j * P + b * S, j * P + (b + 1) * S)
                                last = mm(ps[s][b * S:(b + 1) * S, 2 + par, j * S:(j + 1) * S],
                                          queryT(s)[rows, cols], keys[rows, cols], start=False)
                    last.then_inc(signal["scores_ready"], 1)

                def turn(t, s, source, done):
                    for j in range(8):
                        last = nc.tensor.transpose(pair(s, 0)[:, j * P:(j + 1) * P], source[:, j * P:(j + 1) * P], ident)
                    last.then_inc(signal[done], 1)

                def project(t, s):
                    rows = xT[s] if ph == L1_ATTN else shT[s]
                    wq = part(w, "wqk")
                    for k in range(2):
                        last = mm(bank(s, k), rows[:, :], wq[:, k * 512:(k + 1) * 512])
                    last.then_inc(signal["q_projected"], 1)

                def project_values(t, s):
                    for par in range(2):
                        for b in range(SEQS):
                            o = pair(s, 0)[par * S:(par + 1) * S, b * half * S:(b + 1) * half * S]
                            wv = part(w, "wv")[:, par * half * S:(par + 1) * half * S]
                            if ph == L1_ATTN:
                                last = mm(o, latentT[s][:, b * S:(b + 1) * S], wv[0:S, :])
                            else:
                                last = mm(o, shT[s][:, b * S:(b + 1) * S], wv)
                    last.then_inc(signal["v_projected"], 1)

                def mix(t, s):
                    t.wait("probsT_ready", s)
                    for c in range(half):
                        for b in range(SEQS):
                            last = mm(pair(s, 2)[b * S:(b + 1) * S, c * P:(c + 1) * P],
                                      probsT(s)[:, c * P + b * S:c * P + (b + 1) * S],
                                      values64(s)[:, b, c, :, :].rearrange("p a d -> p (a d)"))
                    last.then_inc(signal["mixed"], 1)

                def turn_heads(t, s):
                    t.wait("heads_normal", s)
                    for j in range(half):
                        last = nc.tensor.transpose(pair(s, 2)[:, j * P:(j + 1) * P],
                                                   mixed_heads(s)[:, j * P:(j + 1) * P], ident)
                    last.then_inc(signal["heads_turned"], 1)

                def output(t, s):
                    t.wait("headsT_ready", s)
                    for j in range(half):
                        last = mm(bank(s, 3, 0, P), headsT(s)[:, j * P:(j + 1) * P],
                                  part(w, "wo")[:, j * D:(j + 1) * D], start=(j == 0), stop=(j == half - 1))
                    last.then_inc(signal["y_ready"], 1)

                def body(back, front):
                    for s in STREAMS:
                        if back:
                            score(back, s)
                        if front:
                            if back:
                                back.wait("values_ready", s)
                            turn_x_pe(front, s)
                    if front:
                        for s in STREAMS:
                            front.wait("xT_ready", s)
                            if ph == L1_ATTN:
                                mm(ps[s][0:S, 1, 0:P], part(w, "down"), xT[s][:, :])\
                                    .then_inc(signal["latent_projected"], 1)
                            else:
                                project(front, s)
                        if ph == L1_ATTN:
                            for s in STREAMS:
                                front.wait("latent_ready", s)
                                project(front, s)
                    if back:
                        turn_probs_pe(back, heads)
                    if front and ph == L1_ATTN:
                        for s in STREAMS:
                            front.wait("q_parts", s)
                            for k in range(2):
                                last = mm(bank(s, k), latentT[s], part(w, "k_up")[0:S, k * 512:(k + 1) * 512])
                            last.then_inc(signal["k_projected"], 1)
                    if back:
                        for s in STREAMS:
                            mix(back, s)
                    if front and ph == L1_ATTN:
                        for s in STREAMS:
                            front.wait("q_rotated", s)
                            front.wait("k_parts", s)
                            turn(front, s, roped(s), "q_turned")
                    if back:
                        for s in STREAMS:
                            turn_heads(back, s)
                        for s in STREAMS:
                            output(back, s)
                    if front:
                        for s in STREAMS:
                            if ph == L1_ATTN:
                                front.wait("k_rotated", s)
                                front.wait("qT_ready", s)
                                turn(front, s, key_rotated(s), "k_turned")
                            else:
                                front.wait("q_rotated", s)
                                turn(front, s, roped(s), "q_turned")
                        for s in STREAMS:
                            front.wait("kT_ready" if ph == L1_ATTN else "qT_ready", s, alone=True)
                            project_values(front, s)
                piped(pe, ph, body)
            return run

        def wide_scalar(act):
            def run(ph):
                heads = wide_heads(ph)
                half = heads // 2

                def body(back, front):
                    if front:
                        for s in STREAMS:
                            turn_x_act(front, s, shifted=ph != L1_ATTN)
                    if front and ph == L1_ATTN:
                        for s in STREAMS:
                            front.wait("latent_projected", s)
                            nc.scalar.copy(latentT[s], ps[s][0:S, 1, 0:P]).then_inc(signal["latent_ready"], 1)
                    if back:
                        exp_scalar(back, heads, 0.125 if ph == L1_ATTN else 8.0)
                    if front and ph != L1_ATTN:
                        for s in STREAMS:
                            front.wait("q_projected", s)
                            nc.scalar.activation(rope_swapped(s), pair(s, 0), ACT.Square)\
                                .then_inc(signal["squares"], 1)
                    if back:
                        probsT_scalar(back, heads)

                    def queries():
                        for s in STREAMS:
                            front.wait("q_turned", s)
                            nc.scalar.copy(queryT(s), pair(s, 0)).then_inc(signal["qT_ready"], 1)

                    if front and ph == L1_ATTN:
                        queries()
                    if back:
                        for s in STREAMS:
                            back.wait("heads_turned", s)
                            nc.scalar.copy(headsT(s)[:, 0:half * P], pair(s, 2)[:, 0:half * P])\
                                .then_inc(signal["headsT_ready"], 1)
                    if front:
                        if ph == L1_ATTN:
                            for s in STREAMS:
                                front.wait("k_turned", s)
                                nc.scalar.copy(keyT(s), pair(s, 0)).then_inc(signal["kT_ready"], 1)
                        else:
                            queries()
                        for s in STREAMS:
                            front.wait("v_projected", s)
                            if back:
                                back.wait("mixed", s)
                            for par in range(2):
                                rows = slice(par * S, (par + 1) * S)
                                last = nc.scalar.copy(values64(s)[rows, :, 0:half, par, :],
                                                      pair(s, 0)[rows, 0:SEQS * half * S]
                                                      .rearrange("p (b c d) -> p b c d", b=SEQS, c=half))
                            last.then_inc(signal["values_ready"], 1)
                piped(act, ph, body)
            return run

        def wide_vector(dve):
            def run(ph):
                heads = wide_heads(ph)
                tables = {F0_ATTN: rope_f[0], F1_ATTN: rope_f[1]}.get(ph)
                tables = part("const", "rope64") if tables is None else tables[:, :]
                tables = tables.rearrange("p (f n d) -> p f n d", f=2, n=2)

                def rotate(x, straight, swapped):
                    def table(f, lo, hi):
                        return tables[:, f, :, lo:hi].unsqueeze(2).broadcast_to([P, 2, 8, hi - lo])
                    nc.vector.tensor_tensor(straight, x, table(0, 0, 64), ALU.mult)
                    nc.vector.tensor_tensor(swapped[:, :, :, 0:32], x[:, :, :, 32:64], table(1, 0, 32), ALU.mult)
                    return nc.vector.tensor_tensor(swapped[:, :, :, 32:64], x[:, :, :, 0:32], table(1, 32, 64), ALU.mult)

                def blocks(x):
                    return x.rearrange("p (n h d) -> p n h d", n=2, h=8)

                def units(t):
                    for s in STREAMS:
                        t.wait("squares", s)
                        nc.vector.reduce_sum(sq_sum[s][:, :], rope_swapped(s).rearrange("p (h d) -> p h d", h=16),
                                             X_AXIS).then_inc(signal["norms_sq"], 1)
                        t.wait("norms_sq", s)
                        nc.vector.tensor_scalar(sq_floor[s][:, :], sq_sum[s][:, :], 1e-24, None, ALU.max)\
                            .then_inc(signal["norms_floor"], 1)
                    for s in STREAMS:
                        t.wait("norms_inv", s)
                        nc.vector.tensor_tensor(key_rotated(s).rearrange("p (h d) -> p h d", h=16),
                                                pair(s, 0).rearrange("p (h d) -> p h d", h=16),
                                                inv_norm[s][:, :].unsqueeze(2).broadcast_to([P, 16, 64]),
                                                ALU.mult).then_inc(signal["unit_ready"], 1)

                def unit_rotated(t, s):
                    t.wait("unit_ready", s)
                    rotate(blocks(key_rotated(s)), blocks(roped(s)), blocks(rope_swapped(s)))\
                        .then_inc(signal["q_parts"], 1)

                def row_sums(t):
                    for s in STREAMS:
                        t.wait("probs_ready", s)
                        nc.vector.reduce_sum(row_sum[s][:, 0:heads],
                                             probs(s)[:, 0:heads * S].rearrange("p (h k) -> p h k", h=heads), X_AXIS)\
                            .then_inc(signal["sums_ready"], 1)
                    for s in STREAMS:
                        t.wait("sums_ready", s)
                        nc.vector.reciprocal(inv_sum[s][:, 0:heads], row_sum[s][:, 0:heads])\
                            .then_inc(signal["sums_inverted"], 1)

                def normal_heads(t):
                    for s in STREAMS:
                        t.wait("mixed", s)
                        t.wait("sums_inverted", s)
                        nc.vector.tensor_tensor(
                            mixed_heads(s)[:, 0:heads * 64].rearrange("p (h d) -> p h d", h=heads),
                            pair(s, 2)[:, 0:heads * 64].rearrange("p (h d) -> p h d", h=heads),
                            inv_sum[s][:, 0:heads].unsqueeze(2).broadcast_to([P, heads, 64]), ALU.mult)\
                            .then_inc(signal["heads_normal"], 1)

                dve.wait_ge(tile_done, 2 + 16 * ph)

                def body(back, front):
                    if back:
                        softmax_vector(back, heads)
                    if ph == L1_ATTN:
                        if front:
                            for s in STREAMS:
                                front.wait("q_projected", s)
                                rotate(blocks(pair(s, 0)), blocks(roped(s)), blocks(rope_swapped(s)))\
                                    .then_inc(signal["q_parts"], 1)
                        if back:
                            row_sums(back)
                        if front:
                            for s in STREAMS:
                                front.wait("k_projected", s)
                                front.wait("q_rotated", s)
                                rotate(blocks(pair(s, 0)), blocks(key_rotated(s)), blocks(rope_swapped(s)))\
                                    .then_inc(signal["k_parts"], 1)
                        if back:
                            normal_heads(back)
                    else:
                        if front:
                            units(front)
                        if back:
                            row_sums(back)
                        if front:
                            unit_rotated(front, 0)
                        if back:
                            normal_heads(back)
                        if front:
                            unit_rotated(front, 1)
                    if back:
                        finish_vector(back, lambda s: bank(s, 3, 0, P), state if ph == L1_ATTN else inner,
                                      src=inner if ph == F1_ATTN else state)
                piped(dve, ph, body)
            return run

        def glu_pack(ph):
            return {F0_GLU: "fg0", F1_GLU: "fg1"}[ph]

        def normal_h(s):
            return heads_out[s]

        def gelu_out(s):
            return big(s, 0, 3 * P)

        def gated_out(s):
            return big(s, 1, 3 * P)

        def glu_pool(pool):
            def run(ph):
                pool.wait_ge(tile_done, 2 + 16 * ph)

                def body(back, front):
                    if front:
                        for s in STREAMS:
                            if back:
                                back.wait("x_turned", s)
                            stage_pool(front, s, inner)
                        for s in STREAMS:
                            front.wait("h_var", s)
                            nc.gpsimd.tensor_tensor(h_rstd[s][:, :], h_var[s][:, :], minus_half[:, 0:1], ALU.pow)\
                                .then_inc(signal["h_rstd"], 1)
                    if back and ph == F1_GLU:
                        for s in STREAMS:
                            norm_pool(back, s)
                piped(pool, ph, body)
            return run

        def glu_tensor(pe):
            def run(ph):
                w = glu_pack(ph)
                pe.wait_ge(loaded[w], 16)

                def body(back, front):
                    for s in STREAMS:
                        if back:
                            back.wait("hnT_ready", s)
                            for side in range(2):
                                first = 0 if side else HID
                                for n, k in enumerate(HCH):
                                    last = mm(ps[s][0:k, 1 + side, n * P:(n + 1) * P],
                                              part(w, "w1")[:, first + n * P:first + n * P + k], xT[s][:, :])
                            last.then_inc(signal["up_ready"], 1)
                        if front:
                            turn_x_pe(front, s)
                    if front:
                        for s in STREAMS:
                            front.wait("xT_ready", s)
                            nc.tensor.transpose(bank(s, 0, P, 2 * P), shT[s][:, :], ident)\
                                .then_inc(signal["h_turned"], 1)
                    if back:
                        for s in STREAMS:
                            back.wait("gated_ready", s)
                            back.wait_last(s)
                            for n, k in enumerate(HCH):
                                mm(bank(s, 3, 0, P), gated_out(s)[0:k, n * P:(n + 1) * P],
                                   part(w, "w2")[0:k, n * D:(n + 1) * D], start=(n == 0), stop=False)
                            mm(bank(s, 3, 0, P), ones_row[:, :], part("rows", w + "_b2"), start=False)\
                                .then_inc(signal["y_ready"], 1)
                    if front:
                        for s in STREAMS:
                            front.wait("h_normal", s)
                            nc.tensor.transpose(bank(s, 0, 2 * P, 3 * P), normal_h(s)[:, :], ident)\
                                .then_inc(signal["hn_turned"], 1)
                piped(pe, ph, body)
            return run

        def glu_scalar(act):
            def run(ph):
                w = glu_pack(ph)
                act.wait_ge(loaded[w], 16)

                def body(back, front):
                    for s in STREAMS:
                        if back:
                            back.wait("up_ready", s)
                            for n, k in enumerate(HCH):
                                last = nc.scalar.activation(gelu_out(s)[0:k, n * P:(n + 1) * P],
                                                            ps[s][0:k, 1, n * P:(n + 1) * P], ACT.Gelu,
                                                            bias=part(w, "b1")[0:k, 3 + n:4 + n])
                            last.then_inc(signal["gelu_ready"], 1)
                        if front:
                            turn_x_act(front, s, True)
                    if front:
                        for s in STREAMS:
                            front.wait("hn_turned", s)
                            nc.scalar.activation(xT[s][:, :], bank(s, 0, 2 * P, 3 * P), ACT.Identity,
                                                 bias=part(w, "ln")[:, 1:2], scale=part(w, "ln")[:, 0:1])\
                                .then_inc(signal["hnT_ready"], 1)
                piped(act, ph, body)
            return run

        def glu_vector(dve):
            def run(ph):
                w = glu_pack(ph)
                dve.wait_ge(loaded[w], 16)
                dve.wait_ge(tile_done, 2 + 16 * ph)

                def gated(t):
                    for s in STREAMS:
                        t.wait("gelu_ready", s)
                        for n, k in enumerate(HCH):
                            last = nc.vector.scalar_tensor_tensor(
                                out=gated_out(s)[0:k, n * P:(n + 1) * P], in0=ps[s][0:k, 2, n * P:(n + 1) * P],
                                scalar=part(w, "b1")[0:k, n:n + 1], in1=gelu_out(s)[0:k, n * P:(n + 1) * P],
                                op0=ALU.add, op1=ALU.mult)
                        last.then_inc(signal["gated_ready"], 1)

                def normal(t):
                    for s in STREAMS:
                        t.wait("h_turned", s)
                        nc.vector.bn_stats(h_stats[s][:, :], bank(s, 0, P, 2 * P)).then_inc(signal["h_stats"], 1)
                    for s in STREAMS:
                        t.wait("h_stats", s, alone=True)
                        nc.vector.bn_aggr(h_moments[s][:, :], h_stats[s][:, :]).then_inc(signal["h_mean"], 1)
                    for s in STREAMS:
                        t.wait("h_mean", s)
                        nc.vector.tensor_scalar(h_var[s][:, :], h_moments[s][:, 1:2], EPS, None, ALU.add)\
                            .then_inc(signal["h_var"], 1)
                    for s in STREAMS:
                        t.wait("h_rstd", s)
                        nc.vector.tensor_scalar(normal_h(s)[:, :], bank(s, 0, P, 2 * P), h_moments[s][:, 0:1],
                                                h_rstd[s][:, 0:1], ALU.subtract, ALU.mult)\
                            .then_inc(signal["h_normal"], 1)

                def body(back, front):
                    if back:
                        gated(back)
                    if front:
                        normal(front)
                    if back:
                        finish_vector(back, lambda s: bank(s, 3, 0, P), inner if ph == F0_GLU else state,
                                      outer=ph == F1_GLU, src=inner)
                piped(dve, ph, body)
            return run

        def both_qk(s):
            return big(s, 0, 512)

        def both_values(s):
            return big(s, 1, SEQS * D)

        def both_probs(s):
            return big(s, 2, 2 * S)

        def both_probsT(s):
            return big(s, 3, P)

        def both_mixed(s):
            return big(s, 4, 2 * D)

        def cross0_pool(pool):
            def run(ph):
                pool.wait_ge(ctx_loaded, 16)
                pool.wait_ge(tile_done, 2 + 16 * ph)

                def body(back, front):
                    if front:
                        for s in STREAMS:
                            if back:
                                back.wait("projected", s)
                            stage_pool(front, s, state, context=True)
                    if back:
                        for s in STREAMS:
                            norm_pool(back, s)
                piped(pool, ph, body)
            return run

        def cross0_tensor(pe):
            def run(ph):
                pe.wait_ge(loaded["x0"], 16)

                def project(t, s):
                    t.wait("xT_ready", s)
                    for n, (name, src) in enumerate((("wq_c", xT[s]), ("wk_s", cs[s]), ("wq_s", cs[s]),
                                                     ("wk_c", xT[s]))):
                        mm(bank(s, 1, n * P, (n + 1) * P), part("x0", name), src[:, :])
                    for way, (name, src) in enumerate((("wv_s", cs[s]), ("wv_c", xT[s]))):
                        for b in range(SEQS):
                            o = ps[s][way * S:(way + 1) * S, 0, (1 + b) * P:(2 + b) * P]
                            mm(o, src[:, b * S:(b + 1) * S], part("x0", name), stop=False)
                            last = mm(o, ones_row[:, 0:S], part("rows", "x0_b" + name[1:]), start=False)
                    last.then_inc(signal["projected"], 1)

                def body(back, front):
                    if back:
                        for s in STREAMS:
                            back.wait_last(s)
                            back.wait("qk_ready", s)
                            for way in range(2):
                                for b in range(SEQS):
                                    q, k = (both_qk(s)[:, (2 * way + n) * P + b * S:(2 * way + n) * P + (b + 1) * S]
                                            for n in range(2))
                                    last = mm(ps[s][b * S:(b + 1) * S, 2, way * S:(way + 1) * S], q, k)
                            last.then_inc(signal["scores_ready"], 1)
                    if front:
                        for s in STREAMS:
                            if back:
                                back.wait("values_ready", s)
                            turn_x_pe(front, s)
                        for s in STREAMS:
                            project(front, s)
                    if back:
                        for s in STREAMS:
                            back.wait("probs_ready", s)
                            nc.tensor.transpose(bank(s, 3, 0, P), both_probs(s), ident)\
                                .then_inc(signal["probs_turned"], 1)
                        for s in STREAMS:
                            back.wait("probsT_ready", s, alone=True)
                            for way in range(2):
                                rows = slice(way * S, (way + 1) * S)
                                for b in range(SEQS):
                                    last = mm(ps[s][b * S:(b + 1) * S, 2 + way, P:2 * P],
                                              both_probsT(s)[rows, b * S:(b + 1) * S],
                                              both_values(s)[rows, b * D:(b + 1) * D])
                            last.then_inc(signal["mixed"], 1)
                        for s in STREAMS:
                            back.wait("heads_normal", s)
                            for way in range(2):
                                last = nc.tensor.transpose(bank(s, 3, (2 + way) * P, (3 + way) * P),
                                                           both_mixed(s)[:, way * D:(way + 1) * D], ident)
                            last.then_inc(signal["heads_turned"], 1)
                        for s in STREAMS:
                            back.wait("headsT_ready", s)
                            for way in range(2):
                                mm(bank(s, 2, 2 * P, 3 * P), outT[s][:, way, :], part("x0", f"wg{way}"),
                                   start=(way == 0), stop=False)
                            mm(bank(s, 2, 2 * P, 3 * P), ones_row[:, :], part("rows", "x0_bg"), start=False)\
                                .then_inc(signal["y_ready"], 1)
                piped(pe, ph, body)
            return run

        def cross0_scalar(act):
            def run(ph):
                def body(back, front):
                    if front:
                        for s in STREAMS:
                            turn_x_act(front, s, False)
                    if back:
                        for s in STREAMS:
                            back.wait("scores_shifted", s)
                            nc.scalar.activation(both_probs(s), both_probs(s), ACT.Exp, scale=float(D) ** -0.5)\
                                .then_inc(signal["probs_ready"], 1)
                        for s in STREAMS:
                            back.wait("probs_turned", s)
                            nc.scalar.copy(both_probsT(s), bank(s, 3, 0, P)).then_inc(signal["probsT_ready"], 1)
                        for s in STREAMS:
                            back.wait("heads_turned", s)
                            nc.scalar.copy(outT[s][:, :, :].rearrange("p w t -> p (w t)"), bank(s, 3, 2 * P, 4 * P))\
                                .then_inc(signal["headsT_ready"], 1)
                    if front:
                        for s in STREAMS:
                            front.wait("projected", s)
                            if back:
                                back.wait("mixed", s)
                            nc.scalar.copy(both_values(s), bank(s, 0, P, 3 * P)).then_inc(signal["values_ready"], 1)
                    if back:
                        for s in STREAMS:
                            back.wait("y_ready", s)
                            nc.scalar.activation(gate[s][:, :], bank(s, 2, 2 * P, 3 * P), ACT.Exp, scale=-1.0)\
                                .then_inc(signal["gate_exp"], 1)
                piped(act, ph, body)
            return run

        def cross0_vector(dve):
            def run(ph):
                dve.wait_ge(loaded["x0"], 16)
                dve.wait_ge(tile_done, 2 + 16 * ph)

                def softmax(t):
                    for s in STREAMS:
                        t.wait("scores_ready", s)
                        sc = bank(s, 2, 0, 2 * S).rearrange("p (w k) -> p w k", w=2)
                        nc.vector.reduce_max(maxima[s][:, 0:2], sc, X_AXIS).then_inc(signal["max_ready"], 1)
                        t.wait("max_ready", s)
                        nc.vector.tensor_tensor(both_probs(s).rearrange("p (w k) -> p w k", w=2), sc,
                                                maxima[s][:, 0:2].unsqueeze(2).broadcast_to([P, 2, S]),
                                                ALU.subtract).then_inc(signal["scores_shifted"], 1)
                    for s in STREAMS:
                        t.wait("probs_ready", s)
                        nc.vector.reduce_sum(sq_sum[s][:, 0:2], both_probs(s).rearrange("p (w k) -> p w k", w=2),
                                             X_AXIS).then_inc(signal["sums_ready"], 1)
                    for s in STREAMS:
                        t.wait("sums_ready", s)
                        nc.vector.reciprocal(inv_sum[s][:, 0:2], sq_sum[s][:, 0:2]).then_inc(signal["sums_inverted"], 1)

                def mix_paths(t):
                    for s in STREAMS:
                        t.wait("mixed", s)
                        t.wait("sums_inverted", s)
                        nc.vector.tensor_tensor(both_mixed(s).rearrange("p (w d) -> p w d", w=2),
                                                ps[s][:, 2:4, P:2 * P],
                                                inv_sum[s][:, 0:2].unsqueeze(2).broadcast_to([P, 2, D]), ALU.mult)\
                            .then_inc(signal["heads_normal"], 1)
                    for s in STREAMS:
                        t.wait("heads_normal", s)
                        nc.vector.tensor_tensor(heads_out[s][:, :], both_mixed(s)[:, 0:D], both_mixed(s)[:, D:2 * D],
                                                ALU.subtract).then_inc(signal["paths_diff"], 1)
                    for s in STREAMS:
                        t.wait("gate_exp", s)
                        nc.vector.tensor_scalar(gate[s][:, :], gate[s][:, :], 1.0, None, ALU.add)\
                            .then_inc(signal["gate_den"], 1)
                    for s in STREAMS:
                        t.wait("gate_den", s)
                        nc.vector.reciprocal(gate[s][:, :], gate[s][:, :]).then_inc(signal["gate_ready"], 1)
                    for s in STREAMS:
                        t.wait("gate_ready", s)
                        t.wait("paths_diff", s)
                        nc.vector.tensor_tensor(heads_out[s][:, :], heads_out[s][:, :], gate[s][:, :], ALU.mult)\
                            .then_inc(signal["diff_gated"], 1)
                    for s in STREAMS:
                        t.wait("diff_gated", s)
                        nc.vector.tensor_tensor(heads_out[s][:, :], heads_out[s][:, :], both_mixed(s)[:, D:2 * D],
                                                ALU.add).then_inc(signal["y_mixed"], 1)

                def body(back, front):
                    if back:
                        softmax(back)
                    if front:
                        for s in STREAMS:
                            front.wait("projected", s)
                            nc.vector.tensor_tensor(both_qk(s).rearrange("p (n t) -> p n t", n=4),
                                                    bank(s, 1).rearrange("p (n t) -> p n t", n=4),
                                                    part("x0", "bias").unsqueeze(2).broadcast_to([P, 4, P]), ALU.add)\
                                .then_inc(signal["qk_ready"], 1)
                    if back:
                        mix_paths(back)
                        finish_vector(back, lambda s: heads_out[s][:, :], state, ready="y_mixed")
                piped(dve, ph, body)
            return run

        def carver():
            used = [0]

            def carve(cols, rows=P, dt=F32):
                words = cols if dt == F32 else -(-cols // (2 if dt == BF16 else 4))
                used[0] += words
                assert used[0] <= 2 * SCRATCH
                view = arena[0:rows, used[0] - words:used[0]]
                return view if dt == F32 else view.bitcast(dt)
            return carve

        def group_of(x, g):
            return x[:, ds(g * 4, 4), :].rearrange("p a n -> p (a n)")

        carve = carver()
        g_x, g_xT, g_acc = carve(GT), carve(GT), carve(GT)
        g_hidden = [carve(GT) for _ in range(2 * FCH)]
        g_onehotT = carve(GT, rows=EXP)
        g_eq, g_onehot = carve(4 * EXP), carve(4 * EXP)
        g_max, g_first = carve(4), carve(4)
        g_stats, g_moments, g_var, g_rstd = carve(24), carve(8), carve(4), carve(4)
        gs = moe_sems

        def group_stage_pool(pool, ph, use, g):
            pool.wait_ge(tile_done, 2 + 16 * ph + g * 4)
            nc.gpsimd.tensor_copy(g_x, group_of(state, g)).then_inc(gs["g_staged"], 1)

        def group_norm_pool(pool, use, g):
            pool.wait_ge(gs["g_var"], 4 * use + 1 + g)
            nc.gpsimd.tensor_tensor(g_rstd, g_var, minus_half[:, 0:4], ALU.pow).then_inc(gs["g_rstd"], 1)

        def group_norm_vector(dve, use, g):
            for tt in range(4):
                last = nc.vector.bn_stats(g_stats[:, 6 * tt:6 * tt + 6], g_acc[:, tt * D:(tt + 1) * D])
            last.then_inc(gs["g_stats"], 1)
            dve.wait_ge(gs["g_stats"], 4 * use + 1 + g)
            dve.nop(nofuse=True)
            for tt in range(4):
                last = nc.vector.bn_aggr(g_moments[:, 2 * tt:2 * tt + 2], g_stats[:, 6 * tt:6 * tt + 6])
            last.then_inc(gs["g_mean"], 1)
            dve.wait_ge(gs["g_mean"], 4 * use + 1 + g)
            nc.vector.tensor_scalar(g_var, g_moments.rearrange("p (t m) -> p t m", m=2)[:, :, 1:2]
                                    .rearrange("p t m -> p (t m)"), EPS, None, ALU.add).then_inc(gs["g_var"], 1)
            dve.wait_ge(gs["g_rstd"], 4 * use + 1 + g)
            for tt in range(4):
                nc.vector.tensor_scalar(state[:, ds(g * 4 + tt, 1), :].rearrange("p a n -> p (a n)"),
                                        g_acc[:, tt * D:(tt + 1) * D], g_moments[:, 2 * tt:2 * tt + 1],
                                        g_rstd[:, tt:tt + 1], ALU.subtract, ALU.mult).then_inc(tile_done, 1)

        def group_turn_tensor(pe, use, g, pack, bias):
            pe.wait_ge(gs["g_staged"], 4 * use + 1 + g)
            for tt in range(4):
                last = nc.tensor.transpose(bank(1, 2, tt * P, (tt + 1) * P), g_x[:, tt * D:(tt + 1) * D], ident)
            last.then_inc(gs["g_turned"], 1)
            pe.wait_ge(gs["g_xT"], 4 * use + 1 + g)
            for tt in range(4):
                o = bank(1, 3, tt * EXP, (tt + 1) * EXP)
                mm(o, g_xT[:, tt * P:(tt + 1) * P], part(pack, "wr"), stop=False)
                last = mm(o, ones_row[:, :], part("rows", bias), start=False)
            last.then_inc(gs["g_logits"], 1)

        def group_turn_scalar(act, use, g):
            act.wait_ge(gs["g_turned"], 4 * use + 1 + g)
            nc.scalar.copy(g_xT, bank(1, 2)).then_inc(gs["g_xT"], 1)

        def moe1_pool(ph):
            with pool_engine.Fori(0, GROUPS) as g:
                group_stage_pool(pool_engine, ph, 0, g)
                group_norm_pool(pool_engine, 0, g)

        def moe1_tensor(ph):
            pe = tensor_engine
            pe.wait_ge(loaded["moe1"], 16)

            def up(g, e):
                for f in range(FCH):
                    if e:
                        pe.wait_ge(gs["relu_done"], g * 32 + 4 * (e - 1) + f + 1)
                    mm(bank(0, f), part("moe1", "w1")[:, (e * FCH + f) * P:(e * FCH + f + 1) * P], g_xT)\
                        .then_inc(gs["h_done"], 1)

            def down(g, e):
                pe.wait_ge(gs["relu_done"], g * 32 + 4 * e + 4)
                if e >= 2:
                    pe.wait_ge(gs["acc_done"], g * 8 + e - 1)
                for tt in range(4):
                    for f in range(FCH):
                        last = mm(bank(1, e % 2, tt * D, (tt + 1) * D),
                                  g_hidden[(e % 2) * FCH + f][:, tt * P:(tt + 1) * P],
                                  part("moe1", "w2")[:, (e * FCH + f) * D:(e * FCH + f + 1) * D],
                                  start=(f == 0), stop=(f == FCH - 1))
                last.then_inc(gs["ye_done"], 1)

            with pe.Fori(0, GROUPS) as g:
                group_turn_tensor(pe, 0, g, "moe1", "m1_br")
                pe.wait_ge(gs["g_onehot"], 1 + g)
                for tt in range(4):
                    last = nc.tensor.transpose(ps[1][0:EXP, 3, tt * P:(tt + 1) * P],
                                               g_onehot[:, tt * EXP:(tt + 1) * EXP], ident)
                last.then_inc(gs["g_oneturned"], 1)
                up(g, 0)
                pe.wait_ge(gs["g_onehotT"], 1 + g)
                for tt in range(4):
                    last = mm(bank(1, 3, tt * D, (tt + 1) * D), g_onehotT[:, tt * P:(tt + 1) * P],
                              part("moe1", "b2")[0:EXP, :])
                last.then_inc(gs["g_bias"], 1)
                for e in range(EXP):
                    if e + 1 < EXP:
                        up(g, e + 1)
                    down(g, e)

        def moe1_scalar(ph):
            act = scalar_engine
            act.wait_ge(loaded["moe1"], 16)
            with act.Fori(0, GROUPS) as g:
                group_turn_scalar(act, 0, g)
                act.wait_ge(gs["g_oneturned"], 1 + g)
                nc.scalar.copy(g_onehotT, ps[1][0:EXP, 3, :]).then_inc(gs["g_onehotT"], 1)
                for e in range(EXP):
                    if e >= 2:
                        act.wait_ge(gs["ye_done"], g * 8 + e - 1)
                    for f in range(FCH):
                        act.wait_ge(gs["h_done"], g * 32 + 4 * e + f + 1)
                        nc.scalar.activation(g_hidden[(e % 2) * FCH + f], bank(0, f), ACT.Relu,
                                             bias=part("moe1", "b1")[:, e * FCH + f:e * FCH + f + 1])\
                            .then_inc(gs["relu_done"], 1)

        def moe1_vector(ph):
            dve = vector_engine

            def four(x):
                return x.rearrange("p (t e) -> p t e", t=4)

            def wide4(x):
                return x.unsqueeze(2).broadcast_to([P, 4, EXP])

            with dve.Fori(0, GROUPS) as g:
                dve.wait_ge(gs["g_logits"], 1 + g)
                logits = four(bank(1, 3, 0, 4 * EXP))
                nc.vector.reduce_max(g_max, logits, X_AXIS).then_inc(gs["g_top"], 1)
                dve.wait_ge(gs["g_top"], 1 + g)
                nc.vector.tensor_tensor(four(g_eq), logits, wide4(g_max), ALU.is_equal).then_inc(gs["g_eq"], 1)
                dve.wait_ge(gs["g_eq"], 1 + g)
                nc.vector.tensor_tensor(four(g_eq), four(g_eq), part("const", "falling").unsqueeze(1)
                                        .broadcast_to([P, 4, EXP]), ALU.mult).then_inc(gs["g_rank"], 1)
                dve.wait_ge(gs["g_rank"], 1 + g)
                nc.vector.reduce_max(g_first, four(g_eq), X_AXIS).then_inc(gs["g_first"], 1)
                dve.wait_ge(gs["g_first"], 1 + g)
                nc.vector.tensor_tensor(four(g_onehot), four(g_eq), wide4(g_first), ALU.is_equal)\
                    .then_inc(gs["g_onehot"], 1)
                dve.wait_ge(gs["g_bias"], 1 + g)
                nc.vector.tensor_tensor(g_acc, g_x, bank(1, 3), ALU.add).then_inc(gs["g_sum"], 1)
                dve.wait_ge(gs["g_sum"], 1 + g)
                for e in range(EXP):
                    dve.wait_ge(gs["ye_done"], g * 8 + e + 1)
                    if e:
                        dve.wait_ge(gs["acc_done"], g * 8 + e)
                    for tt in range(4):
                        cols = slice(tt * D, (tt + 1) * D)
                        last = nc.vector.scalar_tensor_tensor(
                            out=g_acc[:, cols], in0=bank(1, e % 2)[:, cols],
                            scalar=g_onehot[:, tt * EXP + e:tt * EXP + e + 1], in1=g_acc[:, cols],
                            op0=ALU.mult, op1=ALU.add)
                    last.then_inc(gs["acc_done"], 1)
                dve.wait_ge(gs["acc_done"], g * 8 + EXP)
                group_norm_vector(dve, 0, g)

        carve = carver()
        carve(2 * GT)
        NT8 = TILES * EXP
        logits_all, probs_all, rank_all, onehot_all, weighted_all, count_all = (carve(NT8) for _ in range(6))
        top_all, sum_all, inv_all, best_all, first_all, slot_all = (carve(TILES) for _ in range(6))
        onehot16, upto16, ones16 = carve(NT8, dt=BF16), carve(P, dt=BF16), carve(P, dt=BF16)
        zero512 = carve(512)
        at_slot = [carve(CAP) for _ in STREAMS]
        dispatch = [carve(EXP * CAP) for _ in STREAMS]
        dispatchT = [carve(EXP * P, rows=CAP) for _ in STREAMS]
        slotsT = carve(EXP * CAP)
        hidden80 = [carve(FCH * CAP) for _ in range(2)]
        expert_out = carve(EXP * D, rows=CAP)
        cm = gate_sems

        def moe2_pool(ph):
            pool = pool_engine
            for g in range(GROUPS):
                if g:
                    pool.wait_ge(cm["c_logits"], g)
                group_stage_pool(pool, ph, 1, 0) if g == 0 else \
                    nc.gpsimd.tensor_copy(g_x, state[:, 4 * g:4 * g + 4, :].rearrange("p a n -> p (a n)"))\
                    .then_inc(gs["g_staged"], 1)
            with pool.Fori(0, TURNS) as turn:
                for s in STREAMS:
                    pool.wait_ge(cm["c_dispatched"], turn * 2 + s + 1)
                    nc.gpsimd.tensor_copy(xs[s][:, :], state[:, ds(turn * 2 + s, 1), :].rearrange("p a n -> p (a n)"))\
                        .then_inc(cm["c_staged"], 1)
            pool.wait_ge(cm["c_dispatched"], 2 + TILES)

            def body(t):
                for s in STREAMS:
                    stage_pool(t, s, state)
                for s in STREAMS:
                    norm_pool(t, s)
            turns(pool, ph, body)

        def moe2_tensor(ph):
            pe = tensor_engine
            pe.wait_ge(loaded["moe2"], 16)
            pe.wait_ge(loaded["m2rows"], 16)
            for g in range(GROUPS):
                if g:
                    pe.wait_ge(cm["c_logits"], g)
                group_turn_tensor(pe, 1, g, "moe2", "m2_bg")
            pe.wait_ge(cm["c_onehot"], 1)
            count = bank(0, 2, 0, NT8)
            mm(count, upto16, onehot16, stop=False)
            for t in range(TILES - 1):
                last = mm(count[:, (t + 1) * EXP:], ones16, onehot16[:, t * EXP:(t + 1) * EXP].unsqueeze(1)
                          .broadcast_to([P, TILES - 1 - t, EXP]), start=False)
            last.then_inc(cm["c_counts"], 1)
            for half in range(2):
                last = mm(bank(0, half, 0, 320), zero512[:, 0:P], zero512[:, 0:320], stop=False)
            last.then_inc(cm["c_dispatched"], 2)
            with pe.Fori(0, TURNS) as turn:
                for s in STREAMS:
                    pe.wait_ge(cm["c_staged"], turn * 2 + s + 1)
                    pe.wait_ge(cm["c_made"], turn * 2 + s + 1)
                    for half in range(2):
                        last = mm(bank(0, half, 0, 320), xs[s][:, :], dispatch[s][:, half * 320:(half + 1) * 320],
                                  start=False)
                    last.then_inc(cm["c_dispatched"], 1)

            def up(e):
                if e >= 2:
                    pe.wait_ge(cm["c_gelu"], e - 1)
                for f in range(FCH):
                    last = mm(bank(0, 2 + e % 2, f * CAP, (f + 1) * CAP),
                              part("moe2", "w1")[:, (e * FCH + f) * P:(e * FCH + f + 1) * P],
                              slotsT[:, e * CAP:(e + 1) * CAP])
                last.then_inc(cm["c_up"], 1)

            pe.wait_ge(cm["c_slotsT"], 1)
            up(0)
            for e in range(EXP):
                if e + 1 < EXP:
                    up(e + 1)
                pe.wait_ge(cm["c_gelu"], e + 1)
                o = ps[1][0:CAP, e // 4, (e % 4) * D:(e % 4 + 1) * D]
                for f in range(FCH):
                    mm(o, hidden80[e % 2][:, f * CAP:(f + 1) * CAP],
                       part("moe2", "w2")[:, (e * FCH + f) * D:(e * FCH + f + 1) * D], start=(f == 0), stop=False)
                mm(o, ones_row[:, 0:CAP], part("m2rows", "b2")[:, e * D:(e + 1) * D], start=False)\
                    .then_inc(cm["c_down"], 1)
            pe.wait_ge(cm["c_out"], 1)

            def body(t):
                for s in STREAMS:
                    t.wait("dispatched_made", s)
                    for e in range(EXP):
                        last = nc.tensor.transpose(pair(s, 2)[0:CAP, e * P:(e + 1) * P],
                                                   dispatch[s][:, e * CAP:(e + 1) * CAP], ident)
                    last.then_inc(signal["dispatch_turned"], 1)
                for s in STREAMS:
                    t.wait("dispatchT_ready", s)
                    for e in range(EXP):
                        last = mm(bank(s, 0, 0, D), dispatchT[s][:, e * P:(e + 1) * P],
                                  expert_out[:, e * D:(e + 1) * D], start=(e == 0), stop=(e == EXP - 1))
                    last.then_inc(signal["y_ready"], 1)
            turns(pe, ph, body)

        def moe2_scalar(ph):
            act = scalar_engine
            act.wait_ge(loaded["moe2"], 16)
            for g in range(GROUPS):
                group_turn_scalar(act, 1, g)
            act.wait_ge(cm["c_shifted"], 1)
            nc.scalar.activation(probs_all, probs_all, ACT.Exp).then_inc(cm["c_exp"], 1)
            act.wait_ge(cm["c_dispatched"], 2 + TILES)
            nc.scalar.copy(slotsT.rearrange("p (a n) -> p a n", a=2), ps[0][:, 0:2, 0:320]).then_inc(cm["c_slotsT"], 1)
            for e in range(EXP):
                act.wait_ge(cm["c_up"], e + 1)
                if e >= 2:
                    act.wait_ge(cm["c_down"], e - 1)
                for f in range(FCH):
                    last = nc.scalar.activation(hidden80[e % 2][:, f * CAP:(f + 1) * CAP],
                                                bank(0, 2 + e % 2, f * CAP, (f + 1) * CAP), ACT.Gelu_apprx_tanh,
                                                bias=part("moe2", "b1")[:, e * FCH + f:e * FCH + f + 1])
                last.then_inc(cm["c_gelu"], 1)
            act.wait_ge(cm["c_down"], EXP)
            nc.scalar.copy(expert_out, pair(1, 0)[0:CAP, :]).then_inc(cm["c_out"], 1)

            def body(t):
                for s in STREAMS:
                    t.wait("dispatch_turned", s)
                    nc.scalar.copy(dispatchT[s], pair(s, 2)[0:CAP, :]).then_inc(signal["dispatchT_ready"], 1)
            turns(act, ph, body)

        def moe2_vector(ph):
            dve = vector_engine
            steps = [0]

            def then(ins):
                steps[0] += 1
                ins.then_inc(cm["c_chain"], 1)
                dve.wait_ge(cm["c_chain"], steps[0])

            def tiled(x):
                return x.rearrange("p (t e) -> p t e", t=TILES)

            def spread(x):
                return x.unsqueeze(2).broadcast_to([P, TILES, EXP])

            def make_dispatch(tile, s, count, chosen):
                nc.vector.tensor_tensor(at_slot[s], part("const", "slot"),
                                        slot_all[:, ds(tile, 1)].broadcast_to([P, CAP]), ALU.is_equal)\
                    .then_inc(cm["c_slot"], 1)
                dve.wait_ge(cm["c_slot"], count)
                return nc.vector.tensor_tensor(
                    dispatch[s].rearrange("p (e c) -> p e c", e=EXP),
                    chosen[:, ds(tile * EXP, EXP)].unsqueeze(2).broadcast_to([P, EXP, CAP]),
                    at_slot[s].unsqueeze(1).broadcast_to([P, EXP, CAP]), ALU.mult)

            for g in range(GROUPS):
                dve.wait_ge(gs["g_logits"], 4 + g + 1)
                nc.vector.tensor_copy(logits_all[:, g * 4 * EXP:(g + 1) * 4 * EXP], bank(1, 3, 0, 4 * EXP))\
                    .then_inc(cm["c_logits"], 1)
            dve.wait_ge(cm["c_logits"], GROUPS)
            nc.vector.memset(zero512, 0.0)
            nc.vector.memset(ones16, 1.0)
            nc.vector.tensor_copy(upto16, part("const", "upto"))
            then(nc.vector.reduce_max(top_all, tiled(logits_all), X_AXIS))
            nc.vector.tensor_tensor(tiled(probs_all), tiled(logits_all), spread(top_all), ALU.subtract)\
                .then_inc(cm["c_shifted"], 1)
            dve.wait_ge(cm["c_exp"], 1)
            then(nc.vector.reduce_sum(sum_all, tiled(probs_all), X_AXIS))
            then(nc.vector.reciprocal(inv_all, sum_all))
            then(nc.vector.tensor_tensor(tiled(probs_all), tiled(probs_all), spread(inv_all), ALU.mult))
            then(nc.vector.reduce_max(best_all, tiled(probs_all), X_AXIS))
            then(nc.vector.tensor_tensor(tiled(rank_all), tiled(probs_all), spread(best_all), ALU.is_equal))
            then(nc.vector.tensor_tensor(tiled(rank_all), tiled(rank_all), part("const", "falling").unsqueeze(1)
                                         .broadcast_to([P, TILES, EXP]), ALU.mult))
            then(nc.vector.reduce_max(first_all, tiled(rank_all), X_AXIS))
            then(nc.vector.tensor_tensor(tiled(onehot_all), tiled(rank_all), spread(first_all), ALU.is_equal))
            nc.vector.tensor_copy(onehot16, onehot_all).then_inc(cm["c_onehot"], 1)
            nc.vector.tensor_tensor(tiled(weighted_all), tiled(onehot_all), spread(best_all), ALU.mult)
            dve.wait_ge(cm["c_counts"], 1)
            then(nc.vector.tensor_tensor(count_all, bank(0, 2, 0, NT8), onehot_all, ALU.mult))
            then(nc.vector.reduce_sum(slot_all, tiled(count_all), X_AXIS))
            then(nc.vector.tensor_scalar(slot_all, slot_all, -1.0, None, ALU.add))
            with dve.Fori(0, TURNS) as turn:
                for s in STREAMS:
                    dve.wait_ge(cm["c_dispatched"], turn * 2 + s + 1)
                    make_dispatch(turn * 2 + s, s, turn * 2 + s + 1, onehot_all).then_inc(cm["c_made"], 1)
            dve.wait_ge(cm["c_dispatched"], 2 + TILES)

            def body(t):
                for s in STREAMS:
                    t.wait("x_staged", s)
                    make_dispatch(t.tile(s), s, t.v + TILES + s + 1, weighted_all)\
                        .then_inc(signal["dispatched_made"], 1)
                finish_vector(t, lambda s: bank(s, 0, 0, D), state)
            turns(dve, ph, body)

        carve = carver()
        carve(3 * GT)
        q_in, q_abs, q_bad = carve(GT), carve(GT), carve(GT)
        q_small8, q_large8 = carve(GT, dt=FP8), carve(GT, dt=FP8)
        q_large = carve(GT)
        q_mask = carve(GT, dt=U8)
        q_x = carve(GT, dt=BF16)
        q_xT = carve(GT, dt=BF16)
        x16, y16, sum16 = carve(GT, dt=BF16), carve(GT, dt=BF16), carve(GT, dt=BF16)
        f_stats_end = carve(GT * 8)
        q_w = carve(P, dt=BF16)
        w16 = carve(D, dt=BF16)
        bias8 = carve(D, dt=BF16)
        scale8, inv8, scale_both = carve(2), carve(2), carve(1)
        fs = fp_sems

        def fp8_pool(ph):
            with pool_engine.Fori(0, GROUPS) as g:
                group_stage_pool(pool_engine, ph, 2, g)
                group_norm_pool(pool_engine, 1, g)

        def fp8_tensor(ph):
            pe = tensor_engine
            turned = ps[0][:, 0, :].bitcast(BF16)
            with pe.Fori(0, GROUPS) as g:
                pe.wait_ge(fs["f_rounded"], g + 1)
                for tt in range(4):
                    last = nc.tensor.transpose(turned[:, tt * P:(tt + 1) * P], q_x[:, tt * P:(tt + 1) * P],
                                               ident16[:, :])
                last.then_inc(fs["f_turned"], 1)
                pe.wait_ge(fs["f_turned_copy"], g + 1)
                for tt in range(4):
                    last = mm(bank(0, 1, tt * D, (tt + 1) * D), q_xT[:, tt * P:(tt + 1) * P], q_w)
                last.then_inc(fs["f_y"], 1)

        def fp8_scalar(ph):
            act = scalar_engine
            with act.Fori(0, GROUPS) as g:
                act.wait_ge(fs["f_turned"], g + 1)
                nc.scalar.copy(q_xT, ps[0][:, 0, :].bitcast(BF16)[:, 0:GT]).then_inc(fs["f_turned_copy"], 1)

        def fp8_vector(ph):
            dve = vector_engine
            per_group = 13

            def rounded(n, src, scale, dst, then):
                small8, large8, large, mask = q_small8[:, 0:n], q_large8[:, 0:n], q_large[:, 0:n], q_mask[:, 0:n]
                x, size, bad = q_in[:, 0:n], q_abs[:, 0:n], q_bad[:, 0:n]
                then(nc.vector.tensor_scalar(x, src, scale, None, ALU.mult), alone=True)
                nc.vector.tensor_scalar(large8, x, 0.5, None, ALU.mult, saturate=False)
                nc.vector.tensor_tensor(size, x, x, ALU.mult)
                then(nc.vector.tensor_scalar(small8, x, 192.0, -192.0, ALU.min, ALU.max, saturate=False),
                     alone=True)
                nc.vector.tensor_copy(dst, small8)
                nc.vector.tensor_scalar(mask, size, 128.0 ** 2, None, ALU.is_ge)
                then(nc.vector.tensor_scalar(large, large8, 2.0, None, ALU.mult))
                then(nc.vector.tensor_tensor(size, large, large, ALU.mult))
                then(nc.vector.tensor_scalar(bad, size, 480.0 ** 2, 3e38, ALU.is_ge, ALU.mult))
                then(nc.vector.tensor_scalar(bad, bad, 10.0, None, ALU.mult))
                then(nc.vector.tensor_tensor(size, bad, bad, ALU.subtract))
                then(nc.vector.tensor_tensor(large, large, size, ALU.add), alone=True)
                then(nc.vector.copy_predicated(dst, mask, large))

            steps = [0]

            def once(ins, alone=False):
                steps[0] += 1
                ins.then_inc(fs["f_once"], 1)
                dve.wait_ge(fs["f_once"], steps[0])

            dve.wait_ge(loaded8, 3 * 16)
            once(nc.vector.tensor_tensor(scale_both, scale8[:, 0:1], scale8[:, 1:2], ALU.mult))
            once(nc.vector.reciprocal(inv8, scale8))
            rounded(P, w16, inv8[:, 1:2], q_w, once)
            with dve.Fori(0, GROUPS) as g:
                steps_in = [0]

                def then(ins, alone=False):
                    steps_in[0] += 1
                    ins.then_inc(fs["f_chain"], 1)
                    dve.wait_ge(fs["f_chain"], g * per_group + steps_in[0])
                    if alone:
                        dve.nop(nofuse=True)

                dve.wait_ge(gs["g_staged"], 4 + 4 + 1 + g)
                then(nc.vector.tensor_copy(x16, g_x))
                rounded(GT, x16, inv8[:, 0:1], q_x, then)
                nc.vector.nop().then_inc(fs["f_rounded"], 1)
                dve.wait_ge(fs["f_y"], g + 1)
                then(nc.vector.tensor_scalar(y16, bank(0, 1), scale_both[:, 0:1], None, ALU.mult))
                then(nc.vector.tensor_tensor(sum16.rearrange("p (t d) -> p t d", t=4),
                                             y16.rearrange("p (t d) -> p t d", t=4),
                                             bias8.unsqueeze(1).broadcast_to([P, 4, D]), ALU.add))
                then(nc.vector.tensor_tensor(g_acc, g_x, sum16, ALU.add))
                assert steps_in[0] == per_group
                group_norm_vector(dve, 1, g)

        pool_engine, tensor_engine, scalar_engine, vector_engine = nc.gpsimd, nc.tensor, nc.scalar, nc.vector
        block = ctx.enter_context(nc.Block())

        @block.sync
        def _(sp):
            sp.dma_start(weights["const"][:, :], packs["const"][0]).then_inc(loaded["const"], 16)
            sp.dma_start(weights["a0"][:, :], packs["a0"][0]).then_inc(loaded["a0"], 16)
            sp.dma_start(state[:, :, :], dram["x"].rearrange("(t p) d -> p t d", p=P)).then_inc(x_loaded, 16)
            sp.dma_start(weights["rows"][:, :], packs["rows"][0]).then_inc(loaded["rows"], 16)
            sp.dma_start(weights["scales"][:, :], packs["scales"][0][0].partition_broadcast(P))\
                .then_inc(loaded["scales"], 16)
            sp.dma_start(own_u8[:, :], dram["own"].unsqueeze(0).broadcast_to([SEQS, S, S])).then_inc(masks_loaded, 16)
            sp.dma_start(mask_int[:, :], dram["seq"].unsqueeze(0).broadcast_to([SEQS, S, S])).then_inc(masks_loaded, 16)
            for b in range(SEQS):
                sp.dma_start(pads_int[b * S:(b + 1) * S, :, :], dram["pads"][:, b, :].partition_broadcast(S))\
                    .then_inc(masks_loaded, 16)
            sp.dma_start(ctxT[:, :, :], dram["ctxT"].rearrange("d (t p) -> d t p", p=P)).then_inc(ctx_loaded, 16)
            for n in ("x0", "fa0", "fg0", "fa1", "fg1", "a1", "moe1"):
                sp.dma_start(weights[n][:, :], packs[n][0]).then_inc(loaded[n], 16)
            for early, done in (("x0", L0_CROSS), ("fa0", F0_ATTN), ("fa1", F1_ATTN)):
                if PHASES > done + 1:
                    sp.wait_ge(tile_done, 2 + 16 * (done + 1))
                    for n in LATE[early]:
                        sp.dma_start(weights[n], packs[n][0]).then_inc(loaded[n], 16)
                        sp.wait_ge(loaded[n], 16)
            if PHASES > F1_GLU + 1:
                sp.wait_ge(tile_done, 2 + 16 * (F1_GLU + 1))
                sp.dma_start(alibi16.rearrange("p n k -> p (n k)"), packs["alibi"][0]).then_inc(loaded["alibi"], 16)
                sp.wait_ge(loaded["alibi"], 16)
            if PHASES > L1_MOE + 1:
                sp.wait_ge(tile_done, 2 + 16 * (L1_MOE + 1))
                sp.dma_start(experts[:, :], packs["moe2"][0]).then_inc(loaded["moe2"], 16)
                sp.wait_ge(loaded["moe2"], 16)
            if PHASES > L3_CROSS + 1:
                sp.wait_ge(tile_done, 2 + 16 * (L3_CROSS + 1))
                sp.dma_start(w16, dram["kernel8"]).then_inc(loaded8, 16)
                sp.dma_start(bias8, dram["bias8"][0].partition_broadcast(P)).then_inc(loaded8, 16)
                sp.dma_start(scale8, dram["scales8"][0].partition_broadcast(P)).then_inc(loaded8, 16)
            sp.wait_ge(tile_done, 2 + 16 * PHASES)
            sp.dma_start(out.rearrange("(t p) d -> p t d", p=P), state[:, :, :]).then_inc(out_stored, 16)
            sp.wait_ge(out_stored, 16)

        @block.gpsimd
        def _(pool):
            pool.wait_ge(x_loaded, 16)
            pool.wait_ge(tables_ready, 1)
            narrow, wide, glu = narrow_pool(pool), wide_pool(pool), glu_pool(pool)
            cross0 = cross0_pool(pool)
            for run, ph in zip((narrow, cross0, wide, glu, wide, glu, wide, narrow, moe1_pool, narrow, narrow, moe2_pool,
                                narrow, narrow, fp8_pool), range(PHASES)):
                run(ph)

        @block.tensor
        def _(pe):
            pe.wait_ge(loaded["const"], 16)
            pe.wait_ge(loaded["rows"], 16)
            pe.wait_ge(tables_ready, 1)
            narrow, wide, glu = narrow_tensor(pe), wide_tensor(pe), glu_tensor(pe)
            cross0 = cross0_tensor(pe)
            for run, ph in zip((narrow, cross0, wide, glu, wide, glu, wide, narrow, moe1_tensor, narrow, narrow,
                                moe2_tensor, narrow, narrow, fp8_tensor), range(PHASES)):
                run(ph)

        @block.scalar
        def _(act):
            act.wait_ge(tables_ready, 1)
            narrow, wide, glu = narrow_scalar(act), wide_scalar(act), glu_scalar(act)
            cross0 = cross0_scalar(act)
            for run, ph in zip((narrow, cross0, wide, glu, wide, glu, wide, narrow, moe1_scalar, narrow, narrow,
                                moe2_scalar, narrow, narrow, fp8_scalar), range(PHASES)):
                run(ph)

        @block.vector
        def _(dve):
            dve.wait_ge(loaded["const"], 16)
            dve.wait_ge(loaded["scales"], 16)
            dve.wait_ge(masks_loaded, 4 * 16)
            nc.vector.memset(ones_row[:, :], 1.0)
            nc.vector.memset(minus_half[:, :], -0.5)
            for s in STREAMS:
                nc.vector.memset(values8[s][:, :, :, :, :].rearrange("p j b a d -> p (j b a d)"), 0.0)
                nc.vector.memset(shT[s][:, :], 0.0)
                nc.vector.memset(values64(s).rearrange("p b c a d -> p (b c a d)"), 0.0)
            nc.vector.tensor_copy(ident16[:, :], ident)
            for l in range(2):
                nc.vector.tensor_tensor(rope_f[l][:, :], part("const", "rope_xpos"),
                                        weights["scales"][:, l * 256:(l + 1) * 256], ALU.mult)
            nc.vector.tensor_scalar(own16[:, :], own_u8[:, :], 0.0, OFF, ALU.is_equal, ALU.mult)
            nc.vector.tensor_scalar(seq_add[:, :], mask_int[:, :], 0.0, OFF, ALU.is_equal, ALU.mult)
            nc.vector.tensor_scalar(pads16[:, :, :], pads_int, 0.0, OFF, ALU.is_equal, ALU.mult)
            nc.vector.tensor_copy(causal16[:, :], part("const", "causal")).then_inc(setup_done, 1)
            dve.wait_ge(setup_done, 1)
            nc.vector.tensor_tensor(pads16[:, :, :], pads16[:, :, :],
                                    seq_add[:, :].unsqueeze(1).broadcast_to([P, TILES, S]), ALU.min)
            for s in STREAMS:
                for par in range(2):
                    rows = slice(par * S, (par + 1) * S)
                    last = nc.vector.memset(values8[s][rows, :, :, par, HD8:HD8 + 1], 1.0)
            last.then_inc(tables_ready, 1)
            dve.wait_ge(tables_ready, 1)
            nc.vector.memset(stats[0][:, :], 0.0).then_inc(tile_done, 2)
            narrow, wide, glu = narrow_vector(dve), wide_vector(dve), glu_vector(dve)
            cross0 = cross0_vector(dve)
            for run, ph in zip((narrow, cross0, wide, glu, wide, glu, wide, narrow, moe1_vector, narrow, narrow,
                                moe2_vector, narrow, narrow, fp8_vector), range(PHASES)):
                run(ph)


def rope8_table():
    f = np.arange(P) % HD8
    theta = np.arange(S, dtype=np.float32)[None, :] / np.exp(
        2.0 * (f // 2).astype(np.float32) / HD8 * np.log(10000.0)).astype(np.float32)[:, None]
    cos, sin = np.cos(theta), np.sin(theta)
    sign = np.where(f % 2 == 0, -1.0, 1.0)[:, None]
    return np.concatenate([cos, sin * sign], axis=1).astype(np.float32)


def rope64_table(xpos):
    half = np.arange(0, 64, 2, dtype=np.float32)
    t = (np.arange(P) % S).astype(np.float32)
    freqs = np.tile(t[:, None] * (1.0 / 10000.0 ** (half / 64)).astype(np.float32)[None, :], (1, 2))
    cos, sin = np.cos(freqs), np.sin(freqs)
    sin = np.concatenate([-sin[:, :32], sin[:, 32:]], axis=1)
    scale = 1.0
    if xpos:
        base = (half + 0.4 * 64) / (1.4 * 64)
        scale = np.tile(base[None, :] ** ((t - S // 2) / 32.0)[:, None], (1, 2))
    return np.concatenate([cos * scale, cos / scale, sin * scale, sin / scale], axis=1).astype(np.float32)


def alibi_table():
    slopes = (2.0 ** -0.5) ** np.arange(1, H8 + 1)
    diff = np.arange(S)[None, :] - (np.arange(P) % S)[:, None]
    full = slopes[None, :, None] * diff[:, None, :] * np.sqrt(HD8)
    rest = full.reshape(P, H8 * S).astype(np.float32)
    parts = []
    for _ in range(3):
        top = (rest.view(np.uint32) & 0xFFFF0000).view(np.float32)
        parts.append(top)
        rest = rest - top
    future = np.broadcast_to((diff > 0)[:, None, :], (P, H8, S)).reshape(P, H8 * S)
    parts[0] = np.where(future, np.float32(NEG), parts[0]).astype(np.float32)
    return np.concatenate(parts, axis=1)


def constants():
    p = np.arange(P)
    causal = np.where(np.arange(S)[None, :] <= (p % S)[:, None], 0.0, NEG).astype(np.float32)
    own_head = (((p // HD8) % 8)[:, None] == np.arange(8)[None, :]).astype(np.float32)
    return {"ident": np.eye(P, dtype=np.float32), "causal": causal, "own_head": own_head, "rope8": rope8_table(),
            "rope64": rope64_table(False), "rope_xpos": rope64_table(True),
            "falling": np.tile(np.arange(EXP, 0, -1, dtype=np.float32), (P, 1)),
            "slot": np.tile(np.arange(CAP, dtype=np.float32), (P, 1)),
            "upto": (p[:, None] <= p[None, :]).astype(np.float32)}


def by_parity(w, heads, d):
    return w.reshape(w.shape[0], heads // 2, 2, d).transpose(0, 2, 1, 3).reshape(w.shape[0], heads * d)


def chunked(w):
    n = w.shape[0] // P
    return w.reshape(n, P, w.shape[1]).transpose(1, 0, 2).reshape(P, n * w.shape[1])


def rows_to(a, n):
    out = np.zeros((n,) + a.shape[1:], a.dtype)
    out[:a.shape[0]] = a
    return out


def layout(i):
    swap = np.arange(D) ^ 1

    def narrow(wq, wk, wv, wo=None, bq=None, bk=None, bv=None, rope=False):
        out = {"wq": wq.T, "wk": wk.T, "wv": by_parity(wv.T, H8, HD8)}
        if wo is not None:
            out["wo"] = wo.T
        if bq is not None:
            out["bv"] = bv[:, None]
            rows = [bq, bk]
            if rope:
                out |= {"wq_swapped": wq[swap].T, "wk_swapped": wk[swap].T}
                rows += [bq[swap], bk[swap]]
            out["bias"] = np.concatenate([np.stack([r[h * S:(h + 1) * S] for r in rows for h in range(2)], axis=1)] * 2)
        return out

    def named(prefix, names):
        return [i[prefix + n] for n in names.split()]

    packs = {"const": constants()}
    packs["a0"] = narrow(*named("L0_attn_", "wq wk wv wo bq bk bv"), rope=True)
    x0 = {n: i["L0_xattn_" + n] for n in ("Wq_c", "Wk_s", "Wv_s", "Wq_s", "Wk_c", "Wv_c", "Wg")}
    packs["rows"] = {"a0_bo": i["L0_attn_bo"], "x0_bv_s": i["L0_xattn_bv_s"], "x0_bv_c": i["L0_xattn_bv_c"],
                     "x0_bg": i["L0_xattn_bg"], "fg0_b2": i["L0_ffn_b2"][0], "fg1_b2": i["L0_ffn_b2"][1],
                     "x1_bo": i["L1_xattn_bo"], "a2_bo": i["L2_attn_bo"], "x2_bo": i["L2_xattn_bo"],
                     "a3_bo": i["L3_attn_bo"], "x3_bv": by_parity(i["L3_xattn_bv"][None], H8, HD8)[0],
                     "m1_br": i["L1_ffn_br"], "m2_bg": i["L2_ffn_gate_b"], }
    packs["rows"] = {n: a[None] for n, a in packs["rows"].items()}
    packs["m2rows"] = {"b2": i["L2_ffn_b2"].reshape(1, -1)}
    packs["scales"] = {}
    for l in range(2):
        q, k = i["L0_ffn_q_scale"][l], i["L0_ffn_k_scale"][l]
        for n, a in (("q", q), ("k", k), ("q_turned", np.roll(q, 32)), ("k_turned", np.roll(k, 32))):
            packs["scales"][f"{n}{l}"] = a[None]
    packs["x0"] = {"wq_c": x0["Wq_c"].T, "wk_s": x0["Wk_s"].T, "wq_s": x0["Wq_s"].T, "wk_c": x0["Wk_c"].T,
                   "wv_s": x0["Wv_s"].T, "wv_c": x0["Wv_c"].T, "wg0": x0["Wg"][:, :D].T, "wg1": x0["Wg"][:, D:].T,
                   "bias": np.stack(named("L0_xattn_", "bq_c bk_s bq_s bk_c"), axis=1)}
    for l in range(2):
        wqkv, wo = i["L0_ffn_wqkv"][l], i["L0_ffn_wo"][l]
        packs[f"fa{l}"] = {"wqk": wqkv[:, :1024], "wv": by_parity(by_parity(wqkv[:, 1024:], 8, 64), 8, 64),
                           "wo": chunked(by_parity(wo.T, 8, 64).T)}
        b1 = i["L0_ffn_b1"][l]
        w2 = rows_to(i["L0_ffn_w2"][l], 3 * P)
        packs[f"fg{l}"] = {"w1": i["L0_ffn_w1"][l], "w2": chunked(w2),
                           "b1": np.concatenate([rows_to(b1[:HID], 3 * P).reshape(3, P),
                                                 rows_to(b1[HID:], 3 * P).reshape(3, P)]).T,
                           "ln": np.stack([i["L0_ffn_ln_g"][l], i["L0_ffn_ln_b"][l]], axis=1)}
    packs["a1"] = {"wqk": i["L1_attn_wq"].T, "down": i["L1_attn_w_kv_down"].T,
                   "k_up": rows_to(i["L1_attn_w_k_up"].T, P), "wv": rows_to(by_parity(by_parity(i["L1_attn_w_v_up"].T, 16, 64), 16, 64), P),
                   "wo": chunked(by_parity(i["L1_attn_wo"], 16, 64).T)}
    packs["x1"] = narrow(*named("L1_xattn_", "Wq Wk Wv Wo"))
    packs["moe1"] = {"w1": i["L1_ffn_W1"].transpose(2, 0, 1).reshape(D, EXP * FF),
                     "w2": i["L1_ffn_W2"].reshape(EXP, D, FCH, P).transpose(3, 0, 2, 1).reshape(P, EXP * FCH * D),
                     "b1": i["L1_ffn_b1"].reshape(EXP * FCH, P).T, "wr": i["L1_ffn_Wr"].T,
                     "b2": rows_to(i["L1_ffn_b2"], P)}
    packs["a2"] = narrow(*named("L2_attn_", "Wq Wk Wv Wo bq bk bv"))
    packs["x2"] = narrow(*named("L2_xattn_", "Wq Wk Wv Wo bq bk bv"))
    packs["moe2"] = {"w1": i["L2_ffn_w1"].transpose(1, 0, 2).reshape(D, EXP * FF),
                     "w2": i["L2_ffn_w2"].reshape(EXP, FCH, P, D).transpose(2, 0, 1, 3).reshape(P, EXP * FCH * D),
                     "b1": i["L2_ffn_b1"].reshape(EXP * FCH, P).T, "wr": i["L2_ffn_gate_w"],
                     "pad": np.zeros((P, D), np.float32)}
    packs["a3"] = narrow(*named("L3_attn_", "Wq Wk Wv Wo bq bk bv"), rope=True)
    x3 = i["L3_xattn_Wv"]
    packs["x3"] = narrow(i["L3_xattn_Wq"], i["L3_xattn_Wk"], x3, None, *named("L3_xattn_", "bq bk bv"))
    packs["alibi"] = {"alibi": alibi_table()}
    return packs


def kernel(**inputs):
    import concourse.bacc as bacc
    from concourse.bass_utils import run_bass_kernel_spmd

    i = {n: np.asarray(a) for n, a in inputs.items()}
    nc = bacc.Bacc("TRN2", target_bir_lowering=False, num_devices=1)
    arrays, dram, packs = {}, {}, {}

    def declare(name, a):
        a = np.ascontiguousarray(a)
        arrays["in_" + name] = a
        return nc.dram_tensor("in_" + name, a.shape, mybir.dt.from_np(a.dtype), kind="ExternalInput").ap()

    for name, parts in layout(i).items():
        where, first = {}, 0
        for part, a in parts.items():
            where[part] = (first, a.shape[1])
            first += a.shape[1]
        whole = np.concatenate(list(parts.values()), axis=1)
        if name == "alibi":
            whole = whole.astype(i["L3_ffn_kernel"].dtype)
        packs[name] = (declare("pack_" + name, whole), where)
    dram["x"] = declare("x", i["x"].reshape(B * S, D))
    dram["ctxT"] = declare("ctxT", i["ctx_1024"].reshape(B * S, D).T)
    dram["own"] = declare("own", i["mask_1x1xSxS2_bk0"].reshape(S, S))
    dram["seq"] = declare("seq", i["mask_1x1xSxS2_ik0"].reshape(S, S))
    dram["pads"] = declare("pads", i["mask_Bx1x1xS2_ik0"].reshape(TILES, SEQS, S))
    dram["kernel8"] = declare("kernel8", i["L3_ffn_kernel"])
    dram["bias8"] = declare("bias8", i["L3_ffn_bias"][None])
    dram["scales8"] = declare("scales8", np.stack([i["L3_ffn_input_scale"], i["L3_ffn_kernel_scale"]], axis=1))
    out = nc.dram_tensor("out", (B * S, D), F32, kind="ExternalOutput").ap()
    program(nc, packs, dram, out)
    r = run_bass_kernel_spmd(nc, [arrays], core_ids=[0])
    return r.results[0]["out"].reshape(B, S, D)
```

```python
from contextlib import ExitStack

import numpy as np

import concourse.bass as bass
from concourse import mybir

F32 = mybir.dt.float32
BF16 = mybir.dt.bfloat16
FP8 = mybir.dt.float8e4
U8 = mybir.dt.uint8
I32 = mybir.dt.int32
ALU = mybir.AluOpType
ACT = mybir.ActivationFunctionType
X_AXIS = mybir.AxisListType.X
ds = bass.ds

P = 128
B, S, D = 32, 64, 128
TILES = B * S // P
SEQS = P // S
STREAMS = (0, 1)
TURNS = TILES // 2
GROUPS = TILES // 4
GT = 512
H8, HD8 = 16, 8
HID = 341
HCH = [128, 128, 85]
EXP = 8
FF = 512
FCH = FF // P
CAP = 80
EPS = 1e-5
NEG = -1e30
OFF = -1e20
BLOCKS = 12

(L0_ATTN, L0_CROSS, F0_ATTN, F0_GLU, F1_ATTN, F1_GLU, L1_ATTN, L1_CROSS, L1_MOE,
 L2_ATTN, L2_CROSS, L2_MOE, L3_ATTN, L3_CROSS, L3_FP8) = range(15)
PHASES = [1, 2, 6, 7, 8, 9, 10, 11, 12, 13, 14, 15][BLOCKS - 1]

NARROW = (L0_ATTN, L1_CROSS, L2_ATTN, L2_CROSS, L3_ATTN, L3_CROSS)
ROPED = (L0_ATTN, L3_ATTN)
GIVEN_CTX = (L0_CROSS, L1_CROSS, L2_CROSS, L3_CROSS)
PREFIX = {L0_ATTN: "a0", L0_CROSS: "x0", L1_CROSS: "x1", L2_ATTN: "a2", L2_CROSS: "x2", L3_ATTN: "a3", L3_CROSS: "x3"}
WIDE = (F0_ATTN, F1_ATTN, L1_ATTN)
GLU = (F0_GLU, F1_GLU)
ATTN = NARROW + WIDE
TILED = NARROW + WIDE + GLU + (L0_CROSS,)
FINISHED = TILED + (L2_MOE,)
KEPT = (F0_ATTN, F0_GLU, F1_ATTN)

HAS_OUT = tuple(p for p in ATTN if p != L3_CROSS) + (L0_CROSS,)

FIRES = {
    "x_staged": TILED, "x_turned": TILED, "xT_ready": TILED,
    "projected": NARROW + (L0_CROSS,), "rope_biased": ROPED, "rope_scaled": ROPED,
    "qk_ready": NARROW + (L0_CROSS,), "values_ready": ATTN + (L0_CROSS,), "keys_spread": NARROW,
    "scores_ready": ATTN + (L0_CROSS,), "max_ready": ATTN + (L0_CROSS,), "scores_shifted": ATTN + (L0_CROSS,),
    "probs_ready": ATTN + (L0_CROSS,), "probs_turned": ATTN + (L0_CROSS,), "probsT_ready": ATTN + (L0_CROSS,),
    "mixed": ATTN + (L0_CROSS,), "sums_inverted": ATTN + (L0_CROSS,), "heads_normal": ATTN + (L0_CROSS,),
    "heads_turned": HAS_OUT, "headsT_ready": HAS_OUT, "y_ready": tuple(p for p in FINISHED if p != L3_CROSS),
    "sums_ready": WIDE + (L0_CROSS,), "gate_exp": (L0_CROSS,), "gate_den": (L0_CROSS,), "gate_ready": (L0_CROSS,),
    "paths_diff": (L0_CROSS,), "diff_gated": (L0_CROSS,), "y_mixed": (L0_CROSS,),
    "q_projected": WIDE, "k_projected": (L1_ATTN,), "latent_projected": (L1_ATTN,), "latent_ready": (L1_ATTN,),
    "shift_kept": (F0_ATTN, F1_ATTN), "squares": (F0_ATTN, F1_ATTN), "norms_sq": (F0_ATTN, F1_ATTN), "norms_floor": (F0_ATTN, F1_ATTN),
    "norms_inv": (F0_ATTN, F1_ATTN), "unit_ready": (F0_ATTN, F1_ATTN),
    "dispatched_made": (L2_MOE,), "dispatch_turned": (L2_MOE,), "dispatchT_ready": (L2_MOE,),
    "q_parts": WIDE, "q_rotated": WIDE, "q_turned": WIDE, "qT_ready": WIDE,
    "k_parts": (L1_ATTN,), "k_rotated": (L1_ATTN,), "k_turned": (L1_ATTN,), "kT_ready": (L1_ATTN,),
    "v_projected": WIDE + NARROW + (L0_CROSS,),
    "h_turned": GLU, "h_stats": GLU, "h_mean": GLU, "h_var": GLU, "h_rstd": GLU, "h_normal": GLU,
    "hn_turned": GLU, "hnT_ready": GLU, "up_ready": GLU, "gelu_ready": GLU, "gated_ready": GLU,
    "outer_sum": (F1_GLU,), "res_sum": tuple(p for p in FINISHED if p not in KEPT),
    "ln_stats": tuple(p for p in FINISHED if p not in KEPT),
}
for _n in ("ln_mean", "ln_var", "ln_rstd"):
    FIRES[_n] = FIRES["ln_stats"]


STEPS = (("narrow", (L0_ATTN,)), ("cross0", (L0_CROSS,)), ("wide", (F0_ATTN,)), ("glu", (F0_GLU,)),
         ("wide", (F1_ATTN,)), ("glu", (F1_GLU,)), ("wide", (L1_ATTN,)), ("narrow", (L1_CROSS,)),
         ("moe1", (L1_MOE,)), ("narrow", (L2_ATTN, L2_CROSS)), ("moe2", (L2_MOE,)),
         ("narrow", (L3_ATTN, L3_CROSS)), ("fp8", (L3_FP8,)))


def run_phases(parts):
    for kind, phases in STEPS:
        phases = tuple(ph for ph in phases if ph < PHASES)
        if phases and kind == "narrow":
            parts[kind](phases)
        elif phases:
            parts[kind](phases[0])


def program(nc, packs, dram, out):
    with ExitStack() as ctx:
        def sb(name, shape, dt=F32):
            return ctx.enter_context(nc.sbuf_tensor(name, shape, dt))

        def sem(name):
            return ctx.enter_context(nc.semaphore(name))

        state = sb("state", [P, TILES, D])
        inner = sb("inner", [P, TILES, D])
        ctxT = sb("ctxT", [P, TILES, P])
        weights = {n: sb("w_" + n, [P if n == "scales" else ap.shape[0], ap.shape[1]]) for n, (ap, _) in packs.items()
                   if n not in ("moe1", "moe2", "alibi", "a2", "a3", "x3", "x1", "x2", "m2rows", "scales")}
        experts = sb("experts", [P, packs["moe1"][0].shape[1]])
        weights["moe1"] = weights["moe2"] = experts
        LATE = {"fa0": ("a2", "a3", "x3"), "fa1": ("x1", "x2"), "x0": ("m2rows",)}
        for early, late in LATE.items():
            first = 0
            for n in late:
                rows, cols = packs[n][0].shape
                weights[n] = weights[early][0:rows, first:first + cols]
                first += cols

        def part(pack, name):
            first, cols = packs[pack][1][name]
            return weights[pack][:, first:first + cols]

        ident = part("const", "ident")
        ones_row = sb("ones_row", [1, P])
        ident16 = sb("ident16", [P, P], BF16)
        causal16 = sb("causal16", [P, S], BF16)
        alibi16 = inner[:, 0:12, :].rearrange("p a n -> p (a n)").bitcast(BF16).rearrange("p (n k) -> p n k", n=3)
        rope_f = [sb(f"rope_f{l}", [P, 4 * 64]) for l in range(2)]
        seq_add = sb("seq_add", [P, S], BF16)
        own16 = sb("own16", [P, S], BF16)
        pads16 = sb("pads16", [P, TILES, S], BF16)
        pads_tile = [sb(f"pads_tile{s}", [P, S], BF16) for s in STREAMS]
        minus_half = sb("minus_half", [P, 16])

        BIG = 1024
        VALUES64 = SEQS * 8 * 2 * 64
        SCRATCH = 7 * BIG + VALUES64
        arena = sb("arena", [P, 2 * SCRATCH])

        pads_int = arena[:, 0:TILES * S].bitcast(I32).rearrange("p (t k) -> p t k", t=TILES)

        mask_int = arena[:, 1024:1024 + S].bitcast(I32)
        own_u8 = arena[:, 1088:1088 + S // 4].bitcast(U8)
        weights["scales"] = arena[:, 1152:1152 + 512]

        def big(s, k, cols=1024):
            at0 = s * SCRATCH + k * BIG
            return arena[:, at0:at0 + cols]

        xs = [sb(f"xs{s}", [P, D]) for s in STREAMS]
        cs = [sb(f"cs{s}", [P, P]) for s in STREAMS]
        xT = [sb(f"xT{s}", [P, P]) for s in STREAMS]
        shT = [sb(f"shT{s}", [P, P]) for s in STREAMS]
        total = [sb(f"total{s}", [P, D]) for s in STREAMS]
        stats = [sb(f"stats{s}", [P, 6]) for s in STREAMS]
        moments = [sb(f"moments{s}", [P, 2]) for s in STREAMS]
        var_eps = [sb(f"var_eps{s}", [P, 1]) for s in STREAMS]
        rstd = [sb(f"rstd{s}", [P, 1]) for s in STREAMS]
        maxima = [sb(f"maxima{s}", [P, 16]) for s in STREAMS]
        row_sum = [sb(f"row_sum{s}", [P, 16]) for s in STREAMS]
        inv_sum = [sb(f"inv_sum{s}", [P, 16]) for s in STREAMS]
        sq_sum = [sb(f"sq_sum{s}", [P, 16]) for s in STREAMS]
        sq_floor = [sb(f"sq_floor{s}", [P, 16]) for s in STREAMS]
        inv_norm = [sb(f"inv_norm{s}", [P, 16]) for s in STREAMS]
        values8 = [sb(f"values8_{s}", [P, H8 // 2, SEQS, 2, HD8 + 1]) for s in STREAMS]
        heads_out = [sb(f"heads_out{s}", [P, D]) for s in STREAMS]
        outT = [sb(f"outT{s}", [P, 2, P]) for s in STREAMS]
        gate = [sb(f"gate{s}", [P, D]) for s in STREAMS]
        latentT = [shT[s][0:S, :] for s in STREAMS]
        h_stats = [sb(f"h_stats{s}", [P, 6]) for s in STREAMS]
        h_moments = [sb(f"h_moments{s}", [P, 2]) for s in STREAMS]
        h_var = [sb(f"h_var{s}", [P, 1]) for s in STREAMS]
        h_rstd = [sb(f"h_rstd{s}", [P, 1]) for s in STREAMS]

        ps = [ctx.enter_context(nc.psum_tensor(f"ps{s}", [P, 4, 512], F32)) for s in STREAMS]

        def bank(s, b, lo=0, hi=512):
            return ps[s][:, b, lo:hi]

        def pair(s, b):
            return ps[s][:, b:b + 2, :].rearrange("p a n -> p (a n)")

        signal = {n: sem(n) for n in FIRES}
        tile_done = sem("tile_done")
        setup_done = sem("setup_done")
        x_loaded, ctx_loaded, out_stored = sem("x_loaded"), sem("ctx_loaded"), sem("out_stored")
        loaded = {n: sem("loaded_" + n) for n in packs}
        masks_loaded = sem("masks_loaded")
        tables_ready = sem("tables_ready")
        moe_sems = {n: sem(n) for n in (
            "g_staged", "g_turned", "g_xT", "g_logits", "g_top", "g_eq", "g_rank", "g_first", "g_onehot",
            "g_oneturned", "g_onehotT", "g_bias", "h_done", "relu_done", "ye_done", "acc_done",
            "g_sum", "g_stats", "g_mean", "g_var", "g_rstd")}
        gate_sems = {n: sem(n) for n in (
            "c_logits", "c_chain", "c_shifted", "c_exp", "c_onehot", "c_counts", "c_staged", "c_made", "c_slot",
            "c_dispatched", "c_slotsT", "c_up", "c_gelu", "c_down", "c_out")}
        fp_sems = {n: sem(n) for n in ("f_once", "f_chain", "f_back", "f_rounded", "f_turned", "f_turned_copy", "f_y")}
        loaded8 = sem("loaded8")

        def at(name, ph, v, s):
            fires = sorted(FIRES[name])
            return 16 * fires.index(ph) + s + 1 + v

        def tiles_done(ph, v, s):
            return 16 * ph + s + 1 + v

        class Turn:

            def __init__(self, eng, ph, turn):
                self.eng, self.ph = eng, ph
                self.v = turn * 2

            def wait(self, name, s, alone=False):
                self.eng.wait_ge(signal[name], at(name, self.ph, self.v, s))
                if alone:
                    self.eng.nop(nofuse=True)

            def tile(self, s):
                return self.v + s

            def wait_phase_before(self, s):
                self.eng.wait_ge(tile_done, tiles_done(self.ph - 1, self.v, s) + 2)
                self.eng.nop(nofuse=True)

            def wait_last(self, s):
                self.eng.wait_ge(tile_done, tiles_done(self.ph, self.v, s))

        def piped(eng, ph, body):
            body(None, Turn(eng, ph, 0))
            with eng.Fori(0, TURNS - 1) as turn:
                body(Turn(eng, ph, turn), Turn(eng, ph, turn + 1))
            body(Turn(eng, ph, TURNS - 1), None)

        def piped3(eng, phases, body):
            body(None, None, Turn(eng, phases[0], 0))
            body(None, Turn(eng, phases[0], 0), Turn(eng, phases[0], 1))
            for n, ph in enumerate(phases):
                with eng.Fori(0, TURNS - 2) as turn:
                    body(Turn(eng, ph, turn), Turn(eng, ph, turn + 1), Turn(eng, ph, turn + 2))
                following = [Turn(eng, phases[n + 1], k) if n + 1 < len(phases) else None for k in range(2)]
                body(Turn(eng, ph, TURNS - 2), Turn(eng, ph, TURNS - 1), following[0])
                body(Turn(eng, ph, TURNS - 1), following[0], following[1])

        def mm(o, lhsT, rhs, start=True, stop=True):
            return nc.tensor.matmul(o, lhsT, rhs, start=start, stop=stop, skip_group_check=True)

        def tile_of(x, t, s):
            return x[:, ds(t.tile(s), 1), :].rearrange("p a n -> p (a n)")

        def stage_pool(t, s, src, context=False):
            if context:
                nc.gpsimd.tensor_copy(cs[s][:, :], tile_of(ctxT, t, s))
            if t.ph == L3_CROSS:
                nc.gpsimd.tensor_copy(pads_tile[s][:, :], tile_of(pads16, t, s))
            nc.gpsimd.tensor_copy(xs[s][:, :], tile_of(src, t, s))\
                .then_inc(signal["x_staged"], 1)

        def turn_x_pe(t, s):
            t.wait("x_staged", s)
            nc.tensor.transpose(bank(s, 0, 0, P), xs[s][:, :], ident).then_inc(signal["x_turned"], 1)

        def turn_x_act(t, s, shifted):
            t.wait("x_turned", s)
            if not shifted:
                nc.scalar.copy(xT[s][:, :], bank(s, 0, 0, P)).then_inc(signal["xT_ready"], 1)
                return
            nc.scalar.copy(shT[s][0:S, :], ps[s][0:S, 0, 0:P])
            up = shT[s][S:P, :].rearrange("p (b t) -> p b t", b=SEQS)
            nc.scalar.copy(up[:, :, 1:S], ps[s][S:P, 0, 0:P].rearrange("p (b t) -> p b t", b=SEQS)[:, :, 0:S - 1])\
                .then_inc(signal["xT_ready"], 1)

        def norm_pool(t, s):
            t.wait("ln_var", s)
            nc.gpsimd.tensor_tensor(rstd[s][:, :], var_eps[s][:, :], minus_half[:, 0:1], ALU.pow)\
                .then_inc(signal["ln_rstd"], 1)

        def finish_vector(t, y, dst, ready="y_ready", outer=False, src=None):
            sum_vector(t, y, dst, ready, outer, src)
            if t.ph not in KEPT:
                norm_vector(t, dst)

        def sum_vector(t, y, dst, ready="y_ready", outer=False, src=None):
            kept = t.ph in KEPT
            src = src if src is not None else state
            for s in STREAMS:
                t.wait(ready, s)
                if kept:
                    nc.vector.tensor_tensor(tile_of(dst, t, s), tile_of(src, t, s), y(s), ALU.add)\
                        .then_inc(tile_done, 1)
                elif outer:
                    nc.vector.tensor_tensor(total[s][:, :], tile_of(src, t, s), y(s), ALU.add)\
                        .then_inc(signal["outer_sum"], 1)
                    t.wait("outer_sum", s)
                    nc.vector.tensor_tensor(total[s][:, :], total[s][:, :], tile_of(state, t, s), ALU.add)\
                        .then_inc(signal["res_sum"], 1)
                else:
                    nc.vector.tensor_tensor(total[s][:, :], tile_of(src, t, s), y(s), ALU.add)\
                        .then_inc(signal["res_sum"], 1)
            if kept:
                return
            for s in STREAMS:
                t.wait("res_sum", s)
                nc.vector.bn_stats(stats[s][:, :], total[s][:, :]).then_inc(signal["ln_stats"], 1)
            for s in STREAMS:
                t.wait("ln_stats", s, alone=True)
                nc.vector.bn_aggr(moments[s][:, :], stats[s][:, :]).then_inc(signal["ln_mean"], 1)
            for s in STREAMS:
                t.wait("ln_mean", s)
                nc.vector.tensor_scalar(var_eps[s][:, :], moments[s][:, 1:2], EPS, None, ALU.add)\
                    .then_inc(signal["ln_var"], 1)

        def norm_vector(t, dst):
            for s in STREAMS:
                t.wait("ln_rstd", s)
                nc.vector.tensor_scalar(tile_of(dst, t, s), total[s][:, :],
                                        moments[s][:, 0:1], rstd[s][:, 0:1], ALU.subtract, ALU.mult)\
                    .then_inc(tile_done, 1)

        def softmax_vector(t, heads, streams=STREAMS):
            half = heads // 2
            for s in streams:
                t.wait("scores_ready", s)
                sc = ps[s][:, 2:4, 0:half * S].rearrange("p a (h k) -> p a h k", h=half)
                mx = maxima[s][:, 0:heads].rearrange("p (a h) -> p a h", a=2)
                nc.vector.reduce_max(mx, sc, X_AXIS).then_inc(signal["max_ready"], 1)
                t.wait("max_ready", s)
                nc.vector.tensor_tensor(probs(s)[:, 0:heads * S].rearrange("p (a h k) -> p a h k", a=2, h=half), sc,
                                        mx.unsqueeze(3).broadcast_to([P, 2, half, S]),
                                        ALU.subtract).then_inc(signal["scores_shifted"], 1)

        def exp_scalar(t, heads, scale, streams=STREAMS):
            n = heads * S
            for s in streams:
                t.wait("scores_shifted", s)
                nc.scalar.activation(probs(s)[:, 0:n], probs(s)[:, 0:n], ACT.Exp, scale=scale)\
                    .then_inc(signal["probs_ready"], 1)

        def probsT_scalar(t, heads):
            n = heads * S
            for s in STREAMS:
                t.wait("probs_turned", s)
                nc.scalar.copy(probsT(s)[:, 0:n], pair(s, 2)[:, 0:n]).then_inc(signal["probsT_ready"], 1)

        def turn_probs_pe(t, heads, streams=STREAMS):
            for s in streams:
                t.wait("probs_ready", s)
                for j in range(heads // 2):
                    last = nc.tensor.transpose(pair(s, 2)[:, j * P:(j + 1) * P], probs(s)[:, j * P:(j + 1) * P], ident)
                last.then_inc(signal["probs_turned"], 1)

        def roped(s):
            return big(s, 0)

        def query8(s):
            return big(s, 1, 256).rearrange("p (h b t) -> p h b t", h=2, b=SEQS)

        def key8(s):
            return big(s, 1)[:, 256:384]

        def keys_wide(s):
            return big(s, 2)

        def probs(s):
            return big(s, 5)

        def probsT(s):
            return big(s, 6)

        VAL = H8 // 2 * 4 * (HD8 + 1)

        def has_out(ph):
            return ph != L3_CROSS

        def narrow_pool(pool):
            def run(phases):
                pool.wait_ge(ctx_loaded, 16)
                pool.wait_ge(tile_done, 2 + 16 * phases[0])
                for s in STREAMS:
                    nc.gpsimd.memset(big(s, 1, 256), 0.0)

                def spread_keys(t, s):
                    t.wait("qk_ready", s)
                    nc.gpsimd.tensor_tensor(
                        keys_wide(s).rearrange("p (a h t) -> p a h t", a=2, h=8),
                        key8(s).rearrange("p (a t) -> p a t", a=2).unsqueeze(2).broadcast_to([P, 2, 8, S]),
                        part("const", "own_head").unsqueeze(1).unsqueeze(3).broadcast_to([P, 2, 8, S]),
                        ALU.mult).then_inc(signal["keys_spread"], 1)

                def body(tail, middle, front):
                    if front:
                        for s in STREAMS:
                            if middle:
                                middle.wait("scores_ready", s)
                            if front.ph != phases[0]:
                                front.wait_phase_before(s)
                            stage_pool(front, s, state, context=front.ph in GIVEN_CTX)
                    for s in STREAMS:
                        if front:
                            spread_keys(front, s)
                        if s == 0 and tail:
                            for o in STREAMS:
                                norm_pool(tail, o)
                piped3(pool, phases, body)
            return run

        def narrow_tensor(pe):
            def run(phases):
                for ph in phases:
                    pe.wait_ge(loaded[PREFIX[ph]], 16)
                if L2_ATTN in phases:
                    pe.wait_ge(loaded["alibi"], 16)

                def project(t, s):
                    ph, w = t.ph, PREFIX[t.ph]
                    src = cs[s] if ph in GIVEN_CTX else xT[s]
                    kinds = [("wq", xT[s]), ("wk", src)]
                    if ph in ROPED:
                        kinds += [("wq_swapped", xT[s]), ("wk_swapped", src)]
                    for n, (name, rhs) in enumerate(kinds):
                        for half in range(2):
                            for b in range(SEQS):
                                last = mm(ps[s][b * S:(b + 1) * S, 0, n * P + half * S:n * P + (half + 1) * S],
                                          part(w, name)[:, half * S:(half + 1) * S], rhs[:, b * S:(b + 1) * S])
                    last.then_inc(signal["projected"], 1)

                def project_values(t, s):
                    ph, w = t.ph, PREFIX[t.ph]
                    src = cs[s] if ph in GIVEN_CTX else xT[s]
                    for par in range(2):
                        for b in range(SEQS):
                            o = ps[s][par * S:(par + 1) * S, 0, b * S:(b + 1) * S]
                            last = mm(o, src[:, b * S:(b + 1) * S], part(w, "wv")[:, par * S:(par + 1) * S],
                                      stop=has_out(ph))
                            if not has_out(ph):
                                last = mm(o, ones_row[:, 0:S], part("rows", "x3_bv")[:, par * S:(par + 1) * S],
                                          start=False)
                    last.then_inc(signal["v_projected"], 1)

                def score(t, s):
                    ph = t.ph
                    opened = ph != L2_CROSS
                    for half in range(2):
                        if ph == L2_ATTN:
                            for n in range(3):
                                mm(bank(s, 2 + half), ident16[:, :], alibi16[:, n, half * 512:(half + 1) * 512],
                                   start=(n == 0), stop=False)
                        elif opened:
                            table = {L1_CROSS: own16, L3_CROSS: pads_tile[s]}.get(ph, causal16)
                            mm(bank(s, 2 + half), ident16[:, :], table[:, :].unsqueeze(1).broadcast_to([P, 8, S]),
                               stop=False)
                        last = mm(bank(s, 2 + half), query8(s)[:, half, :, :].rearrange("p b t -> p (b t)"),
                                  keys_wide(s)[:, half * 512:(half + 1) * 512], start=not opened)
                    last.then_inc(signal["scores_ready"], 1)

                def mix(t, s):
                    t.wait("values_ready", s)
                    for j in range(H8 // 2):
                        last = mm(bank(s, 1, j * 36, (j + 1) * 36), probsT(s)[:, j * P:(j + 1) * P],
                                  values8[s][:, j, :, :, :].rearrange("p b a d -> p (b a d)"))
                    last.then_inc(signal["mixed"], 1)

                def body(tail, middle, front):
                    for s in STREAMS:
                        if tail:
                            tail.wait("probsT_ready", s)
                            mix(tail, s)
                        if middle:
                            middle.wait("keys_spread", s)
                            project_values(middle, s)
                            score(middle, s)
                    for s in STREAMS:
                        if front:
                            if middle:
                                middle.wait("values_ready", s)
                            turn_x_pe(front, s)
                        if tail and has_out(tail.ph):
                            tail.wait("heads_normal", s)
                            nc.tensor.transpose(bank(s, 1, VAL, VAL + P), heads_out[s][:, :], ident)\
                                .then_inc(signal["heads_turned"], 1)
                    for s in STREAMS:
                        if front:
                            front.wait("xT_ready", s)
                            project(front, s)
                        if middle:
                            turn_probs_pe(middle, H8, streams=(s,))
                        if s == 0 and tail and has_out(tail.ph):
                            for o in STREAMS:
                                tail.wait("headsT_ready", o)
                                mm(bank(o, 1, 0, P), outT[o][:, 0, :], part(PREFIX[tail.ph], "wo"), stop=False)
                                mm(bank(o, 1, 0, P), ones_row[:, :], part("rows", PREFIX[tail.ph] + "_bo"),
                                   start=False).then_inc(signal["y_ready"], 1)
                    if tail:
                        for s in STREAMS:
                            tail.wait("res_sum" if has_out(tail.ph) else "heads_normal", s)
                piped3(pe, phases, body)
            return run

        def narrow_scalar(act):
            def run(phases):
                for ph in phases:
                    act.wait_ge(loaded[PREFIX[ph]], 16)
                scale = float(1.0 / np.sqrt(np.float32(HD8)))

                def body(tail, middle, front):
                    if middle:
                        for s in STREAMS:
                            middle.wait("v_projected", s)
                            if tail:
                                tail.wait("mixed", s)
                            for par in range(2):
                                rows = slice(par * S, (par + 1) * S)
                                for b in range(SEQS):
                                    last = nc.scalar.copy(
                                        values8[s][rows, :, b, par, 0:HD8],
                                        ps[s][rows, 0, b * S:(b + 1) * S].rearrange("p (j d) -> p j d", j=8))
                            last.then_inc(signal["values_ready"], 1)
                    if middle:
                        exp_scalar(middle, H8, scale, streams=(0,))
                    if front:
                        for s in STREAMS:
                            turn_x_act(front, s, False)
                    if tail and has_out(tail.ph):
                        for s in STREAMS:
                            tail.wait("heads_turned", s)
                            if tail.ph == L1_CROSS:
                                nc.scalar.copy(outT[s][:, 0, :], bank(s, 1, VAL, VAL + P))\
                                    .then_inc(signal["headsT_ready"], 1)
                            else:
                                nc.scalar.activation(outT[s][:, 0, :], bank(s, 1, VAL, VAL + P), ACT.Identity,
                                                     bias=part(PREFIX[tail.ph], "bv")[:, 0:1]).then_inc(signal["headsT_ready"], 1)
                    if middle:
                        exp_scalar(middle, H8, scale, streams=(1,))
                        probsT_scalar(middle, H8)
                piped3(act, phases, body)
            return run

        def narrow_vector(dve):
            def run(phases):
                for ph in phases:
                    dve.wait_ge(loaded[PREFIX[ph]], 16)

                def spread_query(s, make):
                    for b in range(SEQS):
                        make(query8(s)[b * S:(b + 1) * S, :, b, :], slice(b * S, (b + 1) * S))

                def queries_and_keys(t, s):
                    ph, w = t.ph, PREFIX[t.ph]

                    def halves(x):
                        return x.rearrange("p (h t) -> p h t", h=2)
                    t.wait("projected", s)
                    if ph in ROPED:
                        n8 = roped(s)[:, 0:512].rearrange("p (n t) -> p n t", n=8)
                        nc.vector.tensor_tensor(n8, bank(s, 0).rearrange("p (n t) -> p n t", n=8),
                                                part(w, "bias").unsqueeze(2).broadcast_to([P, 8, S]), ALU.add)\
                            .then_inc(signal["rope_biased"], 1)
                        t.wait("rope_biased", s)
                        f4 = roped(s)[:, 0:512].rearrange("p (f n t) -> p f n t", f=2, n=4)
                        table = part("const", "rope8").rearrange("p (f t) -> p f t", f=2)
                        nc.vector.tensor_tensor(f4, f4, table.unsqueeze(2).broadcast_to([P, 2, 4, S]), ALU.mult)\
                            .then_inc(signal["rope_scaled"], 1)
                        t.wait("rope_scaled", s)
                        spread_query(s, lambda o, r: nc.vector.tensor_tensor(
                            o, halves(roped(s)[r, 0:128]), halves(roped(s)[r, 256:384]), ALU.add))
                        nc.vector.tensor_tensor(key8(s), roped(s)[:, 128:256], roped(s)[:, 384:512], ALU.add)\
                            .then_inc(signal["qk_ready"], 1)
                    elif ph == L1_CROSS:
                        spread_query(s, lambda o, r: nc.vector.tensor_copy(o, halves(ps[s][r, 0, 0:128])))
                        nc.vector.tensor_copy(key8(s), bank(s, 0, 128, 256)).then_inc(signal["qk_ready"], 1)
                    else:
                        spread_query(s, lambda o, r: nc.vector.tensor_tensor(
                            o, halves(ps[s][r, 0, 0:128]),
                            part(w, "bias")[r, 0:2].unsqueeze(2).broadcast_to([S, 2, S]), ALU.add))
                        nc.vector.tensor_tensor(halves(key8(s)), halves(bank(s, 0, 128, 256)),
                                                part(w, "bias")[:, 2:4].unsqueeze(2).broadcast_to([P, 2, S]), ALU.add)\
                            .then_inc(signal["qk_ready"], 1)

                dve.wait_ge(tile_done, 2 + 16 * phases[0])

                def normal_heads(t, s):
                    t.wait("mixed", s)
                    for b in range(SEQS):
                        rows = slice(b * S, (b + 1) * S)
                        sums = ps[s][rows, 1, 0:VAL].rearrange("p (j b n d) -> p j b n d", j=8, b=SEQS, n=2)
                        last = nc.vector.reciprocal(inv_sum[s][rows, :].rearrange("p (j n) -> p j n", n=2),
                                                    sums[:, :, b, :, HD8])
                    last.then_inc(signal["sums_inverted"], 1)
                    t.wait("sums_inverted", s)
                    for b in range(SEQS):
                        rows = slice(b * S, (b + 1) * S)
                        mix = ps[s][rows, 1, 0:VAL].rearrange("p (j b n d) -> p j b n d", j=8, b=SEQS, n=2)
                        last = nc.vector.tensor_tensor(
                            heads_out[s][rows, :].rearrange("p (j n d) -> p j n d", j=8, n=2),
                            mix[:, :, b, :, 0:HD8],
                            inv_sum[s][rows, :].rearrange("p (j n) -> p j n", n=2).unsqueeze(3)
                            .broadcast_to([S, 8, 2, HD8]), ALU.mult)
                    last.then_inc(signal["heads_normal"], 1)

                def body(tail, middle, front):
                    for s in STREAMS:
                        if tail:
                            normal_heads(tail, s)
                        if middle:
                            softmax_vector(middle, H8, streams=(s,))
                    if front:
                        queries_and_keys(front, 0)
                    if tail:
                        if tail.ph == L3_CROSS:
                            sum_vector(tail, lambda s: heads_out[s][:, :], state, ready="heads_normal")
                        else:
                            sum_vector(tail, lambda s: bank(s, 1, 0, P), state)
                    if front:
                        queries_and_keys(front, 1)
                    if tail:
                        norm_vector(tail, state)
                piped3(dve, phases, body)
            return run

        def wide_heads(ph):
            return 16 if ph == L1_ATTN else 8

        def wide_pack(ph):
            return {F0_ATTN: "fa0", F1_ATTN: "fa1", L1_ATTN: "a1"}[ph]

        def key_rotated(s):
            return big(s, 1)

        def rope_swapped(s):
            return big(s, 2)

        def queryT(s):
            return big(s, 3)

        def keyT(s):
            return big(s, 4)

        def mixed_heads(s):
            return probs(s)

        def headsT(s):
            return probsT(s)

        def values64(s):
            return big(s, 7, VALUES64).rearrange("p (b c a d) -> p b c a d", b=SEQS, c=8, a=2)

        def squares(s):
            return keyT(s)

        def shift_kept(s):
            return outT[s][:, 0, :]

        def wide_pool(pool):
            def run(ph):
                src = state if ph in (F0_ATTN, L1_ATTN) else inner
                pool.wait_ge(tile_done, 2 + 16 * ph)

                def both(back, front):
                    if front:
                        for s in STREAMS:
                            if back:
                                back.wait("x_turned", s)
                            stage_pool(front, s, src)
                        for s in STREAMS:
                            front.wait("q_parts", s)
                            nc.gpsimd.tensor_tensor(roped(s), roped(s), rope_swapped(s), ALU.add)\
                                .then_inc(signal["q_rotated"], 1)
                        for s in STREAMS:
                            front.wait("k_parts", s)
                            nc.gpsimd.tensor_tensor(key_rotated(s), key_rotated(s), rope_swapped(s), ALU.add)\
                                .then_inc(signal["k_rotated"], 1)
                    if back:
                        for s in STREAMS:
                            norm_pool(back, s)

                def three(tail, middle, front):
                    if middle:
                        for s in STREAMS:
                            middle.wait("norms_floor", s)
                            nc.gpsimd.tensor_tensor(inv_norm[s][:, :], sq_floor[s][:, :], minus_half[:, :],
                                                    ALU.pow).then_inc(signal["norms_inv"], 1)
                    if front:
                        for s in STREAMS:
                            if middle:
                                middle.wait("x_turned", s)
                            stage_pool(front, s, src)
                    if middle:
                        for s in STREAMS:
                            middle.wait("xT_ready", s, alone=True)
                            if tail:
                                tail.wait("v_projected", s, alone=True)
                            nc.gpsimd.tensor_copy(shift_kept(s), shT[s][:, :]).then_inc(signal["shift_kept"], 1)
                        for s in STREAMS:
                            middle.wait("q_parts", s)
                            nc.gpsimd.tensor_tensor(roped(s), roped(s), rope_swapped(s), ALU.add)\
                                .then_inc(signal["q_rotated"], 1)

                if ph == L1_ATTN:
                    piped(pool, ph, both)
                else:
                    piped3(pool, (ph,), three)
            return run

        def wide_tensor(pe):
            def run(ph):
                heads, w = wide_heads(ph), wide_pack(ph)
                half = heads // 2
                pe.wait_ge(loaded[w], 16)

                def score(t, s):
                    if ph == L1_ATTN:
                        t.wait_last(s)
                        t.wait("kT_ready", s)
                    else:
                        t.wait("values_ready", s)
                    for k in range(2):
                        mm(bank(s, 2 + k, 0, half * S), ident16[:, :],
                           causal16[:, :].unsqueeze(1).broadcast_to([P, half, S]), stop=False)
                    keys = keyT(s) if ph == L1_ATTN else queryT(s)[:, 512:1024]
                    for par in range(2):
                        rows = slice(par * S, (par + 1) * S)
                        for b in range(SEQS):
                            for j in range(half):
                                cols = slice(j * P + b * S, j * P + (b + 1) * S)
                                last = mm(ps[s][b * S:(b + 1) * S, 2 + par, j * S:(j + 1) * S],
                                          queryT(s)[rows, cols], keys[rows, cols], start=False)
                    last.then_inc(signal["scores_ready"], 1)

                def turn(t, s, source, done, first=0):
                    for j in range(8):
                        last = nc.tensor.transpose(pair(s, first)[:, j * P:(j + 1) * P], source[:, j * P:(j + 1) * P], ident)
                    last.then_inc(signal[done], 1)

                def project(t, s):
                    rows = xT[s] if ph == L1_ATTN else shT[s]
                    wq = part(w, "wqk")
                    for k in range(2):
                        last = mm(bank(s, k), rows[:, :], wq[:, k * 512:(k + 1) * 512])
                    last.then_inc(signal["q_projected"], 1)

                def project_values(t, s):
                    for par in range(2):
                        for b in range(SEQS):
                            o = pair(s, 0 if ph == L1_ATTN else 2)[par * S:(par + 1) * S, b * half * S:(b + 1) * half * S]
                            wv = part(w, "wv")[:, par * half * S:(par + 1) * half * S]
                            if ph == L1_ATTN:
                                last = mm(o, latentT[s][:, b * S:(b + 1) * S], wv[0:S, :])
                            else:
                                last = mm(o, shift_kept(s)[:, b * S:(b + 1) * S], wv)
                    last.then_inc(signal["v_projected"], 1)

                def mix(t, s):
                    t.wait("probsT_ready", s)
                    for c in range(half):
                        for b in range(SEQS):
                            last = mm(pair(s, 2)[b * S:(b + 1) * S, c * P:(c + 1) * P],
                                      probsT(s)[:, c * P + b * S:c * P + (b + 1) * S],
                                      values64(s)[:, b, c, :, :].rearrange("p a d -> p (a d)"))
                    last.then_inc(signal["mixed"], 1)

                def turn_heads(t, s):
                    t.wait("heads_normal", s)
                    for j in range(half):
                        last = nc.tensor.transpose(pair(s, 2)[:, j * P:(j + 1) * P],
                                                   mixed_heads(s)[:, j * P:(j + 1) * P], ident)
                    last.then_inc(signal["heads_turned"], 1)

                def output(t, s):
                    t.wait("headsT_ready", s)
                    for j in range(half):
                        last = mm(bank(s, 3, 0, P), headsT(s)[:, j * P:(j + 1) * P],
                                  part(w, "wo")[:, j * D:(j + 1) * D], start=(j == 0), stop=(j == half - 1))
                    last.then_inc(signal["y_ready"], 1)

                def both(back, front):
                    for s in STREAMS:
                        if back:
                            score(back, s)
                        if front:
                            if back:
                                back.wait("values_ready", s)
                            turn_x_pe(front, s)
                    if front:
                        for s in STREAMS:
                            front.wait("xT_ready", s)
                            mm(ps[s][0:S, 1, 0:P], part(w, "down"), xT[s][:, :])\
                                .then_inc(signal["latent_projected"], 1)
                        for s in STREAMS:
                            front.wait("latent_ready", s)
                            project(front, s)
                    if back:
                        turn_probs_pe(back, heads)
                    if front:
                        for s in STREAMS:
                            front.wait("q_parts", s)
                            for k in range(2):
                                last = mm(bank(s, k), latentT[s], part(w, "k_up")[0:S, k * 512:(k + 1) * 512])
                            last.then_inc(signal["k_projected"], 1)
                    if back:
                        for s in STREAMS:
                            mix(back, s)
                    if front:
                        for s in STREAMS:
                            front.wait("q_rotated", s)
                            front.wait("k_parts", s)
                            turn(front, s, roped(s), "q_turned")
                    if back:
                        for s in STREAMS:
                            turn_heads(back, s)
                        for s in STREAMS:
                            output(back, s)
                    if front:
                        for s in STREAMS:
                            front.wait("k_rotated", s)
                            front.wait("qT_ready", s)
                            turn(front, s, key_rotated(s), "k_turned")
                        for s in STREAMS:
                            front.wait("kT_ready", s, alone=True)
                            project_values(front, s)

                def three(tail, middle, front):
                    if tail:
                        for s in STREAMS:
                            tail.wait_last(s)
                            tail.wait("q_rotated", s)
                            turn(tail, s, roped(s), "q_turned", first=2)
                        for s in STREAMS:
                            tail.wait("shift_kept", s, alone=True)
                            tail.wait("qT_ready", s, alone=True)
                            project_values(tail, s)
                        for s in STREAMS:
                            score(tail, s)
                    if front:
                        for s in STREAMS:
                            if middle:
                                middle.wait("unit_ready", s)
                            turn_x_pe(front, s)
                        for s in STREAMS:
                            front.wait("xT_ready", s)
                            project(front, s)
                    if tail:
                        turn_probs_pe(tail, heads)
                        for s in STREAMS:
                            mix(tail, s)
                    if tail:
                        for s in STREAMS:
                            turn_heads(tail, s)
                        for s in STREAMS:
                            output(tail, s)

                if ph == L1_ATTN:
                    piped(pe, ph, both)
                else:
                    piped3(pe, (ph,), three)
            return run

        def wide_scalar(act):
            def run(ph):
                heads = wide_heads(ph)
                half = heads // 2

                def queries(t, first):
                    for s in STREAMS:
                        t.wait("q_turned", s)
                        nc.scalar.copy(queryT(s), pair(s, first)).then_inc(signal["qT_ready"], 1)

                def values(t, first):
                    for s in STREAMS:
                        t.wait("v_projected", s)
                        for par in range(2):
                            rows = slice(par * S, (par + 1) * S)
                            last = nc.scalar.copy(values64(s)[rows, :, 0:half, par, :],
                                                  pair(s, first)[rows, 0:SEQS * half * S]
                                                  .rearrange("p (b c d) -> p b c d", b=SEQS, c=half))
                        last.then_inc(signal["values_ready"], 1)

                def heads_turned(t):
                    for s in STREAMS:
                        t.wait("heads_turned", s)
                        nc.scalar.copy(headsT(s)[:, 0:half * P], pair(s, 2)[:, 0:half * P])\
                            .then_inc(signal["headsT_ready"], 1)

                def both(back, front):
                    if front:
                        for s in STREAMS:
                            turn_x_act(front, s, shifted=False)
                        for s in STREAMS:
                            front.wait("latent_projected", s)
                            nc.scalar.copy(latentT[s], ps[s][0:S, 1, 0:P]).then_inc(signal["latent_ready"], 1)
                    if back:
                        exp_scalar(back, heads, 0.125)
                        probsT_scalar(back, heads)
                    if front:
                        queries(front, 0)
                    if back:
                        heads_turned(back)
                    if front:
                        for s in STREAMS:
                            front.wait("k_turned", s)
                            nc.scalar.copy(keyT(s), pair(s, 0)).then_inc(signal["kT_ready"], 1)
                        if back:
                            for s in STREAMS:
                                back.wait("mixed", s)
                        values(front, 0)

                def three(tail, middle, front):
                    if tail:
                        queries(tail, 2)
                        values(tail, 2)
                    if front:
                        for s in STREAMS:
                            if middle:
                                middle.wait("shift_kept", s)
                            turn_x_act(front, s, shifted=True)
                    if tail:
                        exp_scalar(tail, heads, 8.0)
                    if front:
                        for s in STREAMS:
                            if middle:
                                middle.wait("norms_sq", s)
                            front.wait("q_projected", s)
                            nc.scalar.activation(squares(s), pair(s, 0), ACT.Square).then_inc(signal["squares"], 1)
                    if tail:
                        probsT_scalar(tail, heads)
                    if tail:
                        heads_turned(tail)

                if ph == L1_ATTN:
                    piped(act, ph, both)
                else:
                    piped3(act, (ph,), three)
            return run

        def wide_vector(dve):
            def run(ph):
                heads = wide_heads(ph)
                tables = {F0_ATTN: rope_f[0], F1_ATTN: rope_f[1]}.get(ph)
                tables = part("const", "rope64") if tables is None else tables[:, :]
                tables = tables.rearrange("p (f n d) -> p f n d", f=2, n=2)

                def rotate(x, straight, swapped):
                    def table(f, lo, hi):
                        return tables[:, f, :, lo:hi].unsqueeze(2).broadcast_to([P, 2, 8, hi - lo])
                    nc.vector.tensor_tensor(straight, x, table(0, 0, 64), ALU.mult)
                    nc.vector.tensor_tensor(swapped[:, :, :, 0:32], x[:, :, :, 32:64], table(1, 0, 32), ALU.mult)
                    return nc.vector.tensor_tensor(swapped[:, :, :, 32:64], x[:, :, :, 0:32], table(1, 32, 64), ALU.mult)

                def blocks(x):
                    return x.rearrange("p (n h d) -> p n h d", n=2, h=8)

                def units(t):
                    for s in STREAMS:
                        t.wait("squares", s)
                        nc.vector.reduce_sum(sq_sum[s][:, :], squares(s).rearrange("p (h d) -> p h d", h=16),
                                             X_AXIS).then_inc(signal["norms_sq"], 1)
                        t.wait("norms_sq", s)
                        nc.vector.tensor_scalar(sq_floor[s][:, :], sq_sum[s][:, :], 1e-24, None, ALU.max)\
                            .then_inc(signal["norms_floor"], 1)
                    for s in STREAMS:
                        t.wait("norms_inv", s)
                        nc.vector.tensor_tensor(key_rotated(s).rearrange("p (h d) -> p h d", h=16),
                                                pair(s, 0).rearrange("p (h d) -> p h d", h=16),
                                                inv_norm[s][:, :].unsqueeze(2).broadcast_to([P, 16, 64]),
                                                ALU.mult).then_inc(signal["unit_ready"], 1)

                def unit_rotated(t, s, last):
                    t.wait("unit_ready", s)
                    if last:
                        last.wait("q_turned", s)
                    rotate(blocks(key_rotated(s)), blocks(roped(s)), blocks(rope_swapped(s)))\
                        .then_inc(signal["q_parts"], 1)

                def row_sums(t):
                    for s in STREAMS:
                        t.wait("probs_ready", s)
                        nc.vector.reduce_sum(row_sum[s][:, 0:heads],
                                             probs(s)[:, 0:heads * S].rearrange("p (h k) -> p h k", h=heads), X_AXIS)\
                            .then_inc(signal["sums_ready"], 1)
                    for s in STREAMS:
                        t.wait("sums_ready", s)
                        nc.vector.reciprocal(inv_sum[s][:, 0:heads], row_sum[s][:, 0:heads])\
                            .then_inc(signal["sums_inverted"], 1)

                def normal_heads(t):
                    for s in STREAMS:
                        t.wait("mixed", s)
                        t.wait("sums_inverted", s)
                        nc.vector.tensor_tensor(
                            mixed_heads(s)[:, 0:heads * 64].rearrange("p (h d) -> p h d", h=heads),
                            pair(s, 2)[:, 0:heads * 64].rearrange("p (h d) -> p h d", h=heads),
                            inv_sum[s][:, 0:heads].unsqueeze(2).broadcast_to([P, heads, 64]), ALU.mult)\
                            .then_inc(signal["heads_normal"], 1)

                dve.wait_ge(tile_done, 2 + 16 * ph)

                def finish(t):
                    finish_vector(t, lambda s: bank(s, 3, 0, P), state if ph == L1_ATTN else inner,
                                  src=inner if ph == F1_ATTN else state)

                def both(back, front):
                    if back:
                        softmax_vector(back, heads)
                    if front:
                        for s in STREAMS:
                            front.wait("q_projected", s)
                            rotate(blocks(pair(s, 0)), blocks(roped(s)), blocks(rope_swapped(s)))\
                                .then_inc(signal["q_parts"], 1)
                    if back:
                        row_sums(back)
                    if front:
                        for s in STREAMS:
                            front.wait("k_projected", s)
                            front.wait("q_rotated", s)
                            rotate(blocks(pair(s, 0)), blocks(key_rotated(s)), blocks(rope_swapped(s)))\
                                .then_inc(signal["k_parts"], 1)
                    if back:
                        normal_heads(back)
                        finish(back)

                def three(tail, middle, front):
                    if middle:
                        units(middle)
                    if tail:
                        softmax_vector(tail, heads)
                    if middle:
                        unit_rotated(middle, 0, tail)
                    if tail:
                        row_sums(tail)
                        normal_heads(tail)
                    if middle:
                        unit_rotated(middle, 1, tail)
                    if tail:
                        finish(tail)

                if ph == L1_ATTN:
                    piped(dve, ph, both)
                else:
                    piped3(dve, (ph,), three)
            return run

        def glu_pack(ph):
            return {F0_GLU: "fg0", F1_GLU: "fg1"}[ph]

        def normal_h(s):
            return heads_out[s]

        def gelu_out(s):
            return big(s, 0, 3 * P)

        def gated_out(s):
            return big(s, 1, 3 * P)

        def glu_pool(pool):
            def run(ph):
                pool.wait_ge(tile_done, 2 + 16 * ph)

                def body(back, front):
                    if front:
                        for s in STREAMS:
                            if back:
                                back.wait("x_turned", s)
                            stage_pool(front, s, inner)
                        for s in STREAMS:
                            front.wait("h_var", s)
                            nc.gpsimd.tensor_tensor(h_rstd[s][:, :], h_var[s][:, :], minus_half[:, 0:1], ALU.pow)\
                                .then_inc(signal["h_rstd"], 1)
                    if back and ph == F1_GLU:
                        for s in STREAMS:
                            norm_pool(back, s)
                piped(pool, ph, body)
            return run

        def glu_tensor(pe):
            def run(ph):
                w = glu_pack(ph)
                pe.wait_ge(loaded[w], 16)

                def body(back, front):
                    for s in STREAMS:
                        if back:
                            back.wait("hnT_ready", s)
                            for side in range(2):
                                first = 0 if side else HID
                                for n, k in enumerate(HCH):
                                    last = mm(ps[s][0:k, 1 + side, n * P:(n + 1) * P],
                                              part(w, "w1")[:, first + n * P:first + n * P + k], xT[s][:, :])
                            last.then_inc(signal["up_ready"], 1)
                        if front:
                            turn_x_pe(front, s)
                    if front:
                        for s in STREAMS:
                            front.wait("xT_ready", s)
                            nc.tensor.transpose(bank(s, 0, P, 2 * P), shT[s][:, :], ident)\
                                .then_inc(signal["h_turned"], 1)
                    if back:
                        for s in STREAMS:
                            back.wait("gated_ready", s)
                            back.wait_last(s)
                            for n, k in enumerate(HCH):
                                mm(bank(s, 3, 0, P), gated_out(s)[0:k, n * P:(n + 1) * P],
                                   part(w, "w2")[0:k, n * D:(n + 1) * D], start=(n == 0), stop=False)
                            mm(bank(s, 3, 0, P), ones_row[:, :], part("rows", w + "_b2"), start=False)\
                                .then_inc(signal["y_ready"], 1)
                    if front:
                        for s in STREAMS:
                            front.wait("h_normal", s)
                            nc.tensor.transpose(bank(s, 0, 2 * P, 3 * P), normal_h(s)[:, :], ident)\
                                .then_inc(signal["hn_turned"], 1)
                piped(pe, ph, body)
            return run

        def glu_scalar(act):
            def run(ph):
                w = glu_pack(ph)
                act.wait_ge(loaded[w], 16)

                def body(back, front):
                    for s in STREAMS:
                        if back:
                            back.wait("up_ready", s)
                            for n, k in enumerate(HCH):
                                last = nc.scalar.activation(gelu_out(s)[0:k, n * P:(n + 1) * P],
                                                            ps[s][0:k, 1, n * P:(n + 1) * P], ACT.Gelu,
                                                            bias=part(w, "b1")[0:k, 3 + n:4 + n])
                            last.then_inc(signal["gelu_ready"], 1)
                        if front:
                            turn_x_act(front, s, True)
                    if front:
                        for s in STREAMS:
                            front.wait("hn_turned", s)
                            nc.scalar.activation(xT[s][:, :], bank(s, 0, 2 * P, 3 * P), ACT.Identity,
                                                 bias=part(w, "ln")[:, 1:2], scale=part(w, "ln")[:, 0:1])\
                                .then_inc(signal["hnT_ready"], 1)
                piped(act, ph, body)
            return run

        def glu_vector(dve):
            def run(ph):
                w = glu_pack(ph)
                dve.wait_ge(loaded[w], 16)
                dve.wait_ge(tile_done, 2 + 16 * ph)

                def gated(t):
                    for s in STREAMS:
                        t.wait("gelu_ready", s)
                        for n, k in enumerate(HCH):
                            last = nc.vector.scalar_tensor_tensor(
                                out=gated_out(s)[0:k, n * P:(n + 1) * P], in0=ps[s][0:k, 2, n * P:(n + 1) * P],
                                scalar=part(w, "b1")[0:k, n:n + 1], in1=gelu_out(s)[0:k, n * P:(n + 1) * P],
                                op0=ALU.add, op1=ALU.mult)
                        last.then_inc(signal["gated_ready"], 1)

                def normal(t):
                    for s in STREAMS:
                        t.wait("h_turned", s)
                        nc.vector.bn_stats(h_stats[s][:, :], bank(s, 0, P, 2 * P)).then_inc(signal["h_stats"], 1)
                    for s in STREAMS:
                        t.wait("h_stats", s, alone=True)
                        nc.vector.bn_aggr(h_moments[s][:, :], h_stats[s][:, :]).then_inc(signal["h_mean"], 1)
                    for s in STREAMS:
                        t.wait("h_mean", s)
                        nc.vector.tensor_scalar(h_var[s][:, :], h_moments[s][:, 1:2], EPS, None, ALU.add)\
                            .then_inc(signal["h_var"], 1)
                    for s in STREAMS:
                        t.wait("h_rstd", s)
                        nc.vector.tensor_scalar(normal_h(s)[:, :], bank(s, 0, P, 2 * P), h_moments[s][:, 0:1],
                                                h_rstd[s][:, 0:1], ALU.subtract, ALU.mult)\
                            .then_inc(signal["h_normal"], 1)

                def body(back, front):
                    if back:
                        gated(back)
                    if front:
                        normal(front)
                    if back:
                        finish_vector(back, lambda s: bank(s, 3, 0, P), inner if ph == F0_GLU else state,
                                      outer=ph == F1_GLU, src=inner)
                piped(dve, ph, body)
            return run

        def both_qk(s):
            return big(s, 0, 512)

        def both_values(s):
            return big(s, 1, SEQS * 2 * D).rearrange("p (b w d) -> p b w d", b=SEQS, w=2)

        def both_probs(s):
            return big(s, 2, 2 * S)

        def both_probsT(s):
            return big(s, 3, P)

        def both_mixed(s):
            return big(s, 4, 2 * D)

        def cross0_pool(pool):
            def run(ph):
                pool.wait_ge(ctx_loaded, 16)
                pool.wait_ge(tile_done, 2 + 16 * ph)
                for s in STREAMS:
                    nc.gpsimd.memset(both_values(s), 0.0)

                def body(tail, middle, front):
                    if front:
                        for s in STREAMS:
                            if middle:
                                middle.wait("scores_ready", s)
                            stage_pool(front, s, state, context=True)
                    if tail:
                        for s in STREAMS:
                            norm_pool(tail, s)
                piped3(pool, (ph,), body)
            return run

        def cross0_tensor(pe):
            def run(ph):
                pe.wait_ge(loaded["x0"], 16)

                def project(t, s):
                    t.wait("xT_ready", s)
                    for n, (name, src) in enumerate((("wq_c", xT[s]), ("wk_s", cs[s]), ("wq_s", cs[s]),
                                                     ("wk_c", xT[s]))):
                        last = mm(bank(s, 1, n * P, (n + 1) * P), part("x0", name), src[:, :])
                    last.then_inc(signal["projected"], 1)

                def project_values(t, s):
                    for way, (name, src) in enumerate((("wv_s", cs[s]), ("wv_c", xT[s]))):
                        for b in range(SEQS):
                            o = ps[s][way * S:(way + 1) * S, 0, (1 + b) * P:(2 + b) * P]
                            mm(o, src[:, b * S:(b + 1) * S], part("x0", name), stop=False)
                            last = mm(o, ones_row[:, 0:S], part("rows", "x0_b" + name[1:]), start=False)
                    last.then_inc(signal["v_projected"], 1)

                def score(t, s):
                    for way in range(2):
                        for b in range(SEQS):
                            q, k = (both_qk(s)[:, (2 * way + n) * P + b * S:(2 * way + n) * P + (b + 1) * S]
                                    for n in range(2))
                            last = mm(ps[s][b * S:(b + 1) * S, 2, way * S:(way + 1) * S], q, k)
                    last.then_inc(signal["scores_ready"], 1)

                def mix(t, s):
                    t.wait("values_ready", s, alone=True)
                    t.wait("probsT_ready", s, alone=True)
                    for b in range(SEQS):
                        last = mm(ps[s][b * S:(b + 1) * S, 3, 0:2 * D], both_probsT(s)[:, b * S:(b + 1) * S],
                                  both_values(s)[:, b, :, :].rearrange("p w d -> p (w d)"))
                    last.then_inc(signal["mixed"], 1)

                def gate_logits(t, s):
                    t.wait("headsT_ready", s)
                    for way in range(2):
                        mm(bank(s, 3, 0, P), outT[s][:, way, :], part("x0", f"wg{way}"), start=(way == 0), stop=False)
                    mm(bank(s, 3, 0, P), ones_row[:, :], part("rows", "x0_bg"), start=False)\
                        .then_inc(signal["y_ready"], 1)

                def body(tail, middle, front):
                    for s in STREAMS:
                        if tail:
                            mix(tail, s)
                        if middle:
                            middle.wait("qk_ready", s)
                            project_values(middle, s)
                            score(middle, s)
                    for s in STREAMS:
                        if front:
                            if middle:
                                middle.wait("values_ready", s)
                            turn_x_pe(front, s)
                        if tail:
                            tail.wait("heads_normal", s)
                            for way in range(2):
                                last = nc.tensor.transpose(bank(s, 3, (2 + way) * P, (3 + way) * P),
                                                           both_mixed(s)[:, way * D:(way + 1) * D], ident)
                            last.then_inc(signal["heads_turned"], 1)
                    for s in STREAMS:
                        if front:
                            project(front, s)
                        if middle:
                            middle.wait("probs_ready", s)
                            nc.tensor.transpose(bank(s, 2, P, 2 * P), both_probs(s), ident)\
                                .then_inc(signal["probs_turned"], 1)
                        if tail and s == 0:
                            for o in STREAMS:
                                gate_logits(tail, o)
                    if tail:
                        for s in STREAMS:
                            tail.wait("gate_exp", s)
                piped3(pe, (ph,), body)
            return run

        def cross0_scalar(act):
            def run(ph):
                def weights_exp(t, s):
                    t.wait("scores_shifted", s)
                    nc.scalar.activation(both_probs(s), both_probs(s), ACT.Exp, scale=float(D) ** -0.5)\
                        .then_inc(signal["probs_ready"], 1)

                def turned(t, s):
                    t.wait("probs_turned", s)
                    nc.scalar.copy(both_probsT(s), bank(s, 2, P, 2 * P)).then_inc(signal["probsT_ready"], 1)

                def body(tail, middle, front):
                    if middle:
                        for s in STREAMS:
                            middle.wait("v_projected", s)
                            if tail:
                                tail.wait("mixed", s)
                            for way in range(2):
                                rows = slice(way * S, (way + 1) * S)
                                last = nc.scalar.copy(both_values(s)[rows, :, way, :],
                                                      ps[s][rows, 0, P:3 * P].rearrange("p (b d) -> p b d", b=SEQS))
                            last.then_inc(signal["values_ready"], 1)
                        weights_exp(middle, 0)
                    if front:
                        for s in STREAMS:
                            turn_x_act(front, s, False)
                    if tail:
                        for s in STREAMS:
                            tail.wait("heads_turned", s)
                            nc.scalar.copy(outT[s][:, :, :].rearrange("p w t -> p (w t)"), bank(s, 3, 2 * P, 4 * P))\
                                .then_inc(signal["headsT_ready"], 1)
                    if middle:
                        weights_exp(middle, 1)
                        turned(middle, 0)
                    if tail:
                        for s in STREAMS:
                            tail.wait("y_ready", s)
                            nc.scalar.activation(gate[s][:, :], bank(s, 3, 0, P), ACT.Exp, scale=-1.0)\
                                .then_inc(signal["gate_exp"], 1)
                    if middle:
                        turned(middle, 1)
                piped3(act, (ph,), body)
            return run

        def cross0_vector(dve):
            def run(ph):
                dve.wait_ge(loaded["x0"], 16)
                dve.wait_ge(tile_done, 2 + 16 * ph)

                def normal_heads(t, s):
                    t.wait("mixed", s)
                    t.wait("sums_inverted", s)
                    nc.vector.tensor_tensor(both_mixed(s).rearrange("p (w d) -> p w d", w=2),
                                            bank(s, 3, 0, 2 * D).rearrange("p (w d) -> p w d", w=2),
                                            inv_sum[s][:, 0:2].unsqueeze(2).broadcast_to([P, 2, D]), ALU.mult)\
                        .then_inc(signal["heads_normal"], 1)

                def shift(t, s):
                    t.wait("scores_ready", s)
                    sc = bank(s, 2, 0, 2 * S).rearrange("p (w k) -> p w k", w=2)
                    nc.vector.reduce_max(maxima[s][:, 0:2], sc, X_AXIS).then_inc(signal["max_ready"], 1)
                    t.wait("max_ready", s)
                    nc.vector.tensor_tensor(both_probs(s).rearrange("p (w k) -> p w k", w=2), sc,
                                            maxima[s][:, 0:2].unsqueeze(2).broadcast_to([P, 2, S]),
                                            ALU.subtract).then_inc(signal["scores_shifted"], 1)

                def bias_qk(t, s):
                    t.wait("projected", s)
                    nc.vector.tensor_tensor(both_qk(s).rearrange("p (n t) -> p n t", n=4),
                                            bank(s, 1).rearrange("p (n t) -> p n t", n=4),
                                            part("x0", "bias").unsqueeze(2).broadcast_to([P, 4, P]), ALU.add)\
                        .then_inc(signal["qk_ready"], 1)

                def paths_diff(t):
                    for s in STREAMS:
                        t.wait("heads_normal", s)
                        nc.vector.tensor_tensor(heads_out[s][:, :], both_mixed(s)[:, 0:D], both_mixed(s)[:, D:2 * D],
                                                ALU.subtract).then_inc(signal["paths_diff"], 1)

                def sums(t):
                    for s in STREAMS:
                        t.wait("probs_ready", s)
                        nc.vector.reduce_sum(sq_sum[s][:, 0:2], both_probs(s).rearrange("p (w k) -> p w k", w=2),
                                             X_AXIS).then_inc(signal["sums_ready"], 1)
                    for s in STREAMS:
                        t.wait("sums_ready", s)
                        nc.vector.reciprocal(inv_sum[s][:, 0:2], sq_sum[s][:, 0:2]).then_inc(signal["sums_inverted"], 1)

                def mix_paths(t):
                    for s in STREAMS:
                        t.wait("gate_exp", s)
                        nc.vector.tensor_scalar(gate[s][:, :], gate[s][:, :], 1.0, None, ALU.add)\
                            .then_inc(signal["gate_den"], 1)
                    for s in STREAMS:
                        t.wait("gate_den", s)
                        nc.vector.reciprocal(gate[s][:, :], gate[s][:, :]).then_inc(signal["gate_ready"], 1)
                    for s in STREAMS:
                        t.wait("gate_ready", s)
                        t.wait("paths_diff", s)
                        nc.vector.tensor_tensor(heads_out[s][:, :], heads_out[s][:, :], gate[s][:, :], ALU.mult)\
                            .then_inc(signal["diff_gated"], 1)
                    for s in STREAMS:
                        t.wait("diff_gated", s)
                        nc.vector.tensor_tensor(heads_out[s][:, :], heads_out[s][:, :], both_mixed(s)[:, D:2 * D],
                                                ALU.add).then_inc(signal["y_mixed"], 1)

                def body(tail, middle, front):
                    for s in STREAMS:
                        if tail:
                            normal_heads(tail, s)
                        if middle:
                            shift(middle, s)
                    if tail:
                        paths_diff(tail)
                    if front:
                        bias_qk(front, 0)
                    if middle:
                        sums(middle)
                    if front:
                        bias_qk(front, 1)
                    if tail:
                        mix_paths(tail)
                        finish_vector(tail, lambda s: heads_out[s][:, :], state, ready="y_mixed")
                piped3(dve, (ph,), body)
            return run

        def carver():
            used = [0]

            def carve(cols, rows=P, dt=F32):
                words = cols if dt == F32 else -(-cols // (2 if dt == BF16 else 4))
                used[0] += words
                assert used[0] <= 2 * SCRATCH
                view = arena[0:rows, used[0] - words:used[0]]
                return view if dt == F32 else view.bitcast(dt)
            return carve

        def group_of(x, g):
            return x[:, ds(g * 4, 4), :].rearrange("p a n -> p (a n)")

        carve = carver()
        g_x, g_xT, g_acc = carve(GT), carve(GT), carve(GT)
        NORM = 24 + 8 + 4 + 4
        g_stats, g_moments, g_var, g_rstd = carve(24), carve(8), carve(4), carve(4)
        g_hidden = [carve(GT) for _ in range(2 * FCH)]
        g_onehotT = carve(GT, rows=EXP)
        g_eq, g_onehot = carve(4 * EXP), carve(4 * EXP)
        g_max, g_first = carve(4), carve(4)
        gs = moe_sems

        def group_stage_pool(pool, ph, use, g):
            pool.wait_ge(tile_done, 2 + 16 * ph + g * 4)
            nc.gpsimd.tensor_copy(g_x, group_of(state, g)).then_inc(gs["g_staged"], 1)

        def group_norm_pool(pool, use, g):
            pool.wait_ge(gs["g_var"], 4 * use + 1 + g)
            nc.gpsimd.tensor_tensor(g_rstd, g_var, minus_half[:, 0:4], ALU.pow).then_inc(gs["g_rstd"], 1)

        def group_norm_vector(dve, use, g):
            for tt in range(4):
                last = nc.vector.bn_stats(g_stats[:, 6 * tt:6 * tt + 6], g_acc[:, tt * D:(tt + 1) * D])
            last.then_inc(gs["g_stats"], 1)
            dve.wait_ge(gs["g_stats"], 4 * use + 1 + g)
            dve.nop(nofuse=True)
            for tt in range(4):
                last = nc.vector.bn_aggr(g_moments[:, 2 * tt:2 * tt + 2], g_stats[:, 6 * tt:6 * tt + 6])
            last.then_inc(gs["g_mean"], 1)
            dve.wait_ge(gs["g_mean"], 4 * use + 1 + g)
            nc.vector.tensor_scalar(g_var, g_moments.rearrange("p (t m) -> p t m", m=2)[:, :, 1:2]
                                    .rearrange("p t m -> p (t m)"), EPS, None, ALU.add).then_inc(gs["g_var"], 1)
            dve.wait_ge(gs["g_rstd"], 4 * use + 1 + g)
            for tt in range(4):
                nc.vector.tensor_scalar(state[:, ds(g * 4 + tt, 1), :].rearrange("p a n -> p (a n)"),
                                        g_acc[:, tt * D:(tt + 1) * D], g_moments[:, 2 * tt:2 * tt + 1],
                                        g_rstd[:, tt:tt + 1], ALU.subtract, ALU.mult).then_inc(tile_done, 1)

        def group_turn(pe, use, g):
            pe.wait_ge(gs["g_staged"], 4 * use + 1 + g)
            for tt in range(4):
                last = nc.tensor.transpose(bank(1, 2, tt * P, (tt + 1) * P), g_x[:, tt * D:(tt + 1) * D], ident)
            last.then_inc(gs["g_turned"], 1)

        def group_logits(pe, use, g, pack, bias):
            pe.wait_ge(gs["g_xT"], 4 * use + 1 + g)
            for tt in range(4):
                o = bank(1, 3, tt * EXP, (tt + 1) * EXP)
                mm(o, g_xT[:, tt * P:(tt + 1) * P], part(pack, "wr"), stop=False)
                last = mm(o, ones_row[:, :], part("rows", bias), start=False)
            last.then_inc(gs["g_logits"], 1)

        def group_turn_scalar(act, use, g):
            act.wait_ge(gs["g_turned"], 4 * use + 1 + g)
            nc.scalar.copy(g_xT, bank(1, 2)).then_inc(gs["g_xT"], 1)

        def groups(eng, body):
            with eng.Fori(0, GROUPS - 1) as g:
                body(g, g + 1)
            body(GROUPS - 1, None)

        def moe1_pool(ph):
            pool = pool_engine
            group_stage_pool(pool, ph, 0, 0)

            def body(g, following):
                if following is not None:
                    pool.wait_ge(gs["g_sum"], 1 + g)
                    pool.nop(nofuse=True)
                    nc.gpsimd.tensor_copy(g_x, group_of(state, following)).then_inc(gs["g_staged"], 1)
                group_norm_pool(pool, 0, g)
            groups(pool, body)

        def moe1_tensor(ph):
            pe = tensor_engine
            pe.wait_ge(loaded["moe1"], 16)

            def up(g, e):
                for f in range(FCH):
                    if e:
                        pe.wait_ge(gs["relu_done"], g * 32 + 4 * (e - 1) + f + 1)
                    mm(bank(0, f), part("moe1", "w1")[:, (e * FCH + f) * P:(e * FCH + f + 1) * P], g_xT)\
                        .then_inc(gs["h_done"], 1)

            def down(g, e):
                pe.wait_ge(gs["relu_done"], g * 32 + 4 * e + 4)
                if e >= 2:
                    pe.wait_ge(gs["acc_done"], g * 8 + e - 1)
                for tt in range(4):
                    for f in range(FCH):
                        last = mm(bank(1, e % 2, tt * D, (tt + 1) * D),
                                  g_hidden[(e % 2) * FCH + f][:, tt * P:(tt + 1) * P],
                                  part("moe1", "w2")[:, (e * FCH + f) * D:(e * FCH + f + 1) * D],
                                  start=(f == 0), stop=(f == FCH - 1))
                last.then_inc(gs["ye_done"], 1)

            def body(g, following):
                pe.wait_ge(gs["g_onehot"], 1 + g)
                for tt in range(4):
                    last = nc.tensor.transpose(ps[1][0:EXP, 3, tt * P:(tt + 1) * P],
                                               g_onehot[:, tt * EXP:(tt + 1) * EXP], ident)
                last.then_inc(gs["g_oneturned"], 1)
                up(g, 0)
                pe.wait_ge(gs["g_onehotT"], 1 + g)
                for tt in range(4):
                    last = mm(bank(1, 3, tt * D, (tt + 1) * D), g_onehotT[:, tt * P:(tt + 1) * P],
                              part("moe1", "b2")[0:EXP, :])
                last.then_inc(gs["g_bias"], 1)
                for e in range(EXP):
                    if e + 1 < EXP:
                        up(g, e + 1)
                    if following is not None and e == EXP - 2:
                        group_turn(pe, 0, following)
                    if following is not None and e == EXP - 1:
                        group_logits(pe, 0, following, "moe1", "m1_br")
                    down(g, e)

            group_turn(pe, 0, 0)
            group_logits(pe, 0, 0, "moe1", "m1_br")
            groups(pe, body)

        def moe1_scalar(ph):
            act = scalar_engine
            act.wait_ge(loaded["moe1"], 16)

            def body(g, following):
                act.wait_ge(gs["g_oneturned"], 1 + g)
                nc.scalar.copy(g_onehotT, ps[1][0:EXP, 3, :]).then_inc(gs["g_onehotT"], 1)
                for e in range(EXP):
                    if e >= 2:
                        act.wait_ge(gs["ye_done"], g * 8 + e - 1)
                    for f in range(FCH):
                        act.wait_ge(gs["h_done"], g * 32 + 4 * e + f + 1)
                        nc.scalar.activation(g_hidden[(e % 2) * FCH + f], bank(0, f), ACT.Relu,
                                             bias=part("moe1", "b1")[:, e * FCH + f:e * FCH + f + 1])\
                            .then_inc(gs["relu_done"], 1)
                if following is not None:
                    group_turn_scalar(act, 0, following)

            group_turn_scalar(act, 0, 0)
            groups(act, body)

        def moe1_vector(ph):
            dve = vector_engine

            def four(x):
                return x.rearrange("p (t e) -> p t e", t=4)

            def wide4(x):
                return x.unsqueeze(2).broadcast_to([P, 4, EXP])

            def first_best(g):
                dve.wait_ge(gs["g_logits"], 1 + g)
                logits = four(bank(1, 3, 0, 4 * EXP))
                nc.vector.reduce_max(g_max, logits, X_AXIS).then_inc(gs["g_top"], 1)
                dve.wait_ge(gs["g_top"], 1 + g)
                nc.vector.tensor_tensor(four(g_eq), logits, wide4(g_max), ALU.is_equal).then_inc(gs["g_eq"], 1)
                dve.wait_ge(gs["g_eq"], 1 + g)
                nc.vector.tensor_tensor(four(g_eq), four(g_eq), part("const", "falling").unsqueeze(1)
                                        .broadcast_to([P, 4, EXP]), ALU.mult).then_inc(gs["g_rank"], 1)
                dve.wait_ge(gs["g_rank"], 1 + g)
                nc.vector.reduce_max(g_first, four(g_eq), X_AXIS).then_inc(gs["g_first"], 1)

            def indicators(g):
                dve.wait_ge(gs["g_first"], 1 + g)
                nc.vector.tensor_tensor(four(g_onehot), four(g_eq), wide4(g_first), ALU.is_equal)\
                    .then_inc(gs["g_onehot"], 1)

            def body(g, following):
                dve.wait_ge(tile_done, 2 + 16 * ph + 4 * g)
                dve.wait_ge(gs["g_bias"], 1 + g)
                nc.vector.tensor_tensor(g_acc, g_x, bank(1, 3), ALU.add).then_inc(gs["g_sum"], 1)
                dve.wait_ge(gs["g_sum"], 1 + g)
                for e in range(EXP):
                    if following is not None and e == EXP - 1:
                        first_best(following)
                    dve.wait_ge(gs["ye_done"], g * 8 + e + 1)
                    if e:
                        dve.wait_ge(gs["acc_done"], g * 8 + e)
                    for tt in range(4):
                        cols = slice(tt * D, (tt + 1) * D)
                        last = nc.vector.scalar_tensor_tensor(
                            out=g_acc[:, cols], in0=bank(1, e % 2)[:, cols],
                            scalar=g_onehot[:, tt * EXP + e:tt * EXP + e + 1], in1=g_acc[:, cols],
                            op0=ALU.mult, op1=ALU.add)
                    last.then_inc(gs["acc_done"], 1)
                dve.wait_ge(gs["acc_done"], g * 8 + EXP)
                if following is not None:
                    indicators(following)
                group_norm_vector(dve, 0, g)

            first_best(0)
            indicators(0)
            groups(dve, body)

        carve = carver()
        carve(2 * GT)
        NT8 = TILES * EXP
        logits_all, probs_all, rank_all, onehot_all, weighted_all, count_all = (carve(NT8) for _ in range(6))
        top_all, sum_all, inv_all, best_all, first_all, slot_all = (carve(TILES) for _ in range(6))
        onehot16, upto16, ones16 = carve(NT8, dt=BF16), carve(P, dt=BF16), carve(P, dt=BF16)
        zero512 = carve(512)
        at_slot = [carve(CAP) for _ in STREAMS]
        dispatch = [carve(EXP * CAP) for _ in STREAMS]
        dispatchT = [carve(EXP * P, rows=CAP) for _ in STREAMS]
        slotsT = carve(EXP * CAP)
        hidden80 = [carve(FCH * CAP) for _ in range(2)]
        expert_out = carve(EXP * D, rows=CAP)
        cm = gate_sems

        def moe2_pool(ph):
            pool = pool_engine
            for g in range(GROUPS):
                if g:
                    pool.wait_ge(cm["c_logits"], g)
                group_stage_pool(pool, ph, 1, 0) if g == 0 else \
                    nc.gpsimd.tensor_copy(g_x, state[:, 4 * g:4 * g + 4, :].rearrange("p a n -> p (a n)"))\
                    .then_inc(gs["g_staged"], 1)
            with pool.Fori(0, TURNS) as turn:
                for s in STREAMS:
                    pool.wait_ge(cm["c_dispatched"], turn * 2 + s + 1)
                    nc.gpsimd.tensor_copy(xs[s][:, :], state[:, ds(turn * 2 + s, 1), :].rearrange("p a n -> p (a n)"))\
                        .then_inc(cm["c_staged"], 1)
            pool.wait_ge(cm["c_dispatched"], 2 + TILES)

            def body(back, front):
                if back:
                    for s in STREAMS:
                        norm_pool(back, s)
            piped(pool, ph, body)

        def moe2_tensor(ph):
            pe = tensor_engine
            pe.wait_ge(loaded["moe2"], 16)
            pe.wait_ge(loaded["m2rows"], 16)
            for g in range(GROUPS):
                if g:
                    pe.wait_ge(cm["c_logits"], g)
                group_turn(pe, 1, g)
                group_logits(pe, 1, g, "moe2", "m2_bg")
            pe.wait_ge(cm["c_onehot"], 1)
            count = bank(0, 2, 0, NT8)
            mm(count, upto16, onehot16, stop=False)
            for t in range(TILES - 1):
                last = mm(count[:, (t + 1) * EXP:], ones16, onehot16[:, t * EXP:(t + 1) * EXP].unsqueeze(1)
                          .broadcast_to([P, TILES - 1 - t, EXP]), start=False)
            last.then_inc(cm["c_counts"], 1)
            for half in range(2):
                last = mm(bank(0, half, 0, 320), zero512[:, 0:P], zero512[:, 0:320], stop=False)
            last.then_inc(cm["c_dispatched"], 2)
            with pe.Fori(0, TURNS) as turn:
                for s in STREAMS:
                    pe.wait_ge(cm["c_staged"], turn * 2 + s + 1)
                    pe.wait_ge(cm["c_made"], turn * 2 + s + 1)
                    for half in range(2):
                        last = mm(bank(0, half, 0, 320), xs[s][:, :], dispatch[s][:, half * 320:(half + 1) * 320],
                                  start=False)
                    last.then_inc(cm["c_dispatched"], 1)

            def up(e):
                if e >= 2:
                    pe.wait_ge(cm["c_gelu"], e - 1)
                for f in range(FCH):
                    last = mm(bank(0, 2 + e % 2, f * CAP, (f + 1) * CAP),
                              part("moe2", "w1")[:, (e * FCH + f) * P:(e * FCH + f + 1) * P],
                              slotsT[:, e * CAP:(e + 1) * CAP])
                last.then_inc(cm["c_up"], 1)

            pe.wait_ge(cm["c_slotsT"], 1)
            up(0)
            for e in range(EXP):
                if e + 1 < EXP:
                    up(e + 1)
                pe.wait_ge(cm["c_gelu"], e + 1)
                o = ps[1][0:CAP, e // 4, (e % 4) * D:(e % 4 + 1) * D]
                for f in range(FCH):
                    mm(o, hidden80[e % 2][:, f * CAP:(f + 1) * CAP],
                       part("moe2", "w2")[:, (e * FCH + f) * D:(e * FCH + f + 1) * D], start=(f == 0), stop=False)
                mm(o, ones_row[:, 0:CAP], part("m2rows", "b2")[:, e * D:(e + 1) * D], start=False)\
                    .then_inc(cm["c_down"], 1)
            pe.wait_ge(cm["c_out"], 1)

            def body(back, front):
                for s in STREAMS:
                    if back:
                        back.wait_last(s)
                        back.wait("dispatchT_ready", s)
                        for e in range(EXP):
                            last = mm(bank(s, 0, 0, D), dispatchT[s][:, e * P:(e + 1) * P],
                                      expert_out[:, e * D:(e + 1) * D], start=(e == 0), stop=(e == EXP - 1))
                        last.then_inc(signal["y_ready"], 1)
                    if front:
                        front.wait("dispatched_made", s)
                        for e in range(EXP):
                            last = nc.tensor.transpose(pair(s, 2)[0:CAP, e * P:(e + 1) * P],
                                                       dispatch[s][:, e * CAP:(e + 1) * CAP], ident)
                        last.then_inc(signal["dispatch_turned"], 1)
            piped(pe, ph, body)

        def moe2_scalar(ph):
            act = scalar_engine
            act.wait_ge(loaded["moe2"], 16)
            for g in range(GROUPS):
                group_turn_scalar(act, 1, g)
            act.wait_ge(cm["c_shifted"], 1)
            nc.scalar.activation(probs_all, probs_all, ACT.Exp).then_inc(cm["c_exp"], 1)
            act.wait_ge(cm["c_dispatched"], 2 + TILES)
            nc.scalar.copy(slotsT.rearrange("p (a n) -> p a n", a=2), ps[0][:, 0:2, 0:320]).then_inc(cm["c_slotsT"], 1)
            for e in range(EXP):
                act.wait_ge(cm["c_up"], e + 1)
                if e >= 2:
                    act.wait_ge(cm["c_down"], e - 1)
                for f in range(FCH):
                    last = nc.scalar.activation(hidden80[e % 2][:, f * CAP:(f + 1) * CAP],
                                                bank(0, 2 + e % 2, f * CAP, (f + 1) * CAP), ACT.Gelu_apprx_tanh,
                                                bias=part("moe2", "b1")[:, e * FCH + f:e * FCH + f + 1])
                last.then_inc(cm["c_gelu"], 1)
            act.wait_ge(cm["c_down"], EXP)
            nc.scalar.copy(expert_out, pair(1, 0)[0:CAP, :]).then_inc(cm["c_out"], 1)

            def body(back, front):
                if front:
                    for s in STREAMS:
                        front.wait("dispatch_turned", s)
                        nc.scalar.copy(dispatchT[s], pair(s, 2)[0:CAP, :]).then_inc(signal["dispatchT_ready"], 1)
            piped(act, ph, body)

        def moe2_vector(ph):
            dve = vector_engine
            steps = [0]

            def then(ins):
                steps[0] += 1
                ins.then_inc(cm["c_chain"], 1)
                dve.wait_ge(cm["c_chain"], steps[0])

            def tiled(x):
                return x.rearrange("p (t e) -> p t e", t=TILES)

            def spread(x):
                return x.unsqueeze(2).broadcast_to([P, TILES, EXP])

            def make_dispatch(tile, s, count, chosen):
                nc.vector.tensor_tensor(at_slot[s], part("const", "slot"),
                                        slot_all[:, ds(tile, 1)].broadcast_to([P, CAP]), ALU.is_equal)\
                    .then_inc(cm["c_slot"], 1)
                dve.wait_ge(cm["c_slot"], count)
                return nc.vector.tensor_tensor(
                    dispatch[s].rearrange("p (e c) -> p e c", e=EXP),
                    chosen[:, ds(tile * EXP, EXP)].unsqueeze(2).broadcast_to([P, EXP, CAP]),
                    at_slot[s].unsqueeze(1).broadcast_to([P, EXP, CAP]), ALU.mult)

            for g in range(GROUPS):
                dve.wait_ge(gs["g_logits"], 4 + g + 1)
                nc.vector.tensor_copy(logits_all[:, g * 4 * EXP:(g + 1) * 4 * EXP], bank(1, 3, 0, 4 * EXP))\
                    .then_inc(cm["c_logits"], 1)
            dve.wait_ge(cm["c_logits"], GROUPS)
            nc.vector.memset(zero512, 0.0)
            nc.vector.memset(ones16, 1.0)
            nc.vector.tensor_copy(upto16, part("const", "upto"))
            then(nc.vector.reduce_max(top_all, tiled(logits_all), X_AXIS))
            nc.vector.tensor_tensor(tiled(probs_all), tiled(logits_all), spread(top_all), ALU.subtract)\
                .then_inc(cm["c_shifted"], 1)
            dve.wait_ge(cm["c_exp"], 1)
            then(nc.vector.reduce_sum(sum_all, tiled(probs_all), X_AXIS))
            then(nc.vector.reciprocal(inv_all, sum_all))
            then(nc.vector.tensor_tensor(tiled(probs_all), tiled(probs_all), spread(inv_all), ALU.mult))
            then(nc.vector.reduce_max(best_all, tiled(probs_all), X_AXIS))
            then(nc.vector.tensor_tensor(tiled(rank_all), tiled(probs_all), spread(best_all), ALU.is_equal))
            then(nc.vector.tensor_tensor(tiled(rank_all), tiled(rank_all), part("const", "falling").unsqueeze(1)
                                         .broadcast_to([P, TILES, EXP]), ALU.mult))
            then(nc.vector.reduce_max(first_all, tiled(rank_all), X_AXIS))
            then(nc.vector.tensor_tensor(tiled(onehot_all), tiled(rank_all), spread(first_all), ALU.is_equal))
            nc.vector.tensor_copy(onehot16, onehot_all).then_inc(cm["c_onehot"], 1)
            nc.vector.tensor_tensor(tiled(weighted_all), tiled(onehot_all), spread(best_all), ALU.mult)
            dve.wait_ge(cm["c_counts"], 1)
            then(nc.vector.tensor_tensor(count_all, bank(0, 2, 0, NT8), onehot_all, ALU.mult))
            then(nc.vector.reduce_sum(slot_all, tiled(count_all), X_AXIS))
            then(nc.vector.tensor_scalar(slot_all, slot_all, -1.0, None, ALU.add))
            with dve.Fori(0, TURNS) as turn:
                for s in STREAMS:
                    dve.wait_ge(cm["c_dispatched"], turn * 2 + s + 1)
                    make_dispatch(turn * 2 + s, s, turn * 2 + s + 1, onehot_all).then_inc(cm["c_made"], 1)
            dve.wait_ge(cm["c_dispatched"], 2 + TILES)

            def body(back, front):
                if front:
                    for s in STREAMS:
                        if back:
                            back.wait("dispatch_turned", s)
                        make_dispatch(front.tile(s), s, front.v + TILES + s + 1, weighted_all)\
                            .then_inc(signal["dispatched_made"], 1)
                if back:
                    finish_vector(back, lambda s: bank(s, 0, 0, D), state)
            piped(dve, ph, body)

        carve = carver()
        carve(3 * GT + NORM)
        q_in, q_abs, q_bad = carve(GT), carve(GT), carve(GT)
        q_small8, q_large8 = carve(GT, dt=FP8), carve(GT, dt=FP8)
        q_large = carve(GT)
        q_mask = carve(GT, dt=U8)
        q_x = carve(GT, dt=BF16)
        q_xT = carve(GT, dt=BF16)
        x16, y16, sum16 = carve(GT, dt=BF16), carve(GT, dt=BF16), carve(GT, dt=BF16)
        q_w = carve(P, dt=BF16)
        w16 = carve(D, dt=BF16)
        bias8 = carve(D, dt=BF16)
        scale8, inv8, scale_both = carve(2), carve(2), carve(1)
        fs = fp_sems

        def fp8_pool(ph):
            with pool_engine.Fori(0, GROUPS) as g:
                group_norm_pool(pool_engine, 1, g)

        def fp8_tensor(ph):
            pe = tensor_engine
            turned = ps[0][:, 0, :].bitcast(BF16)
            with pe.Fori(0, GROUPS) as g:
                pe.wait_ge(fs["f_rounded"], g + 1)
                for tt in range(4):
                    last = nc.tensor.transpose(turned[:, tt * P:(tt + 1) * P], q_x[:, tt * P:(tt + 1) * P],
                                               ident16[:, :])
                last.then_inc(fs["f_turned"], 1)
                pe.wait_ge(fs["f_turned_copy"], g + 1)
                for tt in range(4):
                    last = mm(bank(0, 1, tt * D, (tt + 1) * D), q_xT[:, tt * P:(tt + 1) * P], q_w)
                last.then_inc(fs["f_y"], 1)
                pe.wait_ge(fs["f_back"], 3 * g + 1)

        def fp8_scalar(ph):
            act = scalar_engine
            with act.Fori(0, GROUPS) as g:
                act.wait_ge(fs["f_turned"], g + 1)
                nc.scalar.copy(q_xT, ps[0][:, 0, :].bitcast(BF16)[:, 0:GT]).then_inc(fs["f_turned_copy"], 1)

        def fp8_vector(ph):
            dve = vector_engine
            round_steps, back_steps = 10, 3

            def rounded(n, src, scale, dst, then):
                small8, large8, large, mask = q_small8[:, 0:n], q_large8[:, 0:n], q_large[:, 0:n], q_mask[:, 0:n]
                x, size, bad = q_in[:, 0:n], q_abs[:, 0:n], q_bad[:, 0:n]
                then(nc.vector.tensor_scalar(x, src, scale, None, ALU.mult), alone=True)
                nc.vector.tensor_scalar(large8, x, 0.5, None, ALU.mult, saturate=False)
                nc.vector.tensor_tensor(size, x, x, ALU.mult)
                then(nc.vector.tensor_scalar(small8, x, 192.0, -192.0, ALU.min, ALU.max, saturate=False),
                     alone=True)
                nc.vector.tensor_copy(dst, small8)
                nc.vector.tensor_scalar(mask, size, 128.0 ** 2, None, ALU.is_ge)
                then(nc.vector.tensor_scalar(large, large8, 2.0, None, ALU.mult))
                then(nc.vector.tensor_tensor(size, large, large, ALU.mult))
                then(nc.vector.tensor_scalar(bad, size, 480.0 ** 2, 3e38, ALU.is_ge, ALU.mult))
                then(nc.vector.tensor_scalar(bad, bad, 10.0, None, ALU.mult))
                then(nc.vector.tensor_tensor(size, bad, bad, ALU.subtract))
                then(nc.vector.tensor_tensor(large, large, size, ALU.add), alone=True)
                then(nc.vector.copy_predicated(dst, mask, large))

            steps = [0]

            def once(ins, alone=False):
                steps[0] += 1
                ins.then_inc(fs["f_once"], 1)
                dve.wait_ge(fs["f_once"], steps[0])

            dve.wait_ge(loaded8, 3 * 16)
            once(nc.vector.tensor_tensor(scale_both, scale8[:, 0:1], scale8[:, 1:2], ALU.mult))
            once(nc.vector.reciprocal(inv8, scale8))
            rounded(P, w16, inv8[:, 1:2], q_w, once)

            def chain(name, g, per_group):
                steps = [0]

                def then(ins, alone=False):
                    steps[0] += 1
                    assert steps[0] <= per_group
                    ins.then_inc(fs[name], 1)
                    dve.wait_ge(fs[name], g * per_group + steps[0])
                    if alone:
                        dve.nop(nofuse=True)
                return then

            def round_group(g):
                then = chain("f_chain", g, round_steps)
                then(nc.vector.tensor_copy(x16, group_of(state, g)))
                rounded(GT, x16, inv8[:, 0:1], q_x, then)
                nc.vector.nop().then_inc(fs["f_rounded"], 1)

            def body(g, following):
                if following is not None:
                    dve.wait_ge(fs["f_turned"], g + 1)
                    dve.nop(nofuse=True)
                    round_group(following)
                dve.wait_ge(fs["f_y"], g + 1)
                then = chain("f_back", g, back_steps)
                then(nc.vector.tensor_scalar(y16, bank(0, 1), scale_both[:, 0:1], None, ALU.mult))
                then(nc.vector.tensor_tensor(sum16.rearrange("p (t d) -> p t d", t=4),
                                             y16.rearrange("p (t d) -> p t d", t=4),
                                             bias8.unsqueeze(1).broadcast_to([P, 4, D]), ALU.add))
                then(nc.vector.tensor_tensor(g_acc, group_of(state, g), sum16, ALU.add))
                group_norm_vector(dve, 1, g)

            round_group(0)
            groups(dve, body)

        pool_engine, tensor_engine, scalar_engine, vector_engine = nc.gpsimd, nc.tensor, nc.scalar, nc.vector
        block = ctx.enter_context(nc.Block())

        @block.sync
        def _(sp):
            sp.dma_start(weights["const"][:, :], packs["const"][0]).then_inc(loaded["const"], 16)
            sp.dma_start(weights["a0"][:, :], packs["a0"][0]).then_inc(loaded["a0"], 16)
            sp.dma_start(state[:, :, :], dram["x"].rearrange("(t p) d -> p t d", p=P)).then_inc(x_loaded, 16)
            sp.dma_start(weights["rows"][:, :], packs["rows"][0]).then_inc(loaded["rows"], 16)
            sp.dma_start(weights["scales"][:, :], packs["scales"][0][0].partition_broadcast(P))\
                .then_inc(loaded["scales"], 16)
            sp.dma_start(own_u8[:, :], dram["own"].unsqueeze(0).broadcast_to([SEQS, S, S])).then_inc(masks_loaded, 16)
            sp.dma_start(mask_int[:, :], dram["seq"].unsqueeze(0).broadcast_to([SEQS, S, S])).then_inc(masks_loaded, 16)
            for b in range(SEQS):
                sp.dma_start(pads_int[b * S:(b + 1) * S, :, :], dram["pads"][:, b, :].partition_broadcast(S))\
                    .then_inc(masks_loaded, 16)
            sp.dma_start(ctxT[:, :, :], dram["ctxT"].rearrange("d (t p) -> d t p", p=P)).then_inc(ctx_loaded, 16)
            for n in ("x0", "fa0", "fg0", "fa1", "fg1", "a1", "moe1"):
                sp.dma_start(weights[n][:, :], packs[n][0]).then_inc(loaded[n], 16)
            for early, done in (("x0", L0_CROSS), ("fa0", F0_ATTN), ("fa1", F1_ATTN)):
                if PHASES > done + 1:
                    sp.wait_ge(tile_done, 2 + 16 * (done + 1))
                    for n in LATE[early]:
                        sp.dma_start(weights[n], packs[n][0]).then_inc(loaded[n], 16)
                        sp.wait_ge(loaded[n], 16)
            if PHASES > F1_GLU + 1:
                sp.wait_ge(tile_done, 2 + 16 * (F1_GLU + 1))
                sp.dma_start(alibi16.rearrange("p n k -> p (n k)"), packs["alibi"][0]).then_inc(loaded["alibi"], 16)
                sp.wait_ge(loaded["alibi"], 16)
            if PHASES > L1_MOE + 1:
                sp.wait_ge(tile_done, 2 + 16 * (L1_MOE + 1))
                sp.dma_start(experts[:, :], packs["moe2"][0]).then_inc(loaded["moe2"], 16)
                sp.wait_ge(loaded["moe2"], 16)
            if PHASES > L3_CROSS + 1:
                sp.wait_ge(tile_done, 2 + 16 * (L3_CROSS + 1))
                sp.dma_start(w16, dram["kernel8"]).then_inc(loaded8, 16)
                sp.dma_start(bias8, dram["bias8"][0].partition_broadcast(P)).then_inc(loaded8, 16)
                sp.dma_start(scale8, dram["scales8"][0].partition_broadcast(P)).then_inc(loaded8, 16)
            sp.wait_ge(tile_done, 2 + 16 * PHASES)
            sp.dma_start(out.rearrange("(t p) d -> p t d", p=P), state[:, :, :]).then_inc(out_stored, 16)
            sp.wait_ge(out_stored, 16)

        @block.gpsimd
        def _(pool):
            pool.wait_ge(x_loaded, 16)
            pool.wait_ge(tables_ready, 1)
            narrow, wide, glu = narrow_pool(pool), wide_pool(pool), glu_pool(pool)
            cross0 = cross0_pool(pool)
            run_phases({"narrow": narrow, "cross0": cross0, "wide": wide, "glu": glu, "moe1": moe1_pool,
                        "moe2": moe2_pool, "fp8": fp8_pool})

        @block.tensor
        def _(pe):
            pe.wait_ge(loaded["const"], 16)
            pe.wait_ge(loaded["rows"], 16)
            pe.wait_ge(tables_ready, 1)
            narrow, wide, glu = narrow_tensor(pe), wide_tensor(pe), glu_tensor(pe)
            cross0 = cross0_tensor(pe)
            run_phases({"narrow": narrow, "cross0": cross0, "wide": wide, "glu": glu, "moe1": moe1_tensor,
                        "moe2": moe2_tensor, "fp8": fp8_tensor})

        @block.scalar
        def _(act):
            act.wait_ge(tables_ready, 1)
            narrow, wide, glu = narrow_scalar(act), wide_scalar(act), glu_scalar(act)
            cross0 = cross0_scalar(act)
            run_phases({"narrow": narrow, "cross0": cross0, "wide": wide, "glu": glu, "moe1": moe1_scalar,
                        "moe2": moe2_scalar, "fp8": fp8_scalar})

        @block.vector
        def _(dve):
            dve.wait_ge(loaded["const"], 16)
            dve.wait_ge(loaded["scales"], 16)
            dve.wait_ge(masks_loaded, 4 * 16)
            nc.vector.memset(ones_row[:, :], 1.0)
            nc.vector.memset(minus_half[:, :], -0.5)
            for s in STREAMS:
                nc.vector.memset(values8[s][:, :, :, :, :].rearrange("p j b a d -> p (j b a d)"), 0.0)
                nc.vector.memset(shT[s][:, :], 0.0)
                nc.vector.memset(values64(s).rearrange("p b c a d -> p (b c a d)"), 0.0)
            nc.vector.tensor_copy(ident16[:, :], ident)
            for l in range(2):
                nc.vector.tensor_tensor(rope_f[l][:, :], part("const", "rope_xpos"),
                                        weights["scales"][:, l * 256:(l + 1) * 256], ALU.mult)
            nc.vector.tensor_scalar(own16[:, :], own_u8[:, :], 0.0, OFF, ALU.is_equal, ALU.mult)
            nc.vector.tensor_scalar(seq_add[:, :], mask_int[:, :], 0.0, OFF, ALU.is_equal, ALU.mult)
            nc.vector.tensor_scalar(pads16[:, :, :], pads_int, 0.0, OFF, ALU.is_equal, ALU.mult)
            nc.vector.tensor_copy(causal16[:, :], part("const", "causal")).then_inc(setup_done, 1)
            dve.wait_ge(setup_done, 1)
            nc.vector.tensor_tensor(pads16[:, :, :], pads16[:, :, :],
                                    seq_add[:, :].unsqueeze(1).broadcast_to([P, TILES, S]), ALU.min)
            for s in STREAMS:
                for par in range(2):
                    rows = slice(par * S, (par + 1) * S)
                    last = nc.vector.memset(values8[s][rows, :, :, par, HD8:HD8 + 1], 1.0)
            last.then_inc(tables_ready, 1)
            dve.wait_ge(tables_ready, 1)
            nc.vector.memset(stats[0][:, :], 0.0).then_inc(tile_done, 2)
            narrow, wide, glu = narrow_vector(dve), wide_vector(dve), glu_vector(dve)
            cross0 = cross0_vector(dve)
            run_phases({"narrow": narrow, "cross0": cross0, "wide": wide, "glu": glu, "moe1": moe1_vector,
                        "moe2": moe2_vector, "fp8": fp8_vector})


def rope8_table():
    f = np.arange(P) % HD8
    theta = np.arange(S, dtype=np.float32)[None, :] / np.exp(
        2.0 * (f // 2).astype(np.float32) / HD8 * np.log(10000.0)).astype(np.float32)[:, None]
    cos, sin = np.cos(theta), np.sin(theta)
    sign = np.where(f % 2 == 0, -1.0, 1.0)[:, None]
    return np.concatenate([cos, sin * sign], axis=1).astype(np.float32)


def rope64_table(xpos):
    half = np.arange(0, 64, 2, dtype=np.float32)
    t = (np.arange(P) % S).astype(np.float32)
    freqs = np.tile(t[:, None] * (1.0 / 10000.0 ** (half / 64)).astype(np.float32)[None, :], (1, 2))
    cos, sin = np.cos(freqs), np.sin(freqs)
    sin = np.concatenate([-sin[:, :32], sin[:, 32:]], axis=1)
    scale = 1.0
    if xpos:
        base = (half + 0.4 * 64) / (1.4 * 64)
        scale = np.tile(base[None, :] ** ((t - S // 2) / 32.0)[:, None], (1, 2))
    return np.concatenate([cos * scale, cos / scale, sin * scale, sin / scale], axis=1).astype(np.float32)


def alibi_table():
    slopes = (2.0 ** -0.5) ** np.arange(1, H8 + 1)
    diff = np.arange(S)[None, :] - (np.arange(P) % S)[:, None]
    full = slopes[None, :, None] * diff[:, None, :] * np.sqrt(HD8)
    rest = full.reshape(P, H8 * S).astype(np.float32)
    parts = []
    for _ in range(3):
        top = (rest.view(np.uint32) & 0xFFFF0000).view(np.float32)
        parts.append(top)
        rest = rest - top
    future = np.broadcast_to((diff > 0)[:, None, :], (P, H8, S)).reshape(P, H8 * S)
    parts[0] = np.where(future, np.float32(NEG), parts[0]).astype(np.float32)
    return np.concatenate(parts, axis=1)


def constants():
    p = np.arange(P)
    causal = np.where(np.arange(S)[None, :] <= (p % S)[:, None], 0.0, NEG).astype(np.float32)
    own_head = (((p // HD8) % 8)[:, None] == np.arange(8)[None, :]).astype(np.float32)
    return {"ident": np.eye(P, dtype=np.float32), "causal": causal, "own_head": own_head, "rope8": rope8_table(),
            "rope64": rope64_table(False), "rope_xpos": rope64_table(True),
            "falling": np.tile(np.arange(EXP, 0, -1, dtype=np.float32), (P, 1)),
            "slot": np.tile(np.arange(CAP, dtype=np.float32), (P, 1)),
            "upto": (p[:, None] <= p[None, :]).astype(np.float32)}


def by_parity(w, heads, d):
    return w.reshape(w.shape[0], heads // 2, 2, d).transpose(0, 2, 1, 3).reshape(w.shape[0], heads * d)


def chunked(w):
    n = w.shape[0] // P
    return w.reshape(n, P, w.shape[1]).transpose(1, 0, 2).reshape(P, n * w.shape[1])


def rows_to(a, n):
    out = np.zeros((n,) + a.shape[1:], a.dtype)
    out[:a.shape[0]] = a
    return out


def layout(i):
    swap = np.arange(D) ^ 1

    def narrow(wq, wk, wv, wo=None, bq=None, bk=None, bv=None, rope=False):
        out = {"wq": wq.T, "wk": wk.T, "wv": by_parity(wv.T, H8, HD8)}
        if wo is not None:
            out["wo"] = wo.T
        if bq is not None:
            out["bv"] = bv[:, None]
            rows = [bq, bk]
            if rope:
                out |= {"wq_swapped": wq[swap].T, "wk_swapped": wk[swap].T}
                rows += [bq[swap], bk[swap]]
            out["bias"] = np.concatenate([np.stack([r[h * S:(h + 1) * S] for r in rows for h in range(2)], axis=1)] * 2)
        return out

    def named(prefix, names):
        return [i[prefix + n] for n in names.split()]

    packs = {"const": constants()}
    packs["a0"] = narrow(*named("L0_attn_", "wq wk wv wo bq bk bv"), rope=True)
    x0 = {n: i["L0_xattn_" + n] for n in ("Wq_c", "Wk_s", "Wv_s", "Wq_s", "Wk_c", "Wv_c", "Wg")}
    packs["rows"] = {"a0_bo": i["L0_attn_bo"], "x0_bv_s": i["L0_xattn_bv_s"], "x0_bv_c": i["L0_xattn_bv_c"],
                     "x0_bg": i["L0_xattn_bg"], "fg0_b2": i["L0_ffn_b2"][0], "fg1_b2": i["L0_ffn_b2"][1],
                     "x1_bo": i["L1_xattn_bo"], "a2_bo": i["L2_attn_bo"], "x2_bo": i["L2_xattn_bo"],
                     "a3_bo": i["L3_attn_bo"], "x3_bv": by_parity(i["L3_xattn_bv"][None], H8, HD8)[0],
                     "m1_br": i["L1_ffn_br"], "m2_bg": i["L2_ffn_gate_b"], }
    packs["rows"] = {n: a[None] for n, a in packs["rows"].items()}
    packs["m2rows"] = {"b2": i["L2_ffn_b2"].reshape(1, -1)}
    packs["scales"] = {}
    for l in range(2):
        q, k = i["L0_ffn_q_scale"][l], i["L0_ffn_k_scale"][l]
        for n, a in (("q", q), ("k", k), ("q_turned", np.roll(q, 32)), ("k_turned", np.roll(k, 32))):
            packs["scales"][f"{n}{l}"] = a[None]
    packs["x0"] = {"wq_c": x0["Wq_c"].T, "wk_s": x0["Wk_s"].T, "wq_s": x0["Wq_s"].T, "wk_c": x0["Wk_c"].T,
                   "wv_s": x0["Wv_s"].T, "wv_c": x0["Wv_c"].T, "wg0": x0["Wg"][:, :D].T, "wg1": x0["Wg"][:, D:].T,
                   "bias": np.stack(named("L0_xattn_", "bq_c bk_s bq_s bk_c"), axis=1)}
    for l in range(2):
        wqkv, wo = i["L0_ffn_wqkv"][l], i["L0_ffn_wo"][l]
        packs[f"fa{l}"] = {"wqk": wqkv[:, :1024], "wv": by_parity(by_parity(wqkv[:, 1024:], 8, 64), 8, 64),
                           "wo": chunked(by_parity(wo.T, 8, 64).T)}
        b1 = i["L0_ffn_b1"][l]
        w2 = rows_to(i["L0_ffn_w2"][l], 3 * P)
        packs[f"fg{l}"] = {"w1": i["L0_ffn_w1"][l], "w2": chunked(w2),
                           "b1": np.concatenate([rows_to(b1[:HID], 3 * P).reshape(3, P),
                                                 rows_to(b1[HID:], 3 * P).reshape(3, P)]).T,
                           "ln": np.stack([i["L0_ffn_ln_g"][l], i["L0_ffn_ln_b"][l]], axis=1)}
    packs["a1"] = {"wqk": i["L1_attn_wq"].T, "down": i["L1_attn_w_kv_down"].T,
                   "k_up": rows_to(i["L1_attn_w_k_up"].T, P), "wv": rows_to(by_parity(by_parity(i["L1_attn_w_v_up"].T, 16, 64), 16, 64), P),
                   "wo": chunked(by_parity(i["L1_attn_wo"], 16, 64).T)}
    packs["x1"] = narrow(*named("L1_xattn_", "Wq Wk Wv Wo"))
    packs["moe1"] = {"w1": i["L1_ffn_W1"].transpose(2, 0, 1).reshape(D, EXP * FF),
                     "w2": i["L1_ffn_W2"].reshape(EXP, D, FCH, P).transpose(3, 0, 2, 1).reshape(P, EXP * FCH * D),
                     "b1": i["L1_ffn_b1"].reshape(EXP * FCH, P).T, "wr": i["L1_ffn_Wr"].T,
                     "b2": rows_to(i["L1_ffn_b2"], P)}
    packs["a2"] = narrow(*named("L2_attn_", "Wq Wk Wv Wo bq bk bv"))
    packs["x2"] = narrow(*named("L2_xattn_", "Wq Wk Wv Wo bq bk bv"))
    packs["moe2"] = {"w1": i["L2_ffn_w1"].transpose(1, 0, 2).reshape(D, EXP * FF),
                     "w2": i["L2_ffn_w2"].reshape(EXP, FCH, P, D).transpose(2, 0, 1, 3).reshape(P, EXP * FCH * D),
                     "b1": i["L2_ffn_b1"].reshape(EXP * FCH, P).T, "wr": i["L2_ffn_gate_w"],
                     "pad": np.zeros((P, D), np.float32)}
    packs["a3"] = narrow(*named("L3_attn_", "Wq Wk Wv Wo bq bk bv"), rope=True)
    x3 = i["L3_xattn_Wv"]
    packs["x3"] = narrow(i["L3_xattn_Wq"], i["L3_xattn_Wk"], x3, None, *named("L3_xattn_", "bq bk bv"))
    packs["alibi"] = {"alibi": alibi_table()}
    return packs


def kernel(**inputs):
    import concourse.bacc as bacc
    from concourse.bass_utils import run_bass_kernel_spmd

    i = {n: np.asarray(a) for n, a in inputs.items()}
    nc = bacc.Bacc("TRN2", target_bir_lowering=False, num_devices=1)
    arrays, dram, packs = {}, {}, {}

    def declare(name, a):
        a = np.ascontiguousarray(a)
        arrays["in_" + name] = a
        return nc.dram_tensor("in_" + name, a.shape, mybir.dt.from_np(a.dtype), kind="ExternalInput").ap()

    for name, parts in layout(i).items():
        where, first = {}, 0
        for part, a in parts.items():
            where[part] = (first, a.shape[1])
            first += a.shape[1]
        whole = np.concatenate(list(parts.values()), axis=1)
        if name == "alibi":
            whole = whole.astype(i["L3_ffn_kernel"].dtype)
        packs[name] = (declare("pack_" + name, whole), where)
    dram["x"] = declare("x", i["x"].reshape(B * S, D))
    dram["ctxT"] = declare("ctxT", i["ctx_1024"].reshape(B * S, D).T)
    dram["own"] = declare("own", i["mask_1x1xSxS2_bk0"].reshape(S, S))
    dram["seq"] = declare("seq", i["mask_1x1xSxS2_ik0"].reshape(S, S))
    dram["pads"] = declare("pads", i["mask_Bx1x1xS2_ik0"].reshape(TILES, SEQS, S))
    dram["kernel8"] = declare("kernel8", i["L3_ffn_kernel"])
    dram["bias8"] = declare("bias8", i["L3_ffn_bias"][None])
    dram["scales8"] = declare("scales8", np.stack([i["L3_ffn_input_scale"], i["L3_ffn_kernel_scale"]], axis=1))
    out = nc.dram_tensor("out", (B * S, D), F32, kind="ExternalOutput").ap()
    program(nc, packs, dram, out)
    r = run_bass_kernel_spmd(nc, [arrays], core_ids=[0])
    return r.results[0]["out"].reshape(B, S, D)
```
